# Optimizing a Trainium2 kernel written in Bass

```python
import numpy as np
import jax
import jax.numpy as jnp

def _softmax(x, axis=-1):
    return jax.nn.softmax(x, axis=axis)

def _gelu(x):
    return jax.nn.gelu(x, approximate=True)

def _silu(x):
    return jax.nn.silu(x)

def _sigmoid(x):
    return jax.nn.sigmoid(x)

def _layernorm(x, axis=-1, eps=1e-05):
    m = jnp.mean(x, axis=axis, keepdims=True)
    v = jnp.var(x, axis=axis, keepdims=True)
    return (x - m) / jnp.sqrt(v + eps)

def _scatter_add(tgt, idx, src, axis=0):
    return tgt.at[idx].add(src)

def _segment_sum(src, seg, n):
    return jax.ops.segment_sum(src, seg, n)
kernel_name = 'mk_adaln_d2_jaxref_r8_c41b63'

def setup_inputs(seed: int=0):
    np.random.seed(seed)
    _w = jnp.asarray

    def _L0_attn_setup():
        import jax, jax.numpy as jnp
        import numpy as np
        EMBED = 128
        HEADS = 16
        HEAD_DIM = EMBED // HEADS
        RANK = 8
        ALPHA = 16
        SCALE_LORA = ALPHA / RANK

        def _lora_linear(x, W, b, A, B):
            return x @ W.T + b + SCALE_LORA * (x @ A.T @ B.T)
        key = jax.random.key(seed)
        ks = jax.random.split(key, 17)
        d = {'x': jax.random.normal(ks[0], (2, 256, EMBED), dtype=jnp.float32)}
        names = ['q', 'k', 'v', 'o']
        i = 1
        for n in names:
            d[f'W{n}'] = jax.random.normal(ks[i], (EMBED, EMBED), dtype=jnp.float32) * 0.02
            i += 1
            d[f'b{n}'] = jnp.zeros((EMBED,), dtype=jnp.float32)
            d[f'A{n}'] = jax.random.normal(ks[i], (RANK, EMBED), dtype=jnp.float32) * 0.02
            i += 1
            d[f'B{n}'] = jax.random.normal(ks[i], (EMBED, RANK), dtype=jnp.float32) * 0.02
            i += 1
        return d
    _L0_attn_in = _L0_attn_setup()

    def _L0_ffn_setup():
        import jax, jax.numpy as jnp
        import numpy as np
        import math
        D_MODEL, D_FF, N_EXPERTS, TOP_K, N_SHARED = (128, 512, 8, 2, 1)
        B, T = (4, 128)
        SCALE = 1.0 / math.sqrt(N_SHARED + TOP_K / N_EXPERTS)
        key = jax.random.key(seed)
        ks = jax.random.split(key, 10)
        s1 = 1.0 / math.sqrt(D_MODEL)
        s2 = 1.0 / math.sqrt(D_FF)
        return {'x': jax.random.normal(ks[0], (B, T, D_MODEL), dtype=jnp.float32), 'w_router': jax.random.normal(ks[1], (N_EXPERTS, D_MODEL), dtype=jnp.float32) * s1, 'W1': jax.random.normal(ks[2], (N_EXPERTS, D_FF, D_MODEL), dtype=jnp.float32) * s1, 'b1': jax.random.normal(ks[3], (N_EXPERTS, D_FF), dtype=jnp.float32) * 0.02, 'W2': jax.random.normal(ks[4], (N_EXPERTS, D_MODEL, D_FF), dtype=jnp.float32) * s2, 'b2': jax.random.normal(ks[5], (N_EXPERTS, D_MODEL), dtype=jnp.float32) * 0.02, 'Ws1': jax.random.normal(ks[6], (D_FF, D_MODEL), dtype=jnp.float32) * s1, 'bs1': jax.random.normal(ks[7], (D_FF,), dtype=jnp.float32) * 0.02, 'Ws2': jax.random.normal(ks[8], (D_MODEL, D_FF), dtype=jnp.float32) * s2, 'bs2': jax.random.normal(ks[9], (D_MODEL,), dtype=jnp.float32) * 0.02}
    _L0_ffn_in = _L0_ffn_setup()
    _L0_c = _w((lambda *s: np.random.randn(*s).astype(np.float32) * 0.05)(8, 128))
    _L0_wmod = _w((lambda *s: np.random.randn(*s).astype(np.float32) * 0.05)(128, 6 * 128) * 128 ** (-0.5))

    def _L1_attn_setup():
        import jax, jax.numpy as jnp
        import numpy as np
        B, L, D, N, K, E = (8, 512, 128, 16, 4, 2)
        INNER = E * N

        def _selective_ssm(x, conv_w, conv_b, Win, b_in, Wout, b_out, A_log):
            bsz, seq_len, d_model = x.shape
            n = A_log.shape[0]
            inner = (Win.shape[1] - n) // 2
            pad = (conv_w.shape[2] - 1) // 2
            xc = jnp.transpose(x, (0, 2, 1))
            xc = jax.lax.conv_general_dilated(xc, conv_w, window_strides=(1,), padding=[(pad, pad)], dimension_numbers=('NCH', 'OIH', 'NCH'), feature_group_count=d_model)
            xc = xc + conv_b[None, :, None]
            Lc = xc.shape[2]
            if Lc < seq_len:
                xc = jnp.pad(xc, ((0, 0), (0, 0), (0, seq_len - Lc)))
            elif Lc > seq_len:
                xc = xc[:, :, :seq_len]
            xc = jnp.transpose(xc, (0, 2, 1))
            proj = xc @ Win + b_in
            delta = proj[..., :n]
            B_in = proj[..., n:n + inner].reshape(bsz, seq_len, n, -1).mean(axis=-1)
            C = proj[..., n + inner:].reshape(bsz, seq_len, n, -1).mean(axis=-1)
            A = -jnp.exp(A_log)[None, None, :]
            dA = jax.nn.softplus(delta) * A
            A_bar = jnp.exp(dA)
            eps = 0.0001
            A_safe = jnp.where(jnp.abs(A) < eps, eps * jnp.sign(A) + eps, A)
            taylor = 1.0 + dA / 2.0 + dA * dA / 6.0
            B_bar_scale = jnp.where(jnp.abs(A) < eps, taylor, (A_bar - 1.0) / A_safe)
            B_bar = B_bar_scale * B_in

            def combine(c1, c2):
                a1, b1 = c1
                a2, b2 = c2
                return (a1 * a2, a2 * b1 + b2)
            _, h = jax.lax.associative_scan(combine, (A_bar, B_bar), axis=1)
            y = C * h @ Wout + b_out
            return y
        key = jax.random.key(seed)
        ks = jax.random.split(key, 4)
        x = jax.random.normal(ks[0], (B, L, D), jnp.float32)
        conv_w = jax.random.normal(ks[1], (D, 1, K), jnp.float32) * (1.0 / np.sqrt(K))
        conv_b = jnp.zeros((D,), jnp.float32)
        Win = jax.random.normal(ks[2], (D, 2 * INNER + N), jnp.float32) * (1.0 / np.sqrt(D))
        b_in = jnp.zeros((2 * INNER + N,), jnp.float32)
        Wout = jax.random.normal(ks[3], (N, D), jnp.float32) * (1.0 / np.sqrt(N))
        b_out = jnp.zeros((D,), jnp.float32)
        A_log = jnp.zeros((N,), jnp.float32)
        return {'x': x, 'conv_w': conv_w, 'conv_b': conv_b, 'Win': Win, 'b_in': b_in, 'Wout': Wout, 'b_out': b_out, 'A_log': A_log}
    _L1_attn_in = _L1_attn_setup()

    def _L1_ffn_setup():
        import jax, jax.numpy as jnp
        import numpy as np
        from jax import lax
        B, L, D = (4, 256, 128)
        E, TOPK = (8, 2)
        K, DIL = (3, 1)
        HID = D // 4
        EPS = 1e-06

        def _rmsnorm(h, w):
            rms = jnp.sqrt(jnp.mean(h * h, axis=-1, keepdims=True) + EPS)
            return w * (h / rms)

        def _forward(x, dw_kernel, dw_bias, pw_w, pw_b, router_w, router_b, expert_w, expert_b, out_w, out_b, norm_w, ff_down_w, ff_down_b, ff_up_w, ff_up_b):
            pad = (K - 1) * DIL
            xc = jnp.transpose(x, (0, 2, 1))
            xc = lax.conv_general_dilated(xc, dw_kernel, window_strides=(1,), padding=((pad, 0),), rhs_dilation=(DIL,), dimension_numbers=('NCH', 'OIH', 'NCH'), feature_group_count=D) + dw_bias[None, :, None]
            xc = jax.nn.silu(jnp.einsum('bdl,ed->bel', xc, pw_w) + pw_b[None, :, None])
            x1 = x + jnp.transpose(xc, (0, 2, 1))
            logits = jnp.einsum('bsd,ed->bse', x1, router_w) + router_b
            top_v, top_i = lax.top_k(logits, TOPK)
            top_w = jax.nn.softmax(top_v, axis=-1)
            rw = jnp.sum(jax.nn.one_hot(top_i, E, dtype=x1.dtype) * top_w[..., None], axis=-2)
            ye = jax.nn.silu(jnp.einsum('bsd,eod->bseo', x1, expert_w) + expert_b)
            combined = jnp.einsum('bse,bseo->bso', rw, ye)
            moe_out = jnp.einsum('bsd,od->bso', combined, out_w) + out_b
            h = _rmsnorm(x1 + moe_out, norm_w)
            ff = jax.nn.gelu(jnp.einsum('bsd,hd->bsh', h, ff_down_w) + ff_down_b, approximate=False)
            ff = jnp.einsum('bsh,dh->bsd', ff, ff_up_w) + ff_up_b
            return h + ff
        key = jax.random.key(seed)
        ks = jax.random.split(key, 16)
        s = 0.02
        return {'x': jax.random.normal(ks[0], (B, L, D), dtype=jnp.float32), 'dw_kernel': jax.random.normal(ks[1], (D, 1, K), dtype=jnp.float32) * s, 'dw_bias': jnp.zeros((D,), dtype=jnp.float32), 'pw_w': jax.random.normal(ks[2], (D, D), dtype=jnp.float32) * s, 'pw_b': jnp.zeros((D,), dtype=jnp.float32), 'router_w': jax.random.normal(ks[3], (E, D), dtype=jnp.float32) * s, 'router_b': jnp.zeros((E,), dtype=jnp.float32), 'expert_w': jax.random.normal(ks[4], (E, D, D), dtype=jnp.float32) * s, 'expert_b': jnp.zeros((E, D), dtype=jnp.float32), 'out_w': jax.random.normal(ks[5], (D, D), dtype=jnp.float32) * s, 'out_b': jnp.zeros((D,), dtype=jnp.float32), 'norm_w': jnp.ones((D,), dtype=jnp.float32), 'ff_down_w': jax.random.normal(ks[6], (HID, D), dtype=jnp.float32) * s, 'ff_down_b': jnp.zeros((HID,), dtype=jnp.float32), 'ff_up_w': jax.random.normal(ks[7], (D, HID), dtype=jnp.float32) * s, 'ff_up_b': jnp.zeros((D,), dtype=jnp.float32)}
    _L1_ffn_in = _L1_ffn_setup()
    _L1_c = _w((lambda *s: np.random.randn(*s).astype(np.float32) * 0.05)(8, 128))
    _L1_wmod = _w((lambda *s: np.random.randn(*s).astype(np.float32) * 0.05)(128, 6 * 128) * 128 ** (-0.5))
    _d = {'L0_attn_x': _L0_attn_in['x'], 'L0_attn_Wq': _L0_attn_in['Wq'], 'L0_attn_bq': _L0_attn_in['bq'], 'L0_attn_Aq': _L0_attn_in['Aq'], 'L0_attn_Bq': _L0_attn_in['Bq'], 'L0_attn_Wk': _L0_attn_in['Wk'], 'L0_attn_bk': _L0_attn_in['bk'], 'L0_attn_Ak': _L0_attn_in['Ak'], 'L0_attn_Bk': _L0_attn_in['Bk'], 'L0_attn_Wv': _L0_attn_in['Wv'], 'L0_attn_bv': _L0_attn_in['bv'], 'L0_attn_Av': _L0_attn_in['Av'], 'L0_attn_Bv': _L0_attn_in['Bv'], 'L0_attn_Wo': _L0_attn_in['Wo'], 'L0_attn_bo': _L0_attn_in['bo'], 'L0_attn_Ao': _L0_attn_in['Ao'], 'L0_attn_Bo': _L0_attn_in['Bo'], 'L0_ffn_w_router': _L0_ffn_in['w_router'], 'L0_ffn_W1': _L0_ffn_in['W1'], 'L0_ffn_b1': _L0_ffn_in['b1'], 'L0_ffn_W2': _L0_ffn_in['W2'], 'L0_ffn_b2': _L0_ffn_in['b2'], 'L0_ffn_Ws1': _L0_ffn_in['Ws1'], 'L0_ffn_bs1': _L0_ffn_in['bs1'], 'L0_ffn_Ws2': _L0_ffn_in['Ws2'], 'L0_ffn_bs2': _L0_ffn_in['bs2'], 'L0_c': _L0_c, 'L0_wmod': _L0_wmod, 'L1_attn_conv_w': _L1_attn_in['conv_w'], 'L1_attn_conv_b': _L1_attn_in['conv_b'], 'L1_attn_Win': _L1_attn_in['Win'], 'L1_attn_b_in': _L1_attn_in['b_in'], 'L1_attn_Wout': _L1_attn_in['Wout'], 'L1_attn_b_out': _L1_attn_in['b_out'], 'L1_attn_A_log': _L1_attn_in['A_log'], 'L1_ffn_dw_kernel': _L1_ffn_in['dw_kernel'], 'L1_ffn_dw_bias': _L1_ffn_in['dw_bias'], 'L1_ffn_pw_w': _L1_ffn_in['pw_w'], 'L1_ffn_pw_b': _L1_ffn_in['pw_b'], 'L1_ffn_router_w': _L1_ffn_in['router_w'], 'L1_ffn_router_b': _L1_ffn_in['router_b'], 'L1_ffn_expert_w': _L1_ffn_in['expert_w'], 'L1_ffn_expert_b': _L1_ffn_in['expert_b'], 'L1_ffn_out_w': _L1_ffn_in['out_w'], 'L1_ffn_out_b': _L1_ffn_in['out_b'], 'L1_ffn_norm_w': _L1_ffn_in['norm_w'], 'L1_ffn_ff_down_w': _L1_ffn_in['ff_down_w'], 'L1_ffn_ff_down_b': _L1_ffn_in['ff_down_b'], 'L1_ffn_ff_up_w': _L1_ffn_in['ff_up_w'], 'L1_ffn_ff_up_b': _L1_ffn_in['ff_up_b'], 'L1_c': _L1_c, 'L1_wmod': _L1_wmod}
    _x0 = _d['L0_attn_x']
    _d['L0_attn_x'] = jax.random.normal(jax.random.fold_in(jax.random.key(seed), 1), (8, 512, 128), dtype=_x0.dtype)
    del _x0
    return _d

def reference(L0_attn_x, L0_attn_Wq, L0_attn_bq, L0_attn_Aq, L0_attn_Bq, L0_attn_Wk, L0_attn_bk, L0_attn_Ak, L0_attn_Bk, L0_attn_Wv, L0_attn_bv, L0_attn_Av, L0_attn_Bv, L0_attn_Wo, L0_attn_bo, L0_attn_Ao, L0_attn_Bo, L0_ffn_w_router, L0_ffn_W1, L0_ffn_b1, L0_ffn_W2, L0_ffn_b2, L0_ffn_Ws1, L0_ffn_bs1, L0_ffn_Ws2, L0_ffn_bs2, L0_c, L0_wmod, L1_attn_conv_w, L1_attn_conv_b, L1_attn_Win, L1_attn_b_in, L1_attn_Wout, L1_attn_b_out, L1_attn_A_log, L1_ffn_dw_kernel, L1_ffn_dw_bias, L1_ffn_pw_w, L1_ffn_pw_b, L1_ffn_router_w, L1_ffn_router_b, L1_ffn_expert_w, L1_ffn_expert_b, L1_ffn_out_w, L1_ffn_out_b, L1_ffn_norm_w, L1_ffn_ff_down_w, L1_ffn_ff_down_b, L1_ffn_ff_up_w, L1_ffn_ff_up_b, L1_c, L1_wmod):

    def _L0_attn_ref(x, Wq, bq, Aq, Bq, Wk, bk, Ak, Bk, Wv, bv, Av, Bv, Wo, bo, Ao, Bo):
        import jax, jax.numpy as jnp
        import numpy as np
        EMBED = 128
        HEADS = 16
        HEAD_DIM = EMBED // HEADS
        RANK = 8
        ALPHA = 16
        SCALE_LORA = ALPHA / RANK

        def _lora_linear(x, W, b, A, B):
            return x @ W.T + b + SCALE_LORA * (x @ A.T @ B.T)
        N, S, _ = x.shape
        Q = _lora_linear(x, Wq, bq, Aq, Bq).reshape(N, S, HEADS, HEAD_DIM)
        K = _lora_linear(x, Wk, bk, Ak, Bk).reshape(N, S, HEADS, HEAD_DIM)
        V = _lora_linear(x, Wv, bv, Av, Bv).reshape(N, S, HEADS, HEAD_DIM)
        energy = jnp.einsum('nqhd,nkhd->nhqk', Q, K) / jnp.sqrt(jnp.float32(HEAD_DIM))
        attn = jax.nn.softmax(energy, axis=-1)
        out = jnp.einsum('nhqk,nkhd->nqhd', attn, V).reshape(N, S, EMBED)
        return _lora_linear(out, Wo, bo, Ao, Bo)

    def _L0_ffn_ref(x, w_router, W1, b1, W2, b2, Ws1, bs1, Ws2, bs2):
        import jax, jax.numpy as jnp
        import numpy as np
        import math
        D_MODEL, D_FF, N_EXPERTS, TOP_K, N_SHARED = (128, 512, 8, 2, 1)
        B, T = (4, 128)
        SCALE = 1.0 / math.sqrt(N_SHARED + TOP_K / N_EXPERTS)
        logits = jnp.einsum('btd,ed->bte', x, w_router)
        probs = jax.nn.softmax(logits, axis=-1)
        vals, idx = jax.lax.top_k(probs, TOP_K)
        gates = jnp.sum(jax.nn.one_hot(idx, N_EXPERTS, dtype=x.dtype) * vals[..., None], axis=-2)
        hs = jax.nn.gelu(jnp.einsum('btd,fd->btf', x, Ws1) + bs1)
        acc = jnp.einsum('btf,df->btd', hs, Ws2) + bs2
        h = jax.nn.gelu(jnp.einsum('btd,efd->btef', x, W1) + b1)
        y = jnp.einsum('btef,edf->bted', h, W2) + b2
        acc = acc + jnp.einsum('bted,bte->btd', y, gates)
        return SCALE * acc

    def _L1_attn_ref(x, conv_w, conv_b, Win, b_in, Wout, b_out, A_log):
        import jax, jax.numpy as jnp
        import numpy as np
        B, L, D, N, K, E = (8, 512, 128, 16, 4, 2)
        INNER = E * N

        def _selective_ssm(x, conv_w, conv_b, Win, b_in, Wout, b_out, A_log):
            bsz, seq_len, d_model = x.shape
            n = A_log.shape[0]
            inner = (Win.shape[1] - n) // 2
            pad = (conv_w.shape[2] - 1) // 2
            xc = jnp.transpose(x, (0, 2, 1))
            xc = jax.lax.conv_general_dilated(xc, conv_w, window_strides=(1,), padding=[(pad, pad)], dimension_numbers=('NCH', 'OIH', 'NCH'), feature_group_count=d_model)
            xc = xc + conv_b[None, :, None]
            Lc = xc.shape[2]
            if Lc < seq_len:
                xc = jnp.pad(xc, ((0, 0), (0, 0), (0, seq_len - Lc)))
            elif Lc > seq_len:
                xc = xc[:, :, :seq_len]
            xc = jnp.transpose(xc, (0, 2, 1))
            proj = xc @ Win + b_in
            delta = proj[..., :n]
            B_in = proj[..., n:n + inner].reshape(bsz, seq_len, n, -1).mean(axis=-1)
            C = proj[..., n + inner:].reshape(bsz, seq_len, n, -1).mean(axis=-1)
            A = -jnp.exp(A_log)[None, None, :]
            dA = jax.nn.softplus(delta) * A
            A_bar = jnp.exp(dA)
            eps = 0.0001
            A_safe = jnp.where(jnp.abs(A) < eps, eps * jnp.sign(A) + eps, A)
            taylor = 1.0 + dA / 2.0 + dA * dA / 6.0
            B_bar_scale = jnp.where(jnp.abs(A) < eps, taylor, (A_bar - 1.0) / A_safe)
            B_bar = B_bar_scale * B_in

            def combine(c1, c2):
                a1, b1 = c1
                a2, b2 = c2
                return (a1 * a2, a2 * b1 + b2)
            _, h = jax.lax.associative_scan(combine, (A_bar, B_bar), axis=1)
            y = C * h @ Wout + b_out
            return y
        return _selective_ssm(x, conv_w, conv_b, Win, b_in, Wout, b_out, A_log)

    def _L1_ffn_ref(x, dw_kernel, dw_bias, pw_w, pw_b, router_w, router_b, expert_w, expert_b, out_w, out_b, norm_w, ff_down_w, ff_down_b, ff_up_w, ff_up_b):
        import jax, jax.numpy as jnp
        import numpy as np
        from jax import lax
        B, L, D = (4, 256, 128)
        E, TOPK = (8, 2)
        K, DIL = (3, 1)
        HID = D // 4
        EPS = 1e-06

        def _rmsnorm(h, w):
            rms = jnp.sqrt(jnp.mean(h * h, axis=-1, keepdims=True) + EPS)
            return w * (h / rms)

        def _forward(x, dw_kernel, dw_bias, pw_w, pw_b, router_w, router_b, expert_w, expert_b, out_w, out_b, norm_w, ff_down_w, ff_down_b, ff_up_w, ff_up_b):
            pad = (K - 1) * DIL
            xc = jnp.transpose(x, (0, 2, 1))
            xc = lax.conv_general_dilated(xc, dw_kernel, window_strides=(1,), padding=((pad, 0),), rhs_dilation=(DIL,), dimension_numbers=('NCH', 'OIH', 'NCH'), feature_group_count=D) + dw_bias[None, :, None]
            xc = jax.nn.silu(jnp.einsum('bdl,ed->bel', xc, pw_w) + pw_b[None, :, None])
            x1 = x + jnp.transpose(xc, (0, 2, 1))
            logits = jnp.einsum('bsd,ed->bse', x1, router_w) + router_b
            top_v, top_i = lax.top_k(logits, TOPK)
            top_w = jax.nn.softmax(top_v, axis=-1)
            rw = jnp.sum(jax.nn.one_hot(top_i, E, dtype=x1.dtype) * top_w[..., None], axis=-2)
            ye = jax.nn.silu(jnp.einsum('bsd,eod->bseo', x1, expert_w) + expert_b)
            combined = jnp.einsum('bse,bseo->bso', rw, ye)
            moe_out = jnp.einsum('bsd,od->bso', combined, out_w) + out_b
            h = _rmsnorm(x1 + moe_out, norm_w)
            ff = jax.nn.gelu(jnp.einsum('bsd,hd->bsh', h, ff_down_w) + ff_down_b, approximate=False)
            ff = jnp.einsum('bsh,dh->bsd', ff, ff_up_w) + ff_up_b
            return h + ff
        return _forward(x, dw_kernel, dw_bias, pw_w, pw_b, router_w, router_b, expert_w, expert_b, out_w, out_b, norm_w, ff_down_w, ff_down_b, ff_up_w, ff_up_b)
    x = L0_attn_x
    mod = (_silu(L0_c) @ L0_wmod).reshape(L0_c.shape[0], 6, 1, -1)
    sa, ca, ga, sb, cb, gb = (mod[:, 0], mod[:, 1], mod[:, 2], mod[:, 3], mod[:, 4], mod[:, 5])
    ga = (2 * (ga >= 0) - 1) * jnp.maximum(jnp.abs(ga), 0.25)
    gb = (2 * (gb >= 0) - 1) * jnp.maximum(jnp.abs(gb), 0.25)
    h = _layernorm(x, axis=-1) * (1 + ca) + sa
    x = x + ga * _L0_attn_ref(h, L0_attn_Wq, L0_attn_bq, L0_attn_Aq, L0_attn_Bq, L0_attn_Wk, L0_attn_bk, L0_attn_Ak, L0_attn_Bk, L0_attn_Wv, L0_attn_bv, L0_attn_Av, L0_attn_Bv, L0_attn_Wo, L0_attn_bo, L0_attn_Ao, L0_attn_Bo)
    h = _layernorm(x, axis=-1) * (1 + cb) + sb
    x = x + gb * _L0_ffn_ref(h, L0_ffn_w_router, L0_ffn_W1, L0_ffn_b1, L0_ffn_W2, L0_ffn_b2, L0_ffn_Ws1, L0_ffn_bs1, L0_ffn_Ws2, L0_ffn_bs2)
    mod = (_silu(L1_c) @ L1_wmod).reshape(L1_c.shape[0], 6, 1, -1)
    sa, ca, ga, sb, cb, gb = (mod[:, 0], mod[:, 1], mod[:, 2], mod[:, 3], mod[:, 4], mod[:, 5])
    ga = (2 * (ga >= 0) - 1) * jnp.maximum(jnp.abs(ga), 0.25)
    gb = (2 * (gb >= 0) - 1) * jnp.maximum(jnp.abs(gb), 0.25)
    h = _layernorm(x, axis=-1) * (1 + ca) + sa
    x = x + ga * _L1_attn_ref(h, L1_attn_conv_w, L1_attn_conv_b, L1_attn_Win, L1_attn_b_in, L1_attn_Wout, L1_attn_b_out, L1_attn_A_log)
    h = _layernorm(x, axis=-1) * (1 + cb) + sb
    x = x + gb * _L1_ffn_ref(h, L1_ffn_dw_kernel, L1_ffn_dw_bias, L1_ffn_pw_w, L1_ffn_pw_b, L1_ffn_router_w, L1_ffn_router_b, L1_ffn_expert_w, L1_ffn_expert_b, L1_ffn_out_w, L1_ffn_out_b, L1_ffn_norm_w, L1_ffn_ff_down_w, L1_ffn_ff_down_b, L1_ffn_ff_up_w, L1_ffn_ff_up_b)
    return x

_drawn_inputs = setup_inputs


def setup_inputs(seed=0):
    import zlib

    import numpy as np

    out = dict(_drawn_inputs(seed))
    spreads = {'L0_attn_bq': (0.0, 0.8),
     'L0_attn_bk': (0.0, 2.0),
     'L0_attn_bv': (0.0, 0.8),
     'L0_attn_bo': (0.0, 0.306),
     'L1_attn_conv_b': (0.0, 0.593),
     'L1_attn_b_in': (0.0, 0.729),
     'L1_attn_b_out': (0.0, 0.333),
     'L1_attn_A_log': (0.0, 0.8),
     'L1_ffn_dw_bias': (0.0, 0.8),
     'L1_ffn_pw_b': (0.0, 0.633),
     'L1_ffn_router_b': (0.0, 0.8),
     'L1_ffn_expert_b': (0.0, 0.8),
     'L1_ffn_out_b': (0.0, 1.149),
     'L1_ffn_norm_w': (1.0, 0.2),
     'L1_ffn_ff_down_b': (0.0, 0.8),
     'L1_ffn_ff_up_b': (0.0, 0.336)}
    factors = {'L0_attn_Wq': 8.0,
     'L0_attn_Aq': 8.0,
     'L0_attn_Bq': 8.0,
     'L0_attn_Wk': 8.0,
     'L0_attn_Ak': 8.0,
     'L0_attn_Bk': 8.0,
     'L0_attn_Wv': 8.0,
     'L0_attn_Av': 8.0,
     'L0_attn_Bv': 8.0,
     'L0_attn_Wo': 8.0,
     'L0_attn_Ao': 8.0,
     'L0_attn_Bo': 8.0,
     'L0_ffn_b1': 43.116,
     'L0_ffn_b2': 32.77,
     'L0_ffn_bs1': 23.313,
     'L0_ffn_bs2': 8.0,
     'L1_ffn_dw_kernel': 8.0,
     'L1_ffn_pw_w': 8.0,
     'L1_ffn_router_w': 8.0,
     'L1_ffn_expert_w': 8.0,
     'L1_ffn_out_w': 8.0,
     'L1_ffn_ff_down_w': 8.0,
     'L1_ffn_ff_up_w': 8.0}
    for name, (base, spread) in spreads.items():
        noise = np.random.default_rng([zlib.crc32(name.encode()), seed]).standard_normal(out[name].shape)
        drawn = base * np.exp(spread * noise) if base else spread * noise
        out[name] = jnp.asarray(drawn.astype(out[name].dtype))
    for name, factor in factors.items():
        out[name] = (out[name] * factor).astype(out[name].dtype)
    return out
```

```python
from contextlib import ExitStack

import numpy as np

import concourse.bass as bass
from concourse import mybir

P = 128
NB = 8
NT = 32
F32 = mybir.dt.float32
BF16 = mybir.dt.bfloat16
ALU = mybir.AluOpType
ACT = mybir.ActivationFunctionType
AX = mybir.AxisListType

PACK0 = [("c", 16), ("wmod0", 768), ("ident", 128), ("bq", 1), ("bk", 1), ("WqT", 128), ("WkT", 128),
         ("WvT", 128), ("WoT", 128), ("bvB", 128), ("boB", 128)]
PACK1 = [("W1T", 4608), ("b1T", 36), ("wr0", 8), ("desc", 8)]
PACK2 = [("W2T", 4608)]
PACK3 = [("wmod1", 768), ("convw", 4), ("convb", 1), ("Win", 80), ("bin5", 5), ("Alog", 1), ("WoutBD", 1024),
         ("boutB", 128), ("dw", 3), ("dwb", 1), ("pwT", 128), ("pwb", 1), ("rw1T", 8), ("rb1B", 8),
         ("ewT", 1024), ("ebT", 8), ("owT", 128), ("obB", 128), ("nwB", 128), ("fdT", 32), ("fdb", 1),
         ("fuBD", 512), ("fubB", 128)]

QTERM = [0, 0, 1, 1, 0, 2]
KTERM = [0, 1, 0, 1, 2, 0]


def width(pack):
    return sum(w for _, w in pack)


class Op:

    def __init__(self, fn, waits, sem=None, val=None):
        self.fn, self.waits, self.sem, self.val = fn, waits, sem, val
        self.asked = False


class Queue:

    def __init__(self, sem):
        self.sem, self.ops, self.gate = sem, [], []

    def put(self, op):
        op.waits = flat(op.waits) + self.gate
        self.gate = []
        for w in op.waits:
            w.asked = True
        self.ops.append(op)
        return op

    def __call__(self, fn, *waits):
        return self.put(Op(fn, waits, self.sem))

    def dma(self, out, in_, dsem, *waits):
        dsem[1] += 16
        return self.put(Op(lambda e: e.dma_start(out, in_), waits, dsem[0], dsem[1]))

    def count(self):
        n = 0
        for op in self.ops:
            if op.sem is self.sem and op.asked:
                n += 1
                op.val = n

    def emit(self, eng):
        seen = {}
        for op in self.ops:
            need = {}
            for w in op.waits:
                need[id(w.sem)] = max(need.get(id(w.sem), (0, None))[0], w.val), w.sem
            for k, (v, s) in need.items():
                if seen.get(k, 0) < v:
                    eng.wait_ge(s, v)
                    seen[k] = v
            ins = op.fn(eng)
            if op.sem is not self.sem:
                ins.then_inc(op.sem, 16)
            elif op.asked:
                ins.then_inc(self.sem, 1)


def flat(ws):
    out = []
    for w in ws:
        if isinstance(w, (list, tuple)):
            out += flat(w)
        elif w is not None:
            out.append(w)
    return out


class Ring:

    def __init__(self, slots):
        self.slots, self.n, self.reader = list(slots), 0, {}

    def take(self):
        s = self.slots[self.n % len(self.slots)]
        self.n += 1
        return s, self.reader.get(s)

    def free(self, s, op):
        self.reader[s] = op


def adaln_kernel(nc, x_d, p0_d, p1_d, p2_d, p3_d, small_d, out_d):
    ctx = ExitStack()
    with ctx:
        def sem(name):
            return ctx.enter_context(nc.semaphore(name))

        def sb(name, shape, dt=F32, c=None):
            return (c or ctx).enter_context(nc.sbuf_tensor(name, shape, dt))

        pe, dve, act, pool, sp = (Queue(sem(n)) for n in ("s_pe", "s_dve", "s_act", "s_pool", "s_sp"))
        queues = [pe, dve, act, pool, sp]

        def dsem(name):
            return [sem(name), 0]

        def barrier():
            last = [q.ops[-1] for q in queues if q.ops]
            for q in queues:
                q.gate = q.gate + last
                for w in last:
                    w.asked = True

        PS = ctx.enter_context(nc.psum_tensor("PS", [P, 8, 512], F32))
        X = sb("X", [P, NT, P])
        p0 = sb("p0", [P, width(PACK0)])
        p1 = sb("p1", [P, width(PACK1)])
        small = sb("small", [9, 9 * P])
        stats = sb("stats", [P, NT, 6])
        lnw = sb("lnw", [P, 6, NT])
        cs = sb("cs", [P, 16])
        cst = sb("cst", [P, 3, 16])
        mf = sb("mf", [P, 2, 6, 8])
        mft = sb("mft", [P, 2, 2, 8])

        def views(t, pack):
            d, o = {}, 0
            for n, w in pack:
                d[n] = t[:, o:o + w]
                o += w
            return d

        W = views(p0, PACK0)
        W.update(views(p1, PACK1))
        ident = W["ident"]
        gbT0 = mf

        s_x = [dsem(f"s_x{i}") for i in range(4)]
        s_p0, s_p1, s_p2, s_p3, s_small = (dsem(n) for n in ("s_p0", "s_p1", "s_p2", "s_p3", "s_small"))
        ld_p0 = act.dma(p0[:], p0_d, s_p0)
        ld_x = [sp.dma(X[:, 8 * i:8 * i + 8, :], x_d[:, 8 * i:8 * i + 8, :], s_x[i]) for i in range(4)]
        ld_small = sp.dma(small[:], small_d, s_small)
        ld_p1 = sp.dma(p1[:], p1_d, s_p1)

        def clip_gate(out, g, t0, t1, *w):
            a = dve(lambda e: e.tensor_scalar(t0, g, 0.0, 2.0, ALU.is_ge, ALU.mult), *w)
            b = dve(lambda e: e.scalar_tensor_tensor(t1, t0, 1.0, g, ALU.subtract, ALU.mult), a)
            b = dve(lambda e: e.tensor_scalar(t1, t1, 0.25, None, ALU.max), b)
            return dve(lambda e: e.scalar_tensor_tensor(out, t0, 1.0, t1, ALU.subtract, ALU.mult), a, b)

        def mod_rows(L, k, wmod, dst, t0, t1, banks, *w):
            mms = []
            for b in range(8):
                o = PS[:, banks[b // 4], 128 * (b % 4):128 * (b % 4) + 128]
                l = cs[:, 8 * L + b:8 * L + b + 1].to_broadcast([P, P])
                mms.append(pe(lambda e, o=o, l=l: e.matmul(o, l, wmod[:, k * P:(k + 1) * P], start=True, stop=True), *w))
            g = PS[:, banks[0]:banks[0] + 2, :].rearrange("p a n -> p (a n)")
            return clip_gate(dst[:].rearrange("p b n -> p (b n)"), g, t0, t1, mms[-1])

        def mod_cols(L, wmod, bank, *w):
            o = PS[:, bank, 0:48].rearrange("p (k b) -> p k b", k=6)
            for k in range(6):
                m = pe(lambda e, k=k: e.matmul(o[:, k, :], wmod[:, k * P:(k + 1) * P], cs[:, 8 * L:8 * L + 8],
                                               start=True, stop=True), *w)
            c = dve(lambda e: e.tensor_copy(mf[:, L], o), m)
            r = []
            for k in (1, 4):
                r.append(dve(lambda e, k=k: e.tensor_scalar(mf[:, L, k], mf[:, L, k], 1.0, None, ALU.add), c))
            for k in (2, 5):
                r.append(clip_gate(mf[:, L, k], mf[:, L, k], mft[:, 0, k // 3], mft[:, 1, k // 3], c))
            return r

        def ln_stats(a, n, *w):
            for t in range(a, a + n):
                s = dve(lambda e, t=t: e.bn_stats(stats[:, t, :], X[:, t, :]), *w)
            me, mo, ve, vo = (stats[:, a:a + n, i] for i in (1, 4, 2, 5))
            m, d, v, sd, rs, nm = (lnw[:, i, a:a + n] for i in range(6))
            o1 = dve(lambda e: e.tensor_tensor(m, me, mo, ALU.add), s)
            o2 = dve(lambda e: e.tensor_tensor(d, me, mo, ALU.subtract), s)
            o3 = dve(lambda e: e.tensor_tensor(v, ve, vo, ALU.add), s)
            o4 = dve(lambda e: e.scalar_tensor_tensor(d, d, 0.25, d, ALU.mult, ALU.mult), o2)
            o5 = dve(lambda e: e.scalar_tensor_tensor(v, v, 1.0 / 128, d, ALU.mult, ALU.add), o3, o4)
            o6 = dve(lambda e: e.tensor_scalar(v, v, 1e-5, None, ALU.add), o5)
            o7 = act(lambda e: e.activation(sd, v, ACT.Sqrt), o6)
            o8 = dve(lambda e: e.reciprocal(rs, sd), o7)
            return dve(lambda e: e.scalar_tensor_tensor(nm, m, -0.5, rs, ALU.mult, ALU.mult), o8)

        def ln_batch(b, st, Z, zr, banks, dst, scale, shift, eng, *w):
            z, zfree = zr.take()
            for t in range(4):
                i = 4 * b + t
                o = eng(lambda e, i=i, t=t: e.tensor_scalar(Z[:, z, t, :], X[:, i, :], lnw[:, 4, i:i + 1],
                                                            lnw[:, 5, i:i + 1], ALU.mult, ALU.add), st, zfree, *w)
            bk, bfree = banks.take()
            for t in range(4):
                m = pe(lambda e, t=t: e.transpose(PS[:, bk, t * P:(t + 1) * P], Z[:, z, t, :], ident), o, bfree)
            zr.free(z, m)
            h = act(lambda e: e.activation(dst, PS[:, bk, :], ACT.Identity, bias=shift, scale=scale), m, *w)
            banks.free(bk, h)
            return h, o

        o = act(lambda e: e.activation(cst[:, 0], W["c"], ACT.Exp, scale=-1.0), ld_p0)
        o = dve(lambda e: e.tensor_scalar(cst[:, 1], cst[:, 0], 1.0, None, ALU.add), o)
        o = dve(lambda e: e.reciprocal(cst[:, 2], cst[:, 1]), o)
        cs_ok = dve(lambda e: e.tensor_tensor(cs[:], W["c"], cst[:, 2], ALU.mult), o, ld_p0)
        mc0 = mod_cols(0, W["wmod0"], 0, cs_ok, ld_p0)

        def attention():
            A = ExitStack()
            Q = sb("Q", [P, 3, 16, 512], BF16, A)
            K = sb("K", [P, 3, 8, 512], BF16, A)
            E = sb("E", [P, 2, 4, 2, 512], F32, A)
            V = sb("V", [P, 3, 4, 16, 9], F32, A)
            Wq, Wk, Wv, Wo = (sb(n, [P, P], F32, A) for n in ("Wq", "Wk", "Wv", "Wo"))
            bqs = sb("bqs", [P, 2], F32, A)
            GA = sb("GA", [P, 8, P], F32, A)
            GB = sb("GB", [P, 8, P], F32, A)
            Z = sb("Z", [P, 1, 4, P], F32, A)
            hT = sb("hT", [P, 1, 512], F32, A)
            qf = sb("qf", [P, 2, 512], F32, A)
            SPL = sb("SPL", [P, 2, 3, 512], BF16, A)
            mx = sb("mx", [P, 2, 4, 16], F32, A)
            nmf = sb("nmf", [8, 512], F32, A)
            nms = sb("nms", [8, 3, 512], BF16, A)
            ov = sb("ov", [P, 2, 512], F32, A)
            rec = sb("rec", [P, 4, 4], F32, A)
            otok = sb("otok", [P, 4, P], F32, A)
            oT = sb("oT", [P, 512], F32, A)
            dqk = nc.dram_tensor("dqk", [8, 2, 3, P, 512], BF16, kind="Internal").ap()
            dmx = nc.dram_tensor("dmx", [8, 2, 3, 8, 512], BF16, kind="Internal").ap()

            SC = float(1.0 / np.sqrt(np.float32(8.0)))
            t0 = E[:, 0].rearrange("p a b n -> p (a b n)")[:, 0:1024]
            t1 = E[:, 0].rearrange("p a b n -> p (a b n)")[:, 1024:2048]
            ga_ok = mod_rows(0, 2, W["wmod0"], GA, t0, t1, [2, 3], cs_ok, ld_p0)
            gb_ok = pool(lambda e: e.tensor_tensor(GB[:], GA[:], W["boB"].unsqueeze(1).to_broadcast([P, 8, P]), ALU.mult), ga_ok)
            weff = {}
            for i in range(4):
                m = pe(lambda e, i=i: e.matmul(PS[:, 1, i * P:(i + 1) * P], small[0:8, i * P:(i + 1) * P],
                                               small[0:8, (4 + i) * P:(5 + i) * P], start=True, stop=True), ld_small)
            for i, (n, dst) in enumerate((("q", Wq), ("k", Wk), ("v", Wv), ("o", Wo))):
                weff[n] = dve(lambda e, i=i, n=n, dst=dst: e.scalar_tensor_tensor(
                    dst[:], PS[:, 1, i * P:(i + 1) * P], 2.0, W[f"W{n}T"], ALU.mult, ALU.add), m, ld_p0)
            bqs_ok = [dve(lambda e: e.tensor_scalar(bqs[:, 0:1], W["bq"], SC, None, ALU.mult), ld_p0),
                      dve(lambda e: e.tensor_copy(bqs[:, 1:2], W["bk"]), ld_p0)]
            vz = [pool(lambda e, i=i: e.memset(V[:, i, :, :, 8:9], 1.0)) for i in range(3)]
            oz = dve(lambda e: e.memset(PS[:, 6, :], 0.0))
            qz = [pool(lambda e, i=i: e.memset(Q[:, i], 0.0)) for i in range(3)]
            kz = [dve(lambda e, i=i: e.memset(K[96:99, i], 1.0)) for i in range(3)]

            st = ln_stats(0, NT, ld_x)

            misc = Ring([7])
            zr = Ring([0])
            hr = Ring([0])
            fr = Ring([0, 1])
            sr = Ring([0, 1])
            mring = Ring([4, 5])
            sring = Ring([0, 2])
            ering = Ring([0, 1])
            ovr = Ring([0, 1])
            pvring = Ring([6])
            s_w = [dsem(f"s_w{i}") for i in range(2)]
            s_q = [dsem(f"s_q{i}") for i in range(3)]
            s_mw = [dsem(f"s_mw{i}") for i in range(2)]
            s_m = [dsem(f"s_m{i}") for i in range(2)]
            S = {}

            def split(src, dst, eng, *w):
                a = eng(lambda e: e.tensor_copy(dst[:, 0], src), *w)
                b = eng(lambda e: e.tensor_tensor(src, src, dst[:, 0], ALU.subtract), a)
                c = eng(lambda e: e.tensor_copy(dst[:, 1], src), b)
                return eng(lambda e: e.tensor_tensor(dst[:, 2], src, dst[:, 1], ALU.subtract), c)

            def prep_h(b):
                h, _ = hr.take()
                hop, zop = ln_batch(b, st, Z, zr, misc, hT[:, h], mf[:, 0, 1, b:b + 1], mf[:, 0, 0, b:b + 1], pool,
                                    mc0, hr.reader.get(h))
                S[b, "h"] = h, hop
                xv = X[:, 4 * b:4 * b + 4, :]
                S[b, "xb"] = pool(lambda e: e.tensor_tensor(xv, xv, GB[:, b:b + 1, :].to_broadcast([P, 4, P]), ALU.add), zop, gb_ok)

            def prep_qk(b, i):
                h, hop = S[b, "h"]
                bk, bf = misc.take()
                w, wop = ((Wq, weff["q"]), (Wk, weff["k"]))[i]
                m = pe(lambda e: e.matmul(PS[:, bk, :], w[:], hT[:, h], start=True, stop=True), hop, wop, bf)
                f, ff = fr.take()
                a = act(lambda e: e.activation(qf[:, f], PS[:, bk, :], ACT.Identity, bias=bqs[:, i:i + 1],
                                               scale=(SC, 1.0)[i]), m, bqs_ok, ff)
                misc.free(bk, a)
                s, sf = sr.take()
                d = split(qf[:, f], SPL[:, s], pool, a, sf)
                fr.free(f, d)
                wr = sp.dma(dqk[b, i].rearrange("t p n -> p t n"), SPL[:, s], s_w[i], d)
                sr.free(s, wr)
                u = b % 3
                prev = S.get((b - 3, "E"))
                for par in range(2):
                    for t in range(6):
                        src = dqk[b, i, (QTERM, KTERM)[i][t]].rearrange("(p two d) n -> two d p n", two=2, d=8)[par]
                        r = slice(par * 48 + t * 8, par * 48 + t * 8 + 8)
                        dst = Q[r, u, par:16:2, :] if i == 0 else K[r, u]
                        S[b, "qk"] = sp.dma(dst, src, s_q[u], wr, prev, qz[u] if i == 0 else None)

            def prep_v(b):
                h, hop = S[b, "h"]
                bk, bf = misc.take()
                for t in range(4):
                    m = pe(lambda e, t=t: e.matmul(PS[:, bk, t * P:(t + 1) * P], hT[:, h, t * P:(t + 1) * P], Wv[:],
                                                   start=True, stop=True), hop, weff["v"], bf)
                hr.free(h, m)
                v = b % 3
                S[b, "v"] = dve(lambda e: e.tensor_tensor(
                    V[:, v, :, :, 0:8], PS[:, bk, :].rearrange("p (t h d) -> p t h d", t=4, h=16),
                    W["bvB"].rearrange("p (h d) -> p h d", h=16).unsqueeze(1).to_broadcast([P, 4, 16, 8]), ALU.add),
                    m, vz, S.get((b - 3, "pv")))
                misc.free(bk, S[b, "v"])

            def max_unit(b, i):
                h, qt = i // 4, i % 4
                u = b % 3
                bk, bf = mring.take()
                m = pe(lambda e: e.matmul(PS[:, bk, :], Q[0:96, u, h, qt * P:(qt + 1) * P], K[0:96, u, h // 2, :],
                                          start=True, stop=True), S[b, "qk"], bf)
                r = dve(lambda e: e.tensor_reduce(mx[:, b % 2, qt, h:h + 1], PS[:, bk, :], AX.X, ALU.max), m,
                        S.get((b - 2, "mt")))
                mring.free(bk, r)
                S[b, "mx"] = r

            def max_rows(b, half):
                bk, bf = misc.take()
                for t in range(4):
                    m = pe(lambda e, t=t: e.transpose(PS[0:8, bk, t * P:(t + 1) * P], mx[:, b % 2, t, 8 * half:8 * half + 8],
                                                      ident), S[b, "mx"], bf)
                S[b, "mt"] = m
                a = act(lambda e: e.mul(nmf[:], PS[0:8, bk, :], -1.0), m, S.get("nm"))
                misc.free(bk, a)
                d = split(nmf[:], nms, pool, a, S.get("mw"))
                S["nm"] = d
                wr = sp.dma(dmx[b, half].rearrange("t h n -> h t n"), nms[:], s_mw[half], d)
                S["mw"] = wr
                S[b, "m", half] = sp.dma(Q[96:99, b % 3, 8 * half:8 * half + 8, :], dmx[b, half], s_m[half], wr)

            def exp_unit(b, i):
                g, kp, j = i // 8, i // 4 % 2, i % 4
                h, u = 4 * g + j, b % 3
                bk, bf = sring.take()
                for c in range(2):
                    kt = 2 * kp + c
                    m = pe(lambda e, c=c, kt=kt: e.matmul(
                        PS[:, bk + c, :], K[0:99, u, h // 2, kt * P:(kt + 1) * P], Q[0:99, u, h, :],
                        start=True, stop=True), S[b, "qk"], S[b, "m", h // 8], kz, bf)
                S[b, "E"] = m
                if j == 0:
                    S["e"] = ering.take()
                es, ef = S["e"]
                a = act(lambda e: e.activation(E[:, es, j], PS[:, bk:bk + 2, :], ACT.Exp), m, ef)
                sring.free(bk, a)
                return es, a

            def pv(b, g, kp, c, es, a):
                kt = 2 * kp + c
                if kt == 0:
                    S["pvb"] = pvring.take()
                bk, bf = S["pvb"]
                for j in range(4):
                    m = pe(lambda e, j=j: e.matmul(PS[32 * j:32 * j + 9, bk, :], V[:, b % 3, kt, 4 * g + j, :],
                                                   E[:, es, j, c, :], start=(kt == 0), stop=(kt == 3)),
                           a, S[b, "v"], bf, oz)
                S[b, "pv"] = m
                if c == 1:
                    ering.free(es, m)
                if kt == 3:
                    o, of = ovr.take()
                    cp = act(lambda e: e.activation(ov[:, o], PS[:, bk, :], ACT.Copy), m, of)
                    pvring.free(bk, cp)
                    S["ov"] = o, cp

            def heads_out(b, g):
                o, cp = S["ov"]
                bk, bf = misc.take()
                for t in range(4):
                    m = pe(lambda e, t=t: e.transpose(PS[:, bk, t * P:(t + 1) * P], ov[:, o, t * P:(t + 1) * P], ident), cp, bf)
                ovr.free(o, m)
                v = PS[:, bk, :].rearrange("p (t j r) -> p t j r", t=4, j=4)
                r = dve(lambda e: e.reciprocal(rec[:], v[:, :, :, 8]), m)
                S["o", g] = dve(lambda e: e.tensor_tensor(
                    otok[:].rearrange("p t (g j d) -> p t g j d", g=4, j=4)[:, :, g], v[:, :, :, 0:8],
                    rec[:].unsqueeze(3).to_broadcast([P, 4, 4, 8]), ALU.mult), r, S.get("otr"))
                misc.free(bk, S["o", g])

            def out_turn(b):
                bk, bf = misc.take()
                for t in range(4):
                    m = pe(lambda e, t=t: e.transpose(PS[:, bk, t * P:(t + 1) * P], otok[:, t, :], ident), S["o", 3], bf)
                S["otr"] = m
                S["oT"] = act(lambda e: e.activation(oT[:], PS[:, bk, :], ACT.Copy), m, S.get("om"))
                misc.free(bk, S["oT"])

            def out_proj(b):
                bk, bf = misc.take()
                for t in range(4):
                    m = pe(lambda e, t=t: e.matmul(PS[:, bk, t * P:(t + 1) * P], oT[:, t * P:(t + 1) * P], Wo[:],
                                                   start=True, stop=True), S["oT"], weff["o"], bf)
                S["om"] = m
                v = PS[:, bk, :].rearrange("p (t n) -> p t n", t=4)
                xv = X[:, 4 * b:4 * b + 4, :]
                a = dve(lambda e: e.tensor_tensor(v, v, GA[:, b:b + 1, :].to_broadcast([P, 4, P]), ALU.mult), m, ga_ok)
                S["x", b] = dve(lambda e: e.tensor_tensor(xv, v, xv, ALU.add), a, S[b, "xb"])
                misc.free(bk, S["x", b])

            def prep_step(b, i):
                if b >= NB:
                    return
                if i == 2:
                    prep_h(b)
                if i == 6:
                    prep_qk(b, 0)
                if i == 10:
                    prep_qk(b, 1)
                if i == 14:
                    prep_v(b)

            for b in range(2):
                for i in (2, 6, 10, 14):
                    prep_step(b, i)
            for i in range(64):
                max_unit(0, i)
                if i == 33:
                    max_rows(0, 0)
            max_rows(0, 1)
            pend = []
            late = []
            for b in range(NB):
                for i in range(32):
                    es, a = exp_unit(b, i)
                    if b + 1 < NB:
                        max_unit(b + 1, 2 * i)
                        max_unit(b + 1, 2 * i + 1)
                        if i == 17:
                            max_rows(b + 1, 0)
                    if pend and i % 2 == 1:
                        pend.pop(0)()
                    if i % 4 == 3:
                        g, kp = i // 8, i // 4 % 2
                        for c in range(2):
                            pend.append(lambda b=b, g=g, kp=kp, c=c, es=es, a=a: pv(b, g, kp, c, es, a))
                        if kp == 1:
                            late.append((32 * b + i + 7, lambda b=b, g=g: heads_out(b, g)))
                            if g == 3:
                                late.append((32 * b + i + 9, lambda b=b: out_turn(b)))
                                late.append((32 * b + i + 12, lambda b=b: out_proj(b)))
                    while late and late[0][0] <= 32 * b + i:
                        late.pop(0)[1]()
                    prep_step(b + 2, i)
                if b + 1 < NB:
                    max_rows(b + 1, 1)
            for f in pend:
                f()
            for _, f in late:
                f()
            barrier()
            A.close()

        attention()

        def route(L, lg, M, gates, wk, *w):
            oh1, oh2, t, w2 = (wk[:, i] for i in range(4))
            m1, m2, s = (lnw[:, i, :] for i in range(3))
            bc = lambda a: a.unsqueeze(2).to_broadcast([P, NT, 8])
            desc = W["desc"].unsqueeze(1).to_broadcast([P, NT, 8])

            def first(src, m, oh, *w):
                a = dve(lambda e: e.tensor_reduce(m, src, AX.X, ALU.max), *w)
                a = dve(lambda e: e.tensor_tensor(t, src, bc(m), ALU.is_equal), a)
                a = dve(lambda e: e.tensor_tensor(t, t, desc, ALU.mult), a, ld_p1)
                a = dve(lambda e: e.tensor_reduce(s, t, AX.X, ALU.max), a)
                return dve(lambda e: e.tensor_tensor(oh, t, bc(s), ALU.is_equal), a)
            a = first(M, m1, oh1, *w)
            a = dve(lambda e: e.tensor_scalar(w2, oh1, -3.0e38, None, ALU.mult), a)
            a = dve(lambda e: e.tensor_tensor(w2, w2, M, ALU.add), a)
            a = first(w2, m2, oh2, a)
            return a, m1, m2, oh1, oh2, t, bc

        def ffn0():
            B = ExitStack()
            p2 = sb("p2", [P, width(PACK2)], F32, B)
            W2T = p2[:].rearrange("p (e f d) -> p e f d", e=9, f=4)
            H = sb("H", [P, 8, 512], F32, B)
            Z = sb("Zb", [P, 2, 4, P], F32, B)
            G = sb("G", [P, 2, 4, 512], F32, B)
            gbs = sb("gbs", [P, 2, 512], F32, B)
            ty = sb("ty", [P, 2, 512], F32, B)
            acc = sb("acc", [P, 2, 512], F32, B)
            gt = sb("gt", [P, NT, 9], F32, B)
            lg = sb("lg", [P, NT, 8], F32, B)
            wk = sb("wk", [P, 4, NT, 8], F32, B)
            gT = sb("gT", [9, 2, 512], F32, B)
            gsc = sb("gsc", [P, 8], F32, B)
            ld_p2 = sp.dma(p2[:], p2_d, s_p2)

            SCALE = float(1.0 / np.sqrt(1.25))
            gsc_ok = dve(lambda e: e.tensor_scalar(gsc[:], mf[:, 0, 5, :], SCALE, None, ALU.mult), mc0)
            st = ln_stats(0, NT)
            zr, banks = Ring([0, 1]), Ring([5, 6, 7])
            hs = []
            for b in range(NB):
                h, _ = ln_batch(b, st, Z, zr, banks, H[:, b], mf[:, 0, 4, b:b + 1], mf[:, 0, 3, b:b + 1], (dve, pool)[b % 2])
                hs.append(h)
                for t in range(4):
                    i = 4 * b + t
                    m = pe(lambda e, i=i, b=b, t=t: e.matmul(PS[:, 4, 8 * i:8 * i + 8], H[:, b, t * P:(t + 1) * P], W["wr0"],
                                                             start=True, stop=True), h, ld_p1)
            LG = PS[:, 4, 0:256].rearrange("p (t e) -> p t e", e=8)
            mxl, sm = lnw[:, 0, :], lnw[:, 1, :]
            bc = lambda a: a.unsqueeze(2).to_broadcast([P, NT, 8])
            a = dve(lambda e: e.tensor_reduce(mxl, LG, AX.X, ALU.max), m)
            a = dve(lambda e: e.tensor_tensor(lg[:], LG, bc(mxl), ALU.subtract), a)
            a = act(lambda e: e.activation(lg[:], lg[:], ACT.Exp), a)
            a = dve(lambda e: e.tensor_reduce(sm, lg[:], AX.X, ALU.add), a)
            a = dve(lambda e: e.reciprocal(mxl, sm), a)
            a = dve(lambda e: e.tensor_tensor(lg[:], lg[:], bc(mxl), ALU.mult), a)
            a, m1, m2, oh1, oh2, tt, bc = route(0, None, lg[:], gt, wk, a)
            a = dve(lambda e: e.tensor_tensor(oh1, oh1, oh2, ALU.add), a)
            a = dve(lambda e: e.tensor_tensor(gt[:, :, 0:8], oh1, lg[:], ALU.mult), a)
            gt_ok = dve(lambda e: e.memset(gt[:, :, 8:9], 1.0), a)

            def bcast_gates(b, e_, bk, w):
                for t in range(4):
                    m = pe(lambda e, t=t: e.transpose(PS[:, bk, t * P:(t + 1) * P],
                                                      gt[:, 4 * b + t, e_:e_ + 1].to_broadcast([P, P]), ident), w, gt_ok)
                return m

            upr, dnr, gbr = Ring([0, 1, 2]), Ring([3, 4]), Ring([5, 6])
            miscb = Ring([7])
            miscb.free(7, hs[-1])
            gr, gsr, tyr, accr, gTr = Ring([0, 1]), Ring([0, 1]), Ring([0, 1]), Ring([0, 1]), Ring([0, 1])
            for k in (4,):
                dnr.free(k, gt_ok)
            for k in (5, 6):
                gbr.free(k, hs[-1])
            b1T = W["b1T"].rearrange("p (e f) -> p e f", e=9)
            W1T = W["W1T"].rearrange("p (e f n) -> p e f n", e=9, f=4)
            work = [(b, e_) for b in range(NB) for e_ in (8, 0, 1, 2, 3, 4, 5, 6, 7)]
            G_ok, ST = {}, {}

            def up(b, e_, fc):
                if fc == 0:
                    ST["g", b, e_] = gr.take()
                g, gf = ST["g", b, e_]
                bk, bf = upr.take()
                m = pe(lambda e: e.matmul(PS[:, bk, :], W1T[:, e_, fc, :], H[:, b, :], start=True, stop=True), hs[b], bf)
                a = act(lambda e: e.activation(G[:, g, fc, :], PS[:, bk, :], ACT.Gelu_apprx_tanh,
                                               bias=b1T[:, e_, fc:fc + 1]), m, gf)
                upr.free(bk, a)
                G_ok[b, e_, fc] = a

            def gate_cols(b):
                bk, bf = miscb.take()
                for t in range(4):
                    m = pe(lambda e, t=t: e.transpose(PS[0:9, bk, t * P:(t + 1) * P], gt[:, 4 * b + t, :], ident), gt_ok, bf)
                g, gf = gTr.take()
                c = dve(lambda e: e.tensor_copy(gT[:, g], PS[0:9, bk, :]), m, gf)
                miscb.free(bk, c)
                ST["gT", b] = g, c

            def down(b, e_, fc):
                if fc == 0:
                    ST["d"] = dnr.take()
                bk, bf = ST["d"]
                g, _ = ST["g", b, e_]
                m = pe(lambda e: e.matmul(PS[:, bk, :], W2T[:, e_, fc, :], G[:, g, fc, :], start=(fc == 0),
                                          stop=(fc == 3 and e_ != 8)), G_ok[b, e_, fc], bf, ld_p2)
                if fc < 3:
                    return
                gr.free(g, m)
                if e_ == 8:
                    q, c = ST["gT", b]
                    m = pe(lambda e: e.matmul(PS[:, bk, :], small[:, 8 * P:9 * P], gT[:, q], start=False, stop=True), c)
                    gTr.free(q, m)
                    s, sf = accr.take()
                    ST["acc"] = s
                    a = dve(lambda e: e.tensor_copy(acc[:, s], PS[:, bk, :]), m, sf)
                else:
                    s = ST["acc"]
                    gb, gbf = gbr.take()
                    mg = bcast_gates(b, e_, gb, gbf)
                    q, qf_ = gsr.take()
                    cp = act(lambda e: e.activation(gbs[:, q], PS[:, gb, :], ACT.Copy), mg, qf_)
                    gbr.free(gb, cp)
                    y, yf = tyr.take()
                    mu = dve(lambda e: e.tensor_tensor(ty[:, y], PS[:, bk, :], gbs[:, q], ALU.mult), m, cp, yf)
                    gsr.free(q, mu)
                    a = pool(lambda e: e.tensor_tensor(acc[:, s], acc[:, s], ty[:, y], ALU.add), mu, ST["a"])
                    tyr.free(y, a)
                    dnr.free(bk, mu)
                if e_ == 8:
                    dnr.free(bk, a)
                ST["a"] = a

            def finish(b):
                s, a = ST["acc"], ST["a"]
                o = dve(lambda e: e.tensor_scalar(acc[:, s], acc[:, s], gsc[:, b:b + 1], None, ALU.mult), a, gsc_ok)
                ST["f", b] = s, o

            def finish2(b):
                s, o = ST["f", b]
                bk, bf = miscb.take()
                for t in range(4):
                    m = pe(lambda e, t=t: e.transpose(PS[:, bk, t * P:(t + 1) * P], acc[:, s, t * P:(t + 1) * P], ident), o, bf)
                accr.free(s, m)
                xv = X[:, 4 * b:4 * b + 4, :]
                v = PS[:, bk, :].rearrange("p (t n) -> p t n", t=4)
                x = dve(lambda e: e.tensor_tensor(xv, v, xv, ALU.add), m)
                miscb.free(bk, x)

            for n in range(len(work) + 1):
                for fc in range(4):
                    if n < len(work):
                        up(*work[n], fc)
                    if n > 0:
                        down(*work[n - 1], fc)
                if n < len(work) and work[n][1] == 8:
                    gate_cols(work[n][0])
                if n > 0 and work[n - 1][1] == 7:
                    finish(work[n - 1][0])
                if n > 9 and work[n - 1][1] == 8:
                    finish2(work[n - 1][0] - 1)
            finish2(NB - 1)
            barrier()
            B.close()


        ffn0()

        def ssm():
            C = ExitStack()
            p3 = sb("p3", [P, width(PACK3)])
            W.update(views(p3, PACK3))
            ld_p3 = sp.dma(p3[:], p3_d, s_p3)
            GA1 = sb("GA1", [P, 8, P])
            GB1 = sb("GB1", [P, 8, P])
            Z = sb("Zc", [P, 2, 4, P])
            Hc = sb("Hc", [P, 8, 516], F32, C)
            XC = sb("XC", [P, 2, 512], F32, C)
            WP = sb("WP", [P, 3, 240], F32, C)
            tb = sb("tb", [P, 12, 512], F32, C)
            cv = sb("cv", [P, 12], F32, C)
            tA, tB = tb[:, 0:2].rearrange("p a n -> p (a n)"), tb[:, 2:4].rearrange("p a n -> p (a n)")
            mc1 = mod_cols(1, W["wmod1"], 0, ld_p3)
            g1 = mod_rows(1, 2, W["wmod1"], GA1, tA, tB, [1, 2], ld_p3)
            g2 = mod_rows(1, 5, W["wmod1"], GB1, tA, tB, [3, 4], ld_p3, g1)

            z0 = pool(lambda e: e.memset(WP[:], 0.0))
            Win = W["Win"]
            pr = lambda o: Win[:, o:o + 32].rearrange("p (n k) -> p n k", k=2)
            a = dve(lambda e: e.tensor_copy(WP[:, 0, 112:128], Win[:, 0:16]), z0, ld_p3)
            wp_ok = [a]
            for i, o in ((1, 16), (2, 48)):
                a = dve(lambda e, i=i, o=o: e.tensor_tensor(WP[:, i, 112:128], pr(o)[:, :, 0], pr(o)[:, :, 1], ALU.add), z0)
                wp_ok.append(dve(lambda e, i=i: e.tensor_scalar(WP[:, i, 112:128], WP[:, i, 112:128], 0.5, None, ALU.mult), a))
            b5 = W["bin5"]
            c_ok = []
            for i in range(2):
                a = dve(lambda e, i=i: e.tensor_tensor(cv[:, i:i + 1], b5[:, 1 + 2 * i:2 + 2 * i], b5[:, 2 + 2 * i:3 + 2 * i], ALU.add), ld_p3)
                c_ok.append(dve(lambda e, i=i: e.tensor_scalar(cv[:, i:i + 1], cv[:, i:i + 1], 0.5, None, ALU.mult), a))
            a = act(lambda e: e.activation(cv[:, 6:7], W["Alog"], ACT.Exp), ld_p3)
            a = dve(lambda e: e.tensor_scalar(cv[:, 2:3], cv[:, 6:7], -1.0, None, ALU.mult), a)
            a3 = dve(lambda e: e.tensor_scalar(cv[:, 3:4], cv[:, 6:7], 1e-4, None, ALU.is_lt), a)
            a = dve(lambda e: e.tensor_scalar(cv[:, 7:8], cv[:, 3:4], -1.0, 1.0, ALU.mult, ALU.add), a3)
            a = dve(lambda e: e.scalar_tensor_tensor(cv[:, 8:9], cv[:, 2:3], cv[:, 7:8], cv[:, 3:4], ALU.mult, ALU.add), a)
            a = dve(lambda e: e.reciprocal(cv[:, 9:10], cv[:, 8:9]), a)
            a4 = dve(lambda e: e.tensor_tensor(cv[:, 4:5], cv[:, 9:10], cv[:, 7:8], ALU.mult), a)
            a5 = dve(lambda e: e.tensor_tensor(cv[:, 5:6], cv[:, 2:3], cv[:, 3:4], ALU.mult), a3)

            st = ln_stats(0, NT)
            zr, banks = Ring([0, 1]), Ring([5, 6, 7])
            p0z = pool(lambda e: e.memset(Hc[:, :, 0:1], 0.0))
            p1z = pool(lambda e: e.memset(Hc[:, :, 513:516], 0.0))
            p2z = pool(lambda e: e.memset(XC[:], 0.0))
            xr = Ring([0, 1])
            cw = W["convw"]
            bank_free = [c for c in mc1] + [g1, g2]
            for b in range(NB):
                h, _ = ln_batch(b, st, Z, zr, banks, Hc[:, b, 1:513], mf[:, 1, 1, b:b + 1], mf[:, 1, 0, b:b + 1],
                                (dve, pool)[b % 2], mc1)
                x, xf = xr.take()
                o = XC[:, x, 0:511]
                a = dve(lambda e, b=b, o=o: e.tensor_scalar(o, Hc[:, b, 0:511], cw[:, 0:1], W["convb"], ALU.mult, ALU.add),
                        h, p0z, p1z, p2z, xf)
                for k in range(1, 4):
                    a = dve(lambda e, b=b, o=o, k=k: e.scalar_tensor_tensor(o, Hc[:, b, k:k + 511], cw[:, k:k + 1], o,
                                                                            ALU.mult, ALU.add), a)
                for i in range(3):
                    m = pe(lambda e, i=i, b=b, x=x: e.matmul(PS[:, i, :], WP[:, i, 112 - 16 * b:240 - 16 * b], XC[:, x, :],
                                                             start=(b == 0), stop=(b == 7)), a, wp_ok, bank_free)
                xr.free(x, m)
            T = lambda i: tb[:, i, :]
            z_ = dve(lambda e: e.tensor_scalar(T(0), PS[:, 0, :], b5[:, 0:1], None, ALU.add), m)
            a = dve(lambda e: e.scalar_tensor_tensor(T(1), T(0), -1.0, T(0), ALU.mult, ALU.max), z_)
            a = act(lambda e: e.activation(T(2), T(1), ACT.Exp, scale=-1.0), a)
            a = act(lambda e: e.activation(T(3), T(2), ACT.Ln, bias=1.0), a)
            spl = dve(lambda e: e.scalar_tensor_tensor(T(4), T(0), 0.0, T(3), ALU.max, ALU.add), a)
            ab = act(lambda e: e.activation(T(5), T(4), ACT.Exp, scale=cv[:, 2:3]), spl, a5)
            u = dve(lambda e: e.tensor_scalar(T(1), T(5), -1.0, cv[:, 4:5], ALU.add, ALU.mult), ab, a4)
            d = dve(lambda e: e.tensor_scalar(T(6), T(4), cv[:, 5:6], None, ALU.mult), spl)
            q = dve(lambda e: e.tensor_scalar(T(7), T(6), 1.0 / 6.0, 0.5, ALU.mult, ALU.add), d)
            q = dve(lambda e: e.tensor_tensor(T(7), T(7), T(6), ALU.mult), q)
            q = dve(lambda e: e.tensor_scalar(T(7), T(7), 1.0, cv[:, 3:4], ALU.add, ALU.mult), q)
            q = dve(lambda e: e.tensor_tensor(T(1), T(1), T(7), ALU.add), q, u)
            q = dve(lambda e: e.scalar_tensor_tensor(T(8), PS[:, 1, :], cv[:, 0:1], T(1), ALU.add, ALU.mult), q, c_ok)
            q = dve(lambda e: e.tensor_tensor_scan(T(9), T(5), T(8), 0.0, ALU.mult, ALU.add), q)
            q = dve(lambda e: e.scalar_tensor_tensor(T(10), PS[:, 2, :], cv[:, 1:2], T(9), ALU.add, ALU.mult), q)
            WO = W["WoutBD"].rearrange("p (b n) -> p b n", b=8)
            yr = Ring([3, 4, 5, 6])
            tr = Ring([0, 2, 4, 6])
            for t in range(4):
                for hf in range(2):
                    bk, bf = yr.take()
                    m = pe(lambda e, t=t, hf=hf, bk=bk: e.matmul(PS[:, bk, :], tb[:, 10, t * P:(t + 1) * P],
                                                                 WO[:, 4 * hf:4 * hf + 4, :], start=True, stop=True), q, bf)
                    xv = X[:, 16 * hf + t:16 * hf + 16:4, :] if 16 * hf + 16 <= NT else None
                    v = PS[:, bk, :].rearrange("p (b n) -> p b n", b=4)
                    s, sf = tr.take()
                    tmp = tb[:, s, :].rearrange("p (b n) -> p b n", b=4)
                    a = dve(lambda e, v=v, tmp=tmp: e.tensor_tensor(
                        tmp, v, W["boutB"].unsqueeze(1).to_broadcast([P, 4, P]), ALU.add), m, sf, q)
                    yr.free(bk, a)
                    a = dve(lambda e, tmp=tmp, hf=hf: e.tensor_tensor(tmp, tmp, GA1[:, 4 * hf:4 * hf + 4, :], ALU.mult), a)
                    a = dve(lambda e, tmp=tmp, xv=xv: e.tensor_tensor(xv, xv, tmp, ALU.add), a)
                    tr.free(s, a)
            barrier()
            C.close()

            return GA1, GB1, Z

        GA1, GB1, Z = ssm()

        def ffn1():
            D = ExitStack()
            Hd = sb("Hd", [P, 8, 514], F32, D)
            XD = sb("XD", [P, 2, 512], F32, D)
            X1 = sb("X1", [P, 8, 512], F32, D)
            sx = sb("sx", [P, 2, 512], F32, D)
            gt = sb("gt1", [P, NT, 8], F32, D)
            lg = sb("lg1", [P, NT, 8], F32, D)
            wk = sb("wk1", [P, 4, NT, 8], F32, D)
            ye = sb("ye", [P, 2, 512], F32, D)
            gbs = sb("gbs1", [P, 2, 512], F32, D)
            ty = sb("ty1", [P, 2, 512], F32, D)
            acc = sb("acc1", [P, 2, 512], F32, D)
            HR = sb("HR", [P, NT, P], F32, D)
            hrT = sb("hrT", [P, 2, 512], F32, D)
            ff = sb("ff", [P, 2, 512], F32, D)
            tmpo = sb("tmpo", [P, 4, 4, P], F32, D)
            st = ln_stats(0, NT)
            zr, banks = Ring([0, 1]), Ring([4, 5])
            pz = pool(lambda e: e.memset(Hd[:, :, 0:2], 0.0))
            xr, pr_, sr = Ring([0, 1]), Ring([6, 7]), Ring([0, 1])
            dw = W["dw"]
            x1s = []
            for b in range(NB):
                h, _ = ln_batch(b, st, Z, zr, banks, Hd[:, b, 2:514], mf[:, 1, 4, b:b + 1], mf[:, 1, 3, b:b + 1],
                                (dve, pool)[b % 2])
                x, xf = xr.take()
                o = XD[:, x, :]
                a = dve(lambda e, b=b, o=o: e.tensor_scalar(o, Hd[:, b, 0:512], dw[:, 0:1], W["dwb"], ALU.mult, ALU.add),
                        h, pz, xf)
                for k in range(1, 3):
                    a = dve(lambda e, b=b, o=o, k=k: e.scalar_tensor_tensor(o, Hd[:, b, k:k + 512], dw[:, k:k + 1], o,
                                                                            ALU.mult, ALU.add), a)
                bk, bf = pr_.take()
                m = pe(lambda e, o=o, bk=bk: e.matmul(PS[:, bk, :], W["pwT"], o, start=True, stop=True), a, bf)
                xr.free(x, m)
                s, sf = sr.take()
                a = act(lambda e, s=s, bk=bk: e.activation(sx[:, s], PS[:, bk, :], ACT.Silu, bias=W["pwb"]), m, sf)
                pr_.free(bk, a)
                a = pool(lambda e, s=s, b=b: e.tensor_tensor(X1[:, b], sx[:, s], Hd[:, b, 2:514], ALU.add), a)
                sr.free(s, a)
                x1s.append(a)
                for t in range(4):
                    i = 4 * b + t
                    m = pe(lambda e, i=i, b=b, t=t: e.matmul(PS[:, 3, 8 * i:8 * i + 8], X1[:, b, t * P:(t + 1) * P],
                                                             W["rw1T"], start=True, stop=True), a)
            LG = PS[:, 3, 0:256].rearrange("p (t e) -> p t e", e=8)
            a = dve(lambda e: e.tensor_tensor(lg[:], LG, W["rb1B"].unsqueeze(1).to_broadcast([P, NT, 8]), ALU.add), m)
            a, m1, m2, oh1, oh2, tt, bc = route(1, None, lg[:], gt, wk, a)
            ed, w1, w2 = (lnw[:, i, :] for i in (3, 4, 5))
            a = dve(lambda e: e.tensor_tensor(ed, m2, m1, ALU.subtract), a)
            a = act(lambda e: e.activation(ed, ed, ACT.Exp), a)
            a = dve(lambda e: e.tensor_scalar(w2, ed, 1.0, None, ALU.add), a)
            a = dve(lambda e: e.reciprocal(w1, w2), a)
            a = dve(lambda e: e.tensor_tensor(w2, ed, w1, ALU.mult), a)
            a = dve(lambda e: e.tensor_tensor(oh1, oh1, bc(w1), ALU.mult), a)
            a = dve(lambda e: e.tensor_tensor(oh2, oh2, bc(w2), ALU.mult), a)
            gt_ok = dve(lambda e: e.tensor_tensor(gt[:], oh1, oh2, ALU.add), a)
            EW = W["ewT"].rearrange("p (e n) -> p e n", e=8)
            yr, gbr, mr, dnr = Ring([0, 1]), Ring([2, 4]), Ring([5, 6]), Ring([7])
            gbr.free(4, x1s[-1])
            yer, gsr, tyr, accr, hrr = Ring([0, 1]), Ring([0, 1]), Ring([0, 1]), Ring([0, 1]), Ring([0, 1])
            sq = lnw
            ffb = [3, 3]
            fm = {}
            ST = {}

            def expert(b, e_):
                bk, bf = yr.take()
                m = pe(lambda e: e.matmul(PS[:, bk, :], EW[:, e_, :], X1[:, b], start=True, stop=True), x1s[b], bf)
                y, yf = yer.take()
                a = act(lambda e: e.activation(ye[:, y], PS[:, bk, :], ACT.Silu, bias=W["ebT"][:, e_:e_ + 1]), m, yf)
                yr.free(bk, a)
                gb, gbf = gbr.take()
                for t in range(4):
                    mg = pe(lambda e, t=t: e.transpose(PS[:, gb, t * P:(t + 1) * P],
                                                       gt[:, 4 * b + t, e_:e_ + 1].to_broadcast([P, P]), ident), gbf, gt_ok)
                if e_ == 0:
                    ST["acc"] = accr.take()
                s, sf = ST["acc"]
                dst = acc[:, s] if e_ == 0 else ty[:, tyr.n % 2]
                yy, tf = (None, sf) if e_ == 0 else tyr.take()
                mu = dve(lambda e: e.tensor_tensor(dst, PS[:, gb, :], ye[:, y], ALU.mult), mg, a, tf)
                gbr.free(gb, mu)
                yer.free(y, mu)
                if e_ == 0:
                    ST["a"] = mu
                else:
                    ST["a"] = pool(lambda e: e.tensor_tensor(acc[:, s], acc[:, s], dst, ALU.add), mu, ST["a"])
                    tyr.free(yy, ST["a"])

            def moe_out(b):
                s, a = ST["acc"][0], ST["a"]
                bk, bf = mr.take()
                for t in range(4):
                    o = PS[:, bk, t * P:(t + 1) * P]
                    pe(lambda e, t=t, o=o: e.matmul(o, acc[:, s, t * P:(t + 1) * P], W["owT"], start=True, stop=False), a, bf)
                    m = pe(lambda e, t=t, o=o: e.matmul(o, X1[:, b, t * P:(t + 1) * P], ident, start=False, stop=True))
                accr.free(s, m)
                v = PS[:, bk, :].rearrange("p (t n) -> p t n", t=4)
                h = HR[:, 4 * b:4 * b + 4, :]
                a = dve(lambda e: e.tensor_tensor(h, v, W["obB"].unsqueeze(1).to_broadcast([P, 4, P]), ALU.add), m)
                mr.free(bk, a)
                for t in range(4):
                    a2 = dve(lambda e, t=t: e.bn_stats(stats[:, 4 * b + t, :], HR[:, 4 * b + t, :]), a)
                ST["bn"] = a2

            for b in range(NB):
                for e_ in range(8):
                    expert(b, e_)
                    if b and e_ == 2:
                        pass
                moe_out(b)
            me, mo, ve, vo = (stats[:, :, i] for i in (1, 4, 2, 5))
            m_, d_, v_, sd_, rs_, nm_ = (lnw[:, i, :] for i in range(6))
            a = ST["bn"]
            o1 = dve(lambda e: e.tensor_tensor(m_, me, me, ALU.mult), a)
            o2 = dve(lambda e: e.tensor_tensor(d_, mo, mo, ALU.mult), a)
            o3 = dve(lambda e: e.tensor_tensor(v_, ve, vo, ALU.add), a)
            o2 = dve(lambda e: e.tensor_tensor(m_, m_, d_, ALU.add), o1, o2)
            o2 = dve(lambda e: e.tensor_scalar(m_, m_, 0.5, 1e-6, ALU.mult, ALU.add), o2)
            o2 = dve(lambda e: e.scalar_tensor_tensor(v_, v_, 1.0 / 128, m_, ALU.mult, ALU.add), o2, o3)
            o2 = act(lambda e: e.activation(sd_, v_, ACT.Sqrt), o2)
            rs_ok = dve(lambda e: e.reciprocal(rs_, sd_), o2)
            hb = Ring([0, 1])
            hrt = Ring([0, 1])
            for b in range(NB):
                for t in range(4):
                    i = 4 * b + t
                    a = dve(lambda e, i=i: e.scalar_tensor_tensor(HR[:, i, :], HR[:, i, :], rs_[:, i:i + 1], W["nwB"],
                                                                  ALU.mult, ALU.mult), rs_ok)
                bk, bf = hb.take()
                for t in range(4):
                    m = pe(lambda e, b=b, t=t, bk=bk: e.transpose(PS[:, bk, t * P:(t + 1) * P], HR[:, 4 * b + t, :], ident), a, bf)
                s, sf = hrt.take()
                c = act(lambda e, s=s, bk=bk: e.activation(hrT[:, s], PS[:, bk, :], ACT.Copy), m, sf)
                hb.free(bk, c)
                q = b % 4
                m = pe(lambda e, b=b, q=q, s=s: e.matmul(PS[32 * q:32 * q + 32, 2 + b // 4, :], W["fdT"], hrT[:, s],
                                                         start=True, stop=True), c)
                hrt.free(s, m)
                if q == 3:
                    fm[b // 4] = act(lambda e, b=b: e.activation(ff[:, b // 4], PS[:, 2 + b // 4, :], ACT.Gelu,
                                                                 bias=W["fdb"]), m)
            FU = W["fuBD"].rearrange("p (b n) -> p b n", b=4)
            yr = Ring([4, 5, 6, 7])
            tr = Ring([0, 1, 2, 3])
            s_o = dsem("s_o")
            outs = []
            for hf in range(2):
                for t in range(4):
                    bk, bf = yr.take()
                    m = pe(lambda e, t=t, hf=hf, bk=bk: e.matmul(PS[:, bk, :], ff[:, hf, t * P:(t + 1) * P], FU,
                                                                 start=True, stop=True), fm[hf], bf)
                    v = PS[:, bk, :].rearrange("p (b n) -> p b n", b=4)
                    s, sf = tr.take()
                    tmp = tmpo[:, s]
                    xv = X[:, 16 * hf + t:16 * hf + 16:4, :]
                    hv = HR[:, 16 * hf + t:16 * hf + 16:4, :]
                    a = dve(lambda e, v=v, tmp=tmp, hv=hv: e.tensor_tensor(tmp, v, hv, ALU.add), m, sf)
                    yr.free(bk, a)
                    a = pool(lambda e, tmp=tmp: e.tensor_tensor(tmp, tmp, W["fubB"].unsqueeze(1).to_broadcast([P, 4, P]),
                                                                ALU.add), a)
                    a = dve(lambda e, tmp=tmp, hf=hf: e.tensor_tensor(tmp, tmp, GB1[:, 4 * hf:4 * hf + 4, :], ALU.mult), a)
                    a = dve(lambda e, tmp=tmp, xv=xv: e.tensor_tensor(xv, xv, tmp, ALU.add), a)
                    tr.free(s, a)
                    outs.append(a)
                last = sp.dma(out_d[:, 16 * hf:16 * hf + 16, :], X[:, 16 * hf:16 * hf + 16, :], s_o, a)
            D.close()
            sp(lambda e: e.nop(), last)


        ffn1()

        for q in queues:
            q.count()
        block = ctx.enter_context(nc.Block())

        @block.sync
        def _(e):
            sp.emit(e)

        @block.gpsimd
        def _(e):
            pool.emit(e)

        @block.vector
        def _(e):
            dve.emit(e)

        @block.scalar
        def _(e):
            act.emit(e)

        @block.tensor
        def _(e):
            pe.emit(e)


def kernel(**inputs):
    import concourse.bacc as bacc
    from concourse.bass_utils import run_bass_kernel_spmd

    I = {k: np.asarray(v) for k, v in inputs.items()}
    col = lambda a: np.asarray(a).reshape(-1, 1)
    rows = lambda a: np.broadcast_to(np.asarray(a).reshape(1, -1), (P, np.asarray(a).size))
    z = lambda *s: np.zeros(s, np.float32)
    bd = z(P, 8, P)
    for b in range(8):
        bd[16 * b:16 * b + 16, b, :] = I["L1_attn_Wout"]
    fu = z(P, 4, P)
    for b in range(4):
        fu[32 * b:32 * b + 32, b, :] = I["L1_ffn_ff_up_w"].T
    bin_ = I["L1_attn_b_in"]
    b5 = np.stack([np.tile(v, 8) for v in (bin_[0:16], bin_[16:48:2], bin_[17:48:2], bin_[48:80:2], bin_[49:80:2])], 1)
    W1 = np.concatenate([I["L0_ffn_W1"], I["L0_ffn_Ws1"][None]], 0)
    b1 = np.concatenate([I["L0_ffn_b1"], I["L0_ffn_bs1"][None]], 0)
    W2 = np.concatenate([I["L0_ffn_W2"], I["L0_ffn_Ws2"][None]], 0)
    parts = {
        "c": np.concatenate([I["L0_c"].T, I["L1_c"].T], 1), "wmod0": I["L0_wmod"], "ident": np.eye(P, dtype=np.float32),
        "bq": col(I["L0_attn_bq"]), "bk": col(I["L0_attn_bk"]),
        "WqT": I["L0_attn_Wq"].T, "WkT": I["L0_attn_Wk"].T, "WvT": I["L0_attn_Wv"].T, "WoT": I["L0_attn_Wo"].T,
        "bvB": rows(I["L0_attn_bv"]), "boB": rows(I["L0_attn_bo"]),
        "W1T": W1.transpose(2, 0, 1).reshape(P, -1), "b1T": b1.reshape(9, 4, P).transpose(2, 0, 1).reshape(P, -1),
        "wr0": I["L0_ffn_w_router"].T, "desc": rows(np.arange(8, 0, -1).astype(np.float32)),
        "W2T": W2.reshape(9, P, 4, P).transpose(3, 0, 2, 1).reshape(P, -1),
        "wmod1": I["L1_wmod"], "convw": I["L1_attn_conv_w"][:, 0, :], "convb": col(I["L1_attn_conv_b"]),
        "Win": I["L1_attn_Win"], "bin5": b5, "Alog": col(np.tile(I["L1_attn_A_log"], 8)), "WoutBD": bd.reshape(P, -1),
        "boutB": rows(I["L1_attn_b_out"]), "dw": I["L1_ffn_dw_kernel"][:, 0, :], "dwb": col(I["L1_ffn_dw_bias"]),
        "pwT": I["L1_ffn_pw_w"].T, "pwb": col(I["L1_ffn_pw_b"]), "rw1T": I["L1_ffn_router_w"].T,
        "rb1B": rows(I["L1_ffn_router_b"]), "ewT": I["L1_ffn_expert_w"].transpose(2, 0, 1).reshape(P, -1),
        "ebT": I["L1_ffn_expert_b"].T, "owT": I["L1_ffn_out_w"].T, "obB": rows(I["L1_ffn_out_b"]),
        "nwB": rows(I["L1_ffn_norm_w"]), "fdT": I["L1_ffn_ff_down_w"].T, "fdb": col(np.tile(I["L1_ffn_ff_down_b"], 4)),
        "fuBD": fu.reshape(P, -1), "fubB": rows(I["L1_ffn_ff_up_b"]),
    }
    small = z(9, 9, P)
    for i, n in enumerate("qkvo"):
        small[0:8, i] = I[f"L0_attn_A{n}"]
        small[0:8, 4 + i] = I[f"L0_attn_B{n}"].T
    small[0:8, 8] = I["L0_ffn_b2"]
    small[8, 8] = I["L0_ffn_bs2"]
    arrays = {"x": np.ascontiguousarray(I["L0_attn_x"].reshape(NT, P, P).transpose(1, 0, 2))}
    for i, pack in enumerate((PACK0, PACK1, PACK2, PACK3)):
        arrays[f"p{i}"] = np.ascontiguousarray(np.concatenate([parts[n].reshape(P, w) for n, w in pack], 1))
    arrays["small"] = small.reshape(9, -1)
    nc = bacc.Bacc("TRN2", target_bir_lowering=False, num_devices=1)
    args = [nc.dram_tensor(f"in_{n}", a.shape, F32, kind="ExternalInput").ap() for n, a in arrays.items()]
    args.append(nc.dram_tensor("out_0", (P, NT, P), F32, kind="ExternalOutput").ap())
    adaln_kernel(nc, *args)
    r = run_bass_kernel_spmd(nc, [{f"in_{n}": a for n, a in arrays.items()}], core_ids=[0])
    y = np.asarray(r.results[0]["out_0"])
    return np.ascontiguousarray(y.transpose(1, 0, 2)).reshape(8, 512, P)
```

```python
from contextlib import ExitStack

import numpy as np

import concourse.bass as bass
from concourse import mybir

P = 128
NB = 8
NT = 32
F32 = mybir.dt.float32
F32R = mybir.dt.float32r
BF16 = mybir.dt.bfloat16
ALU = mybir.AluOpType
ACT = mybir.ActivationFunctionType
AX = mybir.AxisListType

PACK0 = [("c", 16), ("wmod0", 768), ("ident", 128), ("bq", 1), ("bk", 1), ("WqT", 128), ("WkT", 128),
         ("WvT", 128), ("WoT", 128), ("bvB", 128), ("boB", 128)]
PACK1 = [("b1T", 36), ("wr0", 8), ("desc", 8), ("b2p", 128)]
PACK3 = [("wmod1", 768), ("convw", 4), ("convb", 1), ("Win", 80), ("bin5", 5), ("Alog", 1), ("WoutBD", 1024),
         ("boutB", 128), ("dw", 3), ("dwb", 1), ("pwT", 128), ("pwb", 1), ("rw1T", 8), ("rb1B", 8),
         ("ewT", 1024), ("ebT", 8), ("owT", 128), ("obB", 128), ("nwB", 128), ("fdT", 32), ("fdb", 1),
         ("fuBD", 512), ("fubB", 128)]

QTERM = [0, 0, 1, 1, 0, 2]
KTERM = [0, 1, 0, 1, 2, 0]


def width(pack):
    return sum(w for _, w in pack)


class Note:

    def activation(self, *a, **k):
        return lambda e: e.activation(*a, **k)

    def bn_stats(self, *a, **k):
        return lambda e: e.bn_stats(*a, **k)

    def matmul(self, *a, **k):
        return lambda e: e.matmul(*a, **k)

    def memset(self, *a, **k):
        return lambda e: e.memset(*a, **k)

    def mul(self, *a, **k):
        return lambda e: e.mul(*a, **k)

    def nop(self, *a, **k):
        return lambda e: e.nop(*a, **k)

    def reciprocal(self, *a, **k):
        return lambda e: e.reciprocal(*a, **k)

    def scalar_tensor_tensor(self, *a, **k):
        return lambda e: e.scalar_tensor_tensor(*a, **k)

    def tensor_copy(self, *a, **k):
        return lambda e: e.tensor_copy(*a, **k)

    def tensor_reduce(self, *a, **k):
        return lambda e: e.tensor_reduce(*a, **k)

    def tensor_scalar(self, *a, **k):
        return lambda e: e.tensor_scalar(*a, **k)

    def tensor_tensor(self, *a, **k):
        return lambda e: e.tensor_tensor(*a, **k)

    def tensor_tensor_scan(self, *a, **k):
        return lambda e: e.tensor_tensor_scan(*a, **k)

    def transpose(self, *a, **k):
        return lambda e: e.transpose(*a, **k)


NOTE = Note()


class Op:

    def __init__(self, fn, waits, sem=None, val=None):
        self.fn, self.waits, self.sem, self.val = fn, waits, sem, val
        self.asked = False


class Queue:

    def __init__(self, sem):
        self.sem, self.ops, self.gate = sem, [], []

    def put(self, op):
        op.waits = flat(op.waits) + self.gate
        self.gate = []
        for w in op.waits:
            w.asked = True
        self.ops.append(op)
        return op

    def __call__(self, fn, *waits):
        return self.put(Op(fn(NOTE), waits, self.sem))

    def dma(self, out, in_, dsem, *waits):
        dsem[1] += 16
        return self.put(Op(lambda e: e.dma_start(out, in_), waits, dsem[0], dsem[1]))

    def count(self):
        n = 0
        for op in self.ops:
            if op.sem is self.sem and op.asked:
                n += 1
                op.val = n

    def emit(self, eng):
        seen = {}
        for op in self.ops:
            need = {}
            for w in op.waits:
                need[id(w.sem)] = max(need.get(id(w.sem), (0, None))[0], w.val), w.sem
            for k, (v, s) in need.items():
                if seen.get(k, 0) < v:
                    eng.wait_ge(s, v)
                    seen[k] = v
            ins = op.fn(eng)
            if op.sem is not self.sem:
                ins.then_inc(op.sem, 16)
            elif op.asked:
                ins.then_inc(self.sem, 1)


def flat(ws):
    out = []
    for w in ws:
        if isinstance(w, (list, tuple)):
            out += flat(w)
        elif w is not None:
            out.append(w)
    return out


class Ring:

    def __init__(self, slots):
        self.slots = [(s, None) for s in slots]

    def __bool__(self):
        return bool(self.slots)

    def take(self):
        return self.slots.pop(0)

    def free(self, s, op):
        self.slots.append((s, op))


class Tasks:

    def __init__(self):
        self.all = []

    def spawn(self, *gens):
        self.all += gens

    def tick(self, n=1):
        for _ in range(n):
            self.all = [g for g in self.all if next(g, self) is not self]

    def finish(self):
        while self.all:
            self.tick()


def adaln_kernel(nc, x_d, p0_d, p1_d, p3_d, w12_d, small_d, out_d):
    ctx = ExitStack()
    with ctx:
        def sem(name):
            return ctx.enter_context(nc.semaphore(name))

        def sb(name, shape, dt=F32, c=None):
            return (c or ctx).enter_context(nc.sbuf_tensor(name, shape, dt))

        pe, dve, act, pool, sp = (Queue(sem(n)) for n in ("s_pe", "s_dve", "s_act", "s_pool", "s_sp"))
        queues = [pe, dve, act, pool, sp]

        def dsem(name):
            return [sem(name), 0]

        def barrier():
            last = [q.ops[-1] for q in queues if q.ops]
            for q in queues:
                q.gate = q.gate + last
                for w in last:
                    w.asked = True

        PS = ctx.enter_context(nc.psum_tensor("PS", [P, 8, 512], F32))
        X = sb("X", [P, NT, P])
        p0 = sb("p0", [P, width(PACK0)])
        p1 = sb("p1", [P, width(PACK1)])
        small = sb("small", [8, 8 * P])
        stats = sb("stats", [P, NT, 6])
        lnw = sb("lnw", [P, 6, NT])
        half = sb("half", [P, 32])
        eb = sb("eb", [P, 32])
        cs = sb("cs", [P, 16])
        cst = sb("cst", [P, 3, 16])
        mf = sb("mf", [P, 2, 6, 8])
        mft = sb("mft", [P, 2, 2, 8])

        def views(t, pack):
            d, o = {}, 0
            for n, w in pack:
                d[n] = t[:, o:o + w]
                o += w
            return d

        W = views(p0, PACK0)
        W.update(views(p1, PACK1))
        ident = W["ident"]

        s_x = [dsem(f"s_x{i}") for i in range(8)]
        s_p0, s_p1, s_p3, s_small = (dsem(n) for n in ("s_p0", "s_p1", "s_p3", "s_small"))
        ld_x = [sp.dma(X[:, 0:4, :], x_d[:, 0:4, :], s_x[0])]
        ld_p0 = act.dma(p0[:], p0_d, s_p0)
        ld_small = sp.dma(small[:], small_d, s_small)
        ld_x += [sp.dma(X[:, 4 * i:4 * i + 4, :], x_d[:, 4 * i:4 * i + 4, :], s_x[i]) for i in range(1, 8)]
        ld_p1 = sp.dma(p1[:], p1_d, s_p1)
        half_ok = pool(lambda e: e.memset(half[:], -0.5))
        eb_ok = pool(lambda e: e.memset(eb[:], float(np.e)))

        def clip_gate(out, g, t0, t1, *w):
            a = dve(lambda e: e.tensor_scalar(t0, g, 0.0, 2.0, ALU.is_ge, ALU.mult), *w)
            b = dve(lambda e: e.scalar_tensor_tensor(t1, t0, 1.0, g, ALU.subtract, ALU.mult), a)
            b = dve(lambda e: e.tensor_scalar(t1, t1, 0.25, None, ALU.max), b)
            return dve(lambda e: e.scalar_tensor_tensor(out, t0, 1.0, t1, ALU.subtract, ALU.mult), a, b)

        def mod_rows(L, k, wmod, dst, t0, t1, banks, *w):
            mms = []
            for b in range(8):
                o = PS[:, banks[b // 4], 128 * (b % 4):128 * (b % 4) + 128]
                l = cs[:, 8 * L + b:8 * L + b + 1].to_broadcast([P, P])
                mms.append(pe(lambda e, o=o, l=l: e.matmul(o, l, wmod[:, k * P:(k + 1) * P], start=True, stop=True), *w))
            g = PS[:, banks[0]:banks[0] + 2, :].rearrange("p a n -> p (a n)")
            return clip_gate(dst[:].rearrange("p b n -> p (b n)"), g, t0, t1, mms[-1])

        def mod_cols(L, wmod, bank, *w):
            o = PS[:, bank, 0:48].rearrange("p (k b) -> p k b", k=6)
            for k in range(6):
                m = pe(lambda e, k=k: e.matmul(o[:, k, :], wmod[:, k * P:(k + 1) * P], cs[:, 8 * L:8 * L + 8],
                                               start=True, stop=True), *w)
            c = dve(lambda e: e.tensor_copy(mf[:, L], o), m)
            r = []
            for k in (1, 4):
                r.append(dve(lambda e, k=k: e.tensor_scalar(mf[:, L, k], mf[:, L, k], 1.0, None, ALU.add), c))
            for k in (2, 5):
                r.append(clip_gate(mf[:, L, k], mf[:, L, k], mft[:, 0, k // 3], mft[:, 1, k // 3], c))
            return r

        def ln_stats(b, src, eps, centred, *w):
            a = 4 * b
            for t in range(4):
                s = dve(lambda e, t=t: e.bn_stats(stats[:, a + t, :], src[:, a + t, :]), *w)
                if t == 1:
                    yield
            yield
            me, mo, ve, vo = (stats[:, a:a + 4, i] for i in (1, 4, 2, 5))
            m, d, v, _, rs, nm = (lnw[:, i, a:a + 4] for i in range(6))
            if centred:
                o1 = dve(lambda e: e.tensor_tensor(m, me, mo, ALU.add), s)
                o2 = dve(lambda e: e.tensor_tensor(d, me, mo, ALU.subtract), s)
                o3 = dve(lambda e: e.tensor_tensor(v, ve, vo, ALU.add), s)
                o4 = dve(lambda e: e.scalar_tensor_tensor(d, d, 0.25, d, ALU.mult, ALU.mult), o2)
            else:
                o1 = dve(lambda e: e.tensor_tensor(m, me, me, ALU.mult), s)
                o2 = dve(lambda e: e.tensor_tensor(d, mo, mo, ALU.mult), s)
                o3 = dve(lambda e: e.tensor_tensor(v, ve, vo, ALU.add), s)
                o4 = dve(lambda e: e.tensor_tensor(d, m, d, ALU.add), o1, o2)
                o4 = dve(lambda e: e.tensor_scalar(d, d, 0.5, None, ALU.mult), o4)
            yield
            o5 = dve(lambda e: e.scalar_tensor_tensor(v, v, 1.0 / 128, d, ALU.mult, ALU.add), o3, o4)
            o6 = dve(lambda e: e.tensor_scalar(v, v, eps, None, ALU.add), o5)
            yield
            o8 = pool(lambda e: e.tensor_tensor(rs, v, half[:, 0:4], ALU.pow), o6, half_ok)
            yield
            yield
            if centred:
                o8 = dve(lambda e: e.scalar_tensor_tensor(nm, m, -0.5, rs, ALU.mult, ALU.mult), o8, o1)
                yield
            return o8

        def ln_batch(b, Z, zr, banks, dsts, scale, shift, engs, *w):
            st = yield from ln_stats(b, X, 1e-5, True, *w)
            while not zr:
                yield
            z, zfree = zr.take()
            os = []
            for t in range(4):
                i = 4 * b + t
                os.append(engs[t](lambda e, i=i, t=t: e.tensor_scalar(
                    Z[:, z, t, :], X[:, i, :], lnw[:, 4, i:i + 1], lnw[:, 5, i:i + 1], ALU.mult, ALU.add), st, zfree))
                if t == 1:
                    yield
            yield
            while not banks:
                yield
            bk, bfree = banks.take()
            for t in range(4):
                m = pe(lambda e, t=t: e.transpose(PS[:, bk, t * P:(t + 1) * P], Z[:, z, t, :], ident), os[t], bfree)
            zr.free(z, m)
            yield
            hs = []
            for dst in dsts:
                hs.append(act(lambda e, dst=dst: e.activation(dst, PS[:, bk, :], ACT.Identity, bias=shift, scale=scale),
                              m, *w))
                yield
            banks.free(bk, hs[-1])
            return hs, os

        o = act(lambda e: e.activation(cst[:, 0], W["c"], ACT.Exp, scale=-1.0), ld_p0)
        o = dve(lambda e: e.tensor_scalar(cst[:, 1], cst[:, 0], 1.0, None, ALU.add), o)
        o = dve(lambda e: e.reciprocal(cst[:, 2], cst[:, 1]), o)
        cs_ok = dve(lambda e: e.tensor_tensor(cs[:], W["c"], cst[:, 2], ALU.mult), o, ld_p0)
        mc0 = mod_cols(0, W["wmod0"], 0, cs_ok, ld_p0)

        def attention():
            A = ExitStack()
            Q = sb("Q", [P, 3, 16, 512], BF16, A)
            K = sb("K", [P, 3, 8, 512], BF16, A)
            E = sb("E", [P, 2, 4, 2, 512], F32, A)
            V = sb("V", [P, 3, 4, 16, 9], F32, A)
            Wq, Wk, Wv, Wo = (sb(n, [P, P], F32, A) for n in ("Wq", "Wk", "Wv", "Wo"))
            bqs = sb("bqs", [P, 2], F32, A)
            GA = sb("GA", [P, 8, P], F32, A)
            GB = sb("GB", [P, 8, P], F32, A)
            Z = sb("Z", [P, 1, 4, P], F32, A)
            hT = sb("hT", [P, 1, 512], F32, A)
            qf = sb("qf", [P, 2, 512], F32, A)
            SPL = sb("SPL", [P, 2, 3, 512], BF16, A)
            mx = sb("mx", [P, 2, 4, 16], F32, A)
            nmf = sb("nmf", [8, 512], F32, A)
            nms = sb("nms", [8, 3, 512], BF16, A)
            ov = sb("ov", [P, 2, 512], F32, A)
            rec = sb("rec", [P, 4, 4], F32, A)
            otok = sb("otok", [P, 4, P], F32, A)
            oT = sb("oT", [P, 512], F32, A)
            dqk = nc.dram_tensor("dqk", [8, 2, 3, P, 512], BF16, kind="Internal").ap()
            dmx = nc.dram_tensor("dmx", [8, 2, 3, 8, 512], BF16, kind="Internal").ap()

            SC = float(1.0 / np.sqrt(np.float32(8.0)))
            t0 = E[:, 0].rearrange("p a b n -> p (a b n)")[:, 0:1024]
            t1 = E[:, 0].rearrange("p a b n -> p (a b n)")[:, 1024:2048]
            ga_ok = mod_rows(0, 2, W["wmod0"], GA, t0, t1, [2, 3], cs_ok, ld_p0)
            gb_ok = pool(lambda e: e.tensor_tensor(GB[:], GA[:], W["boB"].unsqueeze(1).to_broadcast([P, 8, P]), ALU.mult), ga_ok)
            weff = {}
            for i in range(4):
                m = pe(lambda e, i=i: e.matmul(PS[:, 1, i * P:(i + 1) * P], small[0:8, i * P:(i + 1) * P],
                                               small[0:8, (4 + i) * P:(5 + i) * P], start=True, stop=True), ld_small)
            for i, (n, dst) in enumerate((("q", Wq), ("k", Wk), ("v", Wv), ("o", Wo))):
                weff[n] = dve(lambda e, i=i, n=n, dst=dst: e.scalar_tensor_tensor(
                    dst[:], PS[:, 1, i * P:(i + 1) * P], 2.0, W[f"W{n}T"], ALU.mult, ALU.add), m, ld_p0)
            bqs_ok = [dve(lambda e: e.tensor_scalar(bqs[:, 0:1], W["bq"], SC, None, ALU.mult), ld_p0),
                      dve(lambda e: e.tensor_copy(bqs[:, 1:2], W["bk"]), ld_p0)]
            vz = [pool(lambda e, i=i: e.memset(V[:, i, :, :, 8:9], 1.0)) for i in range(3)]
            oz = dve(lambda e: e.memset(PS[:, 6, :], 0.0))
            qz = [(dve, pool, pool)[i](lambda e, i=i: e.memset(Q[:, i].bitcast(F32), 0.0)) for i in range(3)]
            kz = [dve(lambda e, i=i: e.memset(K[96:99, i], 1.0)) for i in range(3)]

            misc = Ring([7])
            zr = Ring([0])
            hr = Ring([0])
            fr = Ring([0, 1])
            sr = Ring([0, 1])
            mring = Ring([3, 4, 5])
            sring = Ring([0, 1, 2])
            ering = Ring([0, 1])
            ovr = Ring([0, 1])
            pvring = Ring([6])
            s_w = [dsem(f"s_w{i}") for i in range(2)]
            s_q = [dsem(f"s_q{i}") for i in range(3)]
            s_mw = [dsem(f"s_mw{i}") for i in range(2)]
            s_m = [dsem(f"s_m{i}") for i in range(2)]
            S = {}

            def split(src, dst, a, *w):
                h = act(lambda e: e.activation(dst[:, 0], src, ACT.Copy), a, *w)
                yield
                r = pool(lambda e: e.tensor_tensor(src, src, dst[:, 0], ALU.subtract), h)
                yield
                yield
                m = act(lambda e: e.activation(dst[:, 1], src, ACT.Copy), r)
                yield
                return pool(lambda e: e.tensor_tensor(dst[:, 2], src, dst[:, 1], ALU.subtract), m)

            def prep_qk(b, i, hop):
                while not (misc and fr and sr):
                    yield
                bk, bf = misc.take()
                f, ff = fr.take()
                s, sf = sr.take()
                w, wop = ((Wq, weff["q"]), (Wk, weff["k"]))[i]
                m = pe(lambda e: e.matmul(PS[:, bk, :], w[:], hT[:, 0], start=True, stop=True), hop, wop, bf)
                yield
                yield
                a = act(lambda e: e.activation(qf[:, f], PS[:, bk, :], ACT.Identity, bias=bqs[:, i:i + 1],
                                               scale=(SC, 1.0)[i]), m, bqs_ok, ff)
                misc.free(bk, a)
                d = yield from split(qf[:, f], SPL[:, s], a, sf)
                fr.free(f, d)
                wr = sp.dma(dqk[b, i].rearrange("t p n -> p t n"), SPL[:, s], s_w[i], d)
                sr.free(s, wr)
                u = b % 3
                while b >= 3 and (b - 3, "done") not in S:
                    yield
                prev = S.get((b - 3, "E"))
                for par in range(2):
                    for t in range(6):
                        src = dqk[b, i, (QTERM, KTERM)[i][t]].rearrange("(p two d) n -> two d p n", two=2, d=8)[par]
                        r = slice(par * 48 + t * 8, par * 48 + t * 8 + 8)
                        dst = Q[r, u, par:16:2, :] if i == 0 else K[r, u]
                        S[b, "qk"] = sp.dma(dst, src, s_q[u], wr, prev, qz[u] if i == 0 else None)
                S[b, "qkn"] = S.get((b, "qkn"), 0) + 1

            def prep(b):
                while not hr:
                    yield
                h, hf = hr.take()
                (hop,), zop = yield from ln_batch(b, Z, zr, misc, [hT[:, 0]], mf[:, 0, 1, b:b + 1], mf[:, 0, 0, b:b + 1],
                                                  [dve] * 4 if b == 0 else [pool] * 4, mc0, hf, ld_x[b])
                tasks.spawn(prep_qk(b, 0, hop))
                yield
                tasks.spawn(prep_qk(b, 1, hop))
                yield
                yield
                while not misc:
                    yield
                bk, bf = misc.take()
                for t in range(4):
                    m = pe(lambda e, t=t: e.matmul(PS[:, bk, t * P:(t + 1) * P], hT[:, 0, t * P:(t + 1) * P], Wv[:],
                                                   start=True, stop=True), hop, weff["v"], bf)
                yield
                yield
                hr.free(h, m)
                v = b % 3
                while b >= 3 and (b - 3, "done") not in S:
                    yield
                S[b, "v"] = dve(lambda e: e.tensor_tensor(
                    V[:, v, :, :, 0:8], PS[:, bk, :].rearrange("p (t h d) -> p t h d", t=4, h=16),
                    W["bvB"].rearrange("p (h d) -> p h d", h=16).unsqueeze(1).to_broadcast([P, 4, 16, 8]), ALU.add),
                    m, vz, S.get((b - 3, "pv")))
                misc.free(bk, S[b, "v"])
                xv = X[:, 4 * b:4 * b + 4, :]
                S[b, "xb"] = pool(lambda e: e.tensor_tensor(xv, xv, GB[:, b:b + 1, :].to_broadcast([P, 4, P]), ALU.add),
                                  zop, gb_ok)

            def max_unit(b, i):
                h, qt = i // 4, i % 4
                u = b % 3
                bk, bf = mring.take()
                m = pe(lambda e: e.matmul(PS[:, bk, :], Q[0:96, u, h, qt * P:(qt + 1) * P], K[0:96, u, h // 2, :],
                                          start=True, stop=True), S[b, "qk"], bf)
                r = dve(lambda e: e.tensor_reduce(mx[:, b % 2, qt, h:h + 1], PS[:, bk, :], AX.X, ALU.max), m,
                        S.get((b - 2, "mt")))
                mring.free(bk, r)
                if i % 32 == 31:
                    S[b, "mx", i // 32] = r

            def max_rows(b, half):
                while not (misc and nmr):
                    yield
                bk, bf = misc.take()
                _, nf = nmr.take()
                for t in range(4):
                    m = pe(lambda e, t=t: e.transpose(PS[0:8, bk, t * P:(t + 1) * P],
                                                      mx[:, b % 2, t, 8 * half:8 * half + 8], ident), S[b, "mx", half], bf)
                S[b, "mt"] = m
                yield
                a = act(lambda e: e.mul(nmf[:], PS[0:8, bk, :], -1.0), m, nf)
                misc.free(bk, a)
                d = yield from split(nmf[:], nms, a, nf)
                yield
                yield
                wr = act.dma(dmx[b, half].rearrange("t h n -> h t n"), nms[:], s_mw[half], d)
                nmr.free(0, wr)
                for _ in range(3):
                    yield
                S[b, "m", half] = act.dma(Q[96:99, b % 3, 8 * half:8 * half + 8, :], dmx[b, half], s_m[half], wr)

            def exp_unit(b, i):
                g, kp, j, c = i // 16, i // 8 % 2, i // 2 % 4, i % 2
                h, u, kt = 4 * g + j, b % 3, 2 * kp + c
                bk, bf = sring.take()
                m = pe(lambda e: e.matmul(PS[:, bk, :], K[0:99, u, h // 2, kt * P:(kt + 1) * P], Q[0:99, u, h, :],
                                          start=True, stop=True), S[b, "qk"], S[b, "m", h // 8], kz, bf)
                S[b, "E"] = m
                if i % 8 == 0:
                    S["e"] = ering.take()
                es, ef = S["e"]
                a = act(lambda e: e.activation(E[:, es, j, c], PS[:, bk, :], ACT.Exp), m, ef)
                sring.free(bk, a)
                return es, a

            def pv(b, g, kp, c, es, a):
                kt = 2 * kp + c
                if kt == 0:
                    S["pvb"] = pvring.take()
                bk, bf = S["pvb"]
                for j in range(4):
                    m = pe(lambda e, j=j: e.matmul(PS[32 * j:32 * j + 9, bk, :], V[:, b % 3, kt, 4 * g + j, :],
                                                   E[:, es, j, c, :], start=(kt == 0), stop=(kt == 3)),
                           a, S[b, "v"], bf, oz)
                S[b, "pv"] = m
                if c == 1:
                    ering.free(es, m)
                if kt == 3:
                    o, of = ovr.take()
                    cp = act(lambda e: e.activation(ov[:, o], PS[:, bk, :], ACT.Copy), m, of)
                    pvring.free(bk, cp)
                    S["ov"] = o, cp
                    tasks.spawn(heads_out(b, g))

            def heads_out(b, g):
                o, cp = S["ov"]
                yield
                while not misc:
                    yield
                bk, bf = misc.take()
                for t in range(4):
                    m = pe(lambda e, t=t: e.transpose(PS[:, bk, t * P:(t + 1) * P], ov[:, o, t * P:(t + 1) * P], ident), cp, bf)
                ovr.free(o, m)
                yield
                yield
                v = PS[:, bk, :].rearrange("p (t j r) -> p t j r", t=4, j=4)
                r = dve(lambda e: e.reciprocal(rec[:], v[:, :, :, 8]), m)
                yield
                S["o"] = dve(lambda e: e.tensor_tensor(
                    otok[:].rearrange("p t (g j d) -> p t g j d", g=4, j=4)[:, :, g], v[:, :, :, 0:8],
                    rec[:].unsqueeze(3).to_broadcast([P, 4, 4, 8]), ALU.mult), r, S.get("otr"))
                misc.free(bk, S["o"])
                if g < 3:
                    return
                S[b, "done"] = True
                yield
                while not misc:
                    yield
                bk, bf = misc.take()
                for t in range(4):
                    m = pe(lambda e, t=t: e.transpose(PS[:, bk, t * P:(t + 1) * P], otok[:, t, :], ident), S["o"], bf)
                S["otr"] = m
                yield
                S["oT"] = act(lambda e: e.activation(oT[:], PS[:, bk, :], ACT.Copy), m, S.get("om"))
                misc.free(bk, S["oT"])
                yield
                while not misc:
                    yield
                bk, bf = misc.take()
                for t in range(4):
                    m = pe(lambda e, t=t: e.matmul(PS[:, bk, t * P:(t + 1) * P], oT[:, t * P:(t + 1) * P], Wo[:],
                                                   start=True, stop=True), S["oT"], weff["o"], bf)
                S["om"] = m
                yield
                yield
                v = PS[:, bk, :].rearrange("p (t n) -> p t n", t=4)
                xv = X[:, 4 * b:4 * b + 4, :]
                a = dve(lambda e: e.tensor_tensor(v, v, GA[:, b:b + 1, :].to_broadcast([P, 4, P]), ALU.mult), m, ga_ok)
                yield
                S["x", b] = dve(lambda e: e.tensor_tensor(xv, v, xv, ALU.add), a, S[b, "xb"])
                misc.free(bk, S["x", b])

            LEAD = 56
            tasks = Tasks()
            nmr = Ring([0])
            mdone = [0]

            def max_next():
                n = mdone[0]
                if n >= 64 * NB:
                    return
                max_unit(n // 64, n % 64)
                mdone[0] += 1
                if n % 32 == 31:
                    tasks.spawn(max_rows(n // 64, n // 32 % 2))

            tasks.spawn(prep(0))
            while S.get((0, "qkn")) != 2:
                tasks.tick()
            tasks.spawn(prep(1))
            for i in range(LEAD):
                max_next()
                tasks.tick()
            pend = []
            for b in range(NB):
                for i in range(64):
                    if i == 4 and b + 2 < NB:
                        tasks.spawn(prep(b + 2))
                    es, a = exp_unit(b, i)
                    max_next()
                    tasks.tick()
                    if pend and i % 4 == 3:
                        pend.pop(0)()
                    if i % 8 == 7:
                        g, kp = i // 16, i // 8 % 2
                        for c in range(2):
                            pend.append(lambda b=b, g=g, kp=kp, c=c, es=es, a=a: pv(b, g, kp, c, es, a))
            for f in pend:
                f()
                tasks.tick(2)
            tasks.finish()
            barrier()
            A.close()
        attention()

        def first(src, m, s, t, oh, bc, desc, *w):
            a = dve(lambda e: e.tensor_reduce(m, src, AX.X, ALU.max), *w)
            a = dve(lambda e: e.tensor_tensor(t, src, bc(m), ALU.is_equal), a)
            yield
            a = dve(lambda e: e.tensor_tensor(t, t, desc, ALU.mult), a, ld_p1)
            a = dve(lambda e: e.tensor_reduce(s, t, AX.X, ALU.max), a)
            return dve(lambda e: e.tensor_tensor(oh, t, bc(s), ALU.is_equal), a)

        def top2(M, wk, *w):
            oh1, oh2, t, w2 = (wk[:, i] for i in range(4))
            m1, m2, s = (wk[:, 4, :, i] for i in range(3))
            bc = lambda a: a.unsqueeze(2).to_broadcast([P, 4, 8])
            desc = W["desc"].unsqueeze(1).to_broadcast([P, 4, 8])
            a = yield from first(M, m1, s, t, oh1, bc, desc, *w)
            yield
            a = dve(lambda e: e.tensor_scalar(w2, oh1, -3.0e38, None, ALU.mult), a)
            a = dve(lambda e: e.tensor_tensor(w2, w2, M, ALU.add), a)
            yield
            a = yield from first(w2, m2, s, t, oh2, bc, desc, a)
            yield
            return a, m1, m2, oh1, oh2, bc

        def halves(src, hi, lo, eng_hi, eng_lo, *w):
            a = (act(lambda e: e.activation(hi, src, ACT.Copy), *w) if eng_hi is act
                 else eng_hi(lambda e: e.tensor_copy(hi, src), *w))
            b = eng_lo(lambda e: e.tensor_tensor(lo, src, hi.bitcast(F32), ALU.subtract), a)
            return a, b

        def product(o, ws, xs, start, stop, *w):
            (wh, wl), (xh, xl) = ws, xs
            pe(lambda e: e.matmul(o, wh, xh, start=start, stop=False), *w)
            pe(lambda e: e.matmul(o, wl, xh, start=False, stop=False))
            return pe(lambda e: e.matmul(o, wh, xl, start=False, stop=stop))

        def ffn0():
            B = ExitStack()
            stage = sb("stage", [P, 2, 2, 512], F32, B)
            Wh = sb("Wh", [P, 9, 2, 512], F32R, B)
            Wl = sb("Wl", [P, 9, 2, 512], F32R, B)
            Hf = sb("Hf", [P, 2, 512], F32, B)
            Hh = sb("Hh", [P, 2, 512], F32R, B)
            Hl = sb("Hl", [P, 2, 512], F32R, B)
            Z = sb("Zb", [P, 1, 4, P], F32, B)
            Gf = sb("Gf", [P, 3, 512], F32, B)
            Gh = sb("Gh", [P, 8, 512], F32R, B)
            Gl = sb("Gl", [P, 8, 512], F32R, B)
            gbs = sb("gbs", [P, 4, 512], F32, B)
            ty = sb("ty", [P, 2, 512], F32, B)
            acc = sb("acc", [P, 2, 512], F32, B)
            gt = sb("gt", [P, 2, 4, 9], F32, B)
            lg = sb("lg", [P, 4, 8], F32, B)
            wk = sb("wk", [P, 5, 4, 8], F32, B)
            gT = sb("gT", [P, 2, 512], F32, B)
            gsc = sb("gsc", [P, 8], F32, B)
            dg = nc.dram_tensor("dg", [8, 8, 512], F32, kind="Internal").ap()

            SCALE = float(1.0 / np.sqrt(1.25))
            gsc_ok = dve(lambda e: e.tensor_scalar(gsc[:], mf[:, 0, 5, :], SCALE, None, ALU.mult), mc0)
            gz = pool(lambda e: e.memset(gT[:], 0.0))
            g1s = [pool(lambda e, i=i: e.memset(gt[:, i, :, 8:9], 1.0)) for i in range(2)]
            s_w12 = [dsem(f"s_w12{i}") for i in range(2)]
            s_gw = [dsem(f"s_gw{i}") for i in range(2)]
            s_g = [dsem(f"s_g{i}") for i in range(4)]
            zr, hr, stg, misc = Ring([0]), Ring([0, 1]), Ring([0, 1]), Ring([5, 6, 7])
            upr, dnr = Ring([0, 1, 2]), Ring([3, 4])
            gfr, gr, gsr, tyr, accr, gTr, gtr = (Ring(range(n)) for n in (3, 8, 4, 2, 2, 2, 2))
            b1T = W["b1T"].rearrange("p (e f) -> p e f", e=9)
            order = (8, 0, 1, 2, 3, 4, 5, 6, 7)
            work = [(b, e_) for b in range(NB) for e_ in order]
            wok, hok, gok, ST, wld = {}, {}, {}, {}, {}

            def load_w(e_):
                s, f = stg.take()
                wld[e_] = s, sp.dma(stage[:, s], w12_d[:, e_], s_w12[s], f)

            def split_w(e_):
                s, ld = wld[e_]
                v = lambda t: t.rearrange("p a n -> p (a n)")
                wok[e_] = halves(v(stage[:, s]), v(Wh[:, e_]), v(Wl[:, e_]), dve, dve, ld)
                stg.free(s, wok[e_][1])

            def prep(b):
                while not hr:
                    yield
                h, hf = hr.take()
                (a1, a2), _ = yield from ln_batch(b, Z, zr, misc, [Hf[:, h], Hh[:, h]], mf[:, 0, 4, b:b + 1],
                                                  mf[:, 0, 3, b:b + 1], [dve] * 4, hf)
                lo = dve(lambda e: e.tensor_tensor(Hl[:, h], Hf[:, h], Hh[:, h].bitcast(F32), ALU.subtract), a2)
                hok[b] = h, a2, lo
                while not misc:
                    yield
                bk, bf = misc.take()
                L = PS[:, bk, 0:32].rearrange("p (t e) -> p t e", t=4)
                for t in range(4):
                    m = pe(lambda e, t=t: e.matmul(L[:, t, :], Hf[:, h, t * P:(t + 1) * P], W["wr0"],
                                                   start=True, stop=True), a2, bf, ld_p1)
                yield
                bc = lambda a: a.unsqueeze(2).to_broadcast([P, 4, 8])
                mx, sm = wk[:, 4, :, 4], wk[:, 4, :, 5]
                a = dve(lambda e: e.tensor_reduce(mx, L, AX.X, ALU.max), m)
                a = dve(lambda e: e.tensor_tensor(lg[:], L, bc(mx), ALU.subtract), a)
                misc.free(bk, a)
                yield
                f = lg[:].rearrange("p t e -> p (t e)")
                a = pool(lambda e: e.tensor_tensor(f, eb[:], f, ALU.pow), a, eb_ok)
                for _ in range(5):
                    yield
                a = dve(lambda e: e.tensor_reduce(sm, lg[:], AX.X, ALU.add), a)
                a = dve(lambda e: e.reciprocal(mx, sm), a)
                yield
                a = dve(lambda e: e.tensor_tensor(lg[:], lg[:], bc(mx), ALU.mult), a)
                a, _, _, oh1, oh2, _ = yield from top2(lg[:], wk, a)
                a = dve(lambda e: e.tensor_tensor(oh1, oh1, oh2, ALU.add), a)
                yield
                g, gf = gtr.take()
                ok = dve(lambda e: e.tensor_tensor(gt[:, g, :, 0:8], oh1, lg[:], ALU.mult), a, gf)
                yield
                while not (misc and gTr):
                    yield
                bk, bf = misc.take()
                for t in range(4):
                    m = pe(lambda e, t=t: e.transpose(PS[0:9, bk, t * P:(t + 1) * P], gt[:, g, t, :], ident), ok, bf, g1s)
                gtr.free(g, m)
                yield
                s, sf = gTr.take()
                c = act(lambda e: e.activation(gT[0:9, s], PS[0:9, bk, :], ACT.Copy), m, sf, gz)
                misc.free(bk, c)
                gok[b] = s, c, sp.dma(dg[b], gT[0:8, s], s_gw[b % 2], c)

            def load_g(b, e_):
                s, f = gsr.take()
                ST["gb", b, e_] = s, sp.dma(gbs[:, s], dg[b, e_:e_ + 1, :].to_broadcast([P, 512]), s_g[s], f, gok[b][2])

            def up(b, e_, fc):
                h, hi, lo = hok[b]
                bk, bf = upr.take()
                m = product(PS[:, bk, :], [w[:, e_, 0, fc * P:(fc + 1) * P] for w in (Wh, Wl)], (Hh[:, h], Hl[:, h]),
                            True, True, hi, lo, wok[e_], bf)
                if e_ == 7 and fc == 3:
                    hr.free(h, m)
                f, ff = gfr.take()
                a = act(lambda e: e.activation(Gf[:, f], PS[:, bk, :], ACT.Gelu_apprx_tanh,
                                               bias=b1T[:, e_, fc:fc + 1]), m, ff)
                upr.free(bk, a)
                g, gf = gr.take()
                ok = halves(Gf[:, f], Gh[:, g], Gl[:, g], act if fc % 2 else dve, pool if fc == 3 else dve, a, gf)
                gfr.free(f, ok[1])
                ST["g", b, e_, fc] = g, ok

            def down(b, e_, fc):
                if fc == 0:
                    ST["d"] = dnr.take()
                bk, bf = ST["d"]
                g, ok = ST["g", b, e_, fc]
                m = product(PS[:, bk, :], [w[:, e_, 1, fc * P:(fc + 1) * P] for w in (Wh, Wl)], (Gh[:, g], Gl[:, g]),
                            fc == 0, fc == 3 and e_ != 8, ok, bf)
                gr.free(g, m)
                if fc < 3:
                    return
                if e_ == 8:
                    while b not in gok:
                        tasks.tick()
                    q, c, wr = gok[b]
                    m = pe(lambda e: e.matmul(PS[:, bk, :], W["b2p"], gT[:, q], start=False, stop=True), c, ld_p1)
                    gTr.free(q, [m, wr])
                    s, sf = accr.take()
                    ST["acc"] = s
                    a = act(lambda e: e.activation(acc[:, s], PS[:, bk, :], ACT.Copy), m, sf)
                    dnr.free(bk, a)
                else:
                    s = ST["acc"]
                    if ("gb", b, e_) not in ST:
                        load_g(b, e_)
                    q, ld = ST["gb", b, e_]
                    y, yf = tyr.take()
                    mu = dve(lambda e: e.tensor_tensor(ty[:, y], PS[:, bk, :], gbs[:, q], ALU.mult), m, ld, yf)
                    gsr.free(q, mu)
                    dnr.free(bk, mu)
                    a = pool(lambda e: e.tensor_tensor(acc[:, s], acc[:, s], ty[:, y], ALU.add), mu, ST["a"])
                    tyr.free(y, a)
                ST["a"] = a

            def finish(b):
                s, a = ST["acc"], ST["a"]
                yield
                yield
                o = dve(lambda e: e.tensor_scalar(acc[:, s], acc[:, s], gsc[:, b:b + 1], None, ALU.mult), a, gsc_ok)
                yield
                while not misc:
                    yield
                bk, bf = misc.take()
                for t in range(4):
                    m = pe(lambda e, t=t: e.transpose(PS[:, bk, t * P:(t + 1) * P], acc[:, s, t * P:(t + 1) * P], ident), o, bf)
                accr.free(s, m)
                yield
                yield
                xv = X[:, 4 * b:4 * b + 4, :]
                v = PS[:, bk, :].rearrange("p (t n) -> p t n", t=4)
                x = dve(lambda e: e.tensor_tensor(xv, v, xv, ALU.add), m)
                misc.free(bk, x)

            tasks = Tasks()
            for e_ in (8, 0):
                load_w(e_)
            tasks.spawn(prep(0))
            while 0 not in hok:
                tasks.tick()
            split_w(8)
            for n in range(len(work) + 1):
                if n < 8:
                    split_w(order[n + 1])
                if n < 7:
                    load_w(order[n + 2])
                for fc in range(4):
                    for d in range(n, n + 3):
                        if d < len(work) and work[d][1] != 8 and ("gb",) + work[d] not in ST and work[d][0] in gok and gsr:
                            load_g(*work[d])
                    if n < len(work):
                        up(*work[n], fc)
                    if n > 0:
                        down(*work[n - 1], fc)
                    tasks.tick()
                if n % 9 == 0 and n // 9 + 1 < NB:
                    tasks.spawn(prep(n // 9 + 1))
                if n > 0 and work[n - 1][1] == 7:
                    tasks.spawn(finish(work[n - 1][0]))
            tasks.finish()
            barrier()
            B.close()

        ffn0()

        def ssm():
            C = ExitStack()
            p3 = sb("p3", [P, width(PACK3)])
            W.update(views(p3, PACK3))
            ld_p3 = sp.dma(p3[:], p3_d, s_p3)
            GA1 = sb("GA1", [P, 8, P])
            GB1 = sb("GB1", [P, 8, P])
            Z = sb("Zc", [P, 2, 4, P])
            Hc = sb("Hc", [P, 3, 516], F32, C)
            XC = sb("XC", [P, 2, 512], F32, C)
            WP = sb("WP", [P, 3, 240], F32, C)
            WPh = sb("WPh", [P, 3, 240], F32R, C)
            WPl = sb("WPl", [P, 3, 240], F32R, C)
            XCh = sb("XCh", [P, 2, 512], F32R, C)
            XCl = sb("XCl", [P, 2, 512], F32R, C)
            tb = sb("tb", [P, 12, 512], F32, C)
            cv = sb("cv", [P, 12], F32, C)
            tA, tB = tb[:, 0:2].rearrange("p a n -> p (a n)"), tb[:, 2:4].rearrange("p a n -> p (a n)")
            mc1 = mod_cols(1, W["wmod1"], 0, ld_p3)
            g1 = mod_rows(1, 2, W["wmod1"], GA1, tA, tB, [1, 2], ld_p3)
            g2 = mod_rows(1, 5, W["wmod1"], GB1, tA, tB, [3, 4], ld_p3, g1)

            z0 = pool(lambda e: e.memset(WP[:], 0.0))
            Win = W["Win"]
            pr = lambda o: Win[:, o:o + 32].rearrange("p (n k) -> p n k", k=2)
            a = dve(lambda e: e.tensor_copy(WP[:, 0, 112:128], Win[:, 0:16]), z0, ld_p3)
            wp_ok = [a]
            for i, o in ((1, 16), (2, 48)):
                a = dve(lambda e, i=i, o=o: e.tensor_tensor(WP[:, i, 112:128], pr(o)[:, :, 0], pr(o)[:, :, 1], ALU.add), z0)
                wp_ok.append(dve(lambda e, i=i: e.tensor_scalar(WP[:, i, 112:128], WP[:, i, 112:128], 0.5, None, ALU.mult), a))
            b5 = W["bin5"]
            c_ok = []
            for i in range(2):
                a = dve(lambda e, i=i: e.tensor_tensor(cv[:, i:i + 1], b5[:, 1 + 2 * i:2 + 2 * i], b5[:, 2 + 2 * i:3 + 2 * i], ALU.add), ld_p3)
                c_ok.append(dve(lambda e, i=i: e.tensor_scalar(cv[:, i:i + 1], cv[:, i:i + 1], 0.5, None, ALU.mult), a))
            a = act(lambda e: e.activation(cv[:, 6:7], W["Alog"], ACT.Exp), ld_p3)
            a = dve(lambda e: e.tensor_scalar(cv[:, 2:3], cv[:, 6:7], -1.0, None, ALU.mult), a)
            a3 = dve(lambda e: e.tensor_scalar(cv[:, 3:4], cv[:, 6:7], 1e-4, None, ALU.is_lt), a)
            a = dve(lambda e: e.tensor_scalar(cv[:, 7:8], cv[:, 3:4], -1.0, 1.0, ALU.mult, ALU.add), a3)
            a = dve(lambda e: e.scalar_tensor_tensor(cv[:, 8:9], cv[:, 2:3], cv[:, 7:8], cv[:, 3:4], ALU.mult, ALU.add), a)
            a = dve(lambda e: e.reciprocal(cv[:, 9:10], cv[:, 8:9]), a)
            a4 = dve(lambda e: e.tensor_tensor(cv[:, 4:5], cv[:, 9:10], cv[:, 7:8], ALU.mult), a)
            a5 = dve(lambda e: e.tensor_tensor(cv[:, 5:6], cv[:, 2:3], cv[:, 3:4], ALU.mult), a3)

            zr, banks = Ring([0, 1]), Ring([5, 6, 7])
            p0z = pool(lambda e: e.memset(Hc[:, :, 0:1], 0.0))
            p1z = pool(lambda e: e.memset(Hc[:, :, 513:516], 0.0))
            p2z = pool(lambda e: e.memset(XC[:], 0.0))
            for i in range(3):
                wp_ok.append(halves(WP[:, i], WPh[:, i], WPl[:, i], dve, dve, wp_ok[i]))
            xr, xhr, hcr = Ring([0, 1]), Ring([0, 1]), Ring([0, 1, 2])
            cw = W["convw"]
            bank_free = [c for c in mc1] + [g1, g2]
            last = []
            turn = [0]

            def conv(b):
                while not hcr:
                    yield
                hb_, hbf = hcr.take()
                (h,), _ = yield from ln_batch(b, Z, zr, banks, [Hc[:, hb_, 1:513]], mf[:, 1, 1, b:b + 1],
                                              mf[:, 1, 0, b:b + 1], [dve, pool, dve, pool], mc1, hbf)
                while not (xr and xhr and turn[0] == b):
                    yield
                x, xf = xr.take()
                o = XC[:, x, 0:511]
                a = dve(lambda e: e.tensor_scalar(o, Hc[:, hb_, 0:511], cw[:, 0:1], W["convb"], ALU.mult, ALU.add),
                        h, p0z, p1z, p2z, xf)
                for k in range(1, 4):
                    yield
                    a = dve(lambda e, k=k: e.scalar_tensor_tensor(
                        o, Hc[:, hb_, k:k + 511], cw[:, k:k + 1], o, ALU.mult, ALU.add), a)
                hcr.free(hb_, a)
                yield
                y, yf = xhr.take()
                ok = halves(XC[:, x], XCh[:, y], XCl[:, y], act, dve, a, yf)
                xr.free(x, ok[1])
                yield
                for i in range(3):
                    c = slice(112 - 16 * b, 240 - 16 * b)
                    m = product(PS[:, i, :], (WPh[:, i, c], WPl[:, i, c]), (XCh[:, y], XCl[:, y]), b == 0, b == 7,
                                ok, wp_ok, bank_free)
                xhr.free(y, m)
                turn[0] += 1
                last[:] = [m]

            tasks = Tasks()
            for b in range(NB):
                tasks.spawn(conv(b))
                tasks.tick(5)
            tasks.finish()
            m = last[0]
            T = lambda i: tb[:, i, :]
            z_ = dve(lambda e: e.tensor_scalar(T(0), PS[:, 0, :], b5[:, 0:1], None, ALU.add), m)
            a = dve(lambda e: e.scalar_tensor_tensor(T(1), T(0), -1.0, T(0), ALU.mult, ALU.max), z_)
            a = act(lambda e: e.activation(T(2), T(1), ACT.Exp, scale=-1.0), a)
            a = act(lambda e: e.activation(T(3), T(2), ACT.Ln, bias=1.0), a)
            spl = dve(lambda e: e.scalar_tensor_tensor(T(4), T(0), 0.0, T(3), ALU.max, ALU.add), a)
            ab = act(lambda e: e.activation(T(5), T(4), ACT.Exp, scale=cv[:, 2:3]), spl, a5)
            u = dve(lambda e: e.tensor_scalar(T(1), T(5), -1.0, cv[:, 4:5], ALU.add, ALU.mult), ab, a4)
            d = dve(lambda e: e.tensor_scalar(T(6), T(4), cv[:, 5:6], None, ALU.mult), spl)
            q = dve(lambda e: e.tensor_scalar(T(7), T(6), 1.0 / 6.0, 0.5, ALU.mult, ALU.add), d)
            q = dve(lambda e: e.tensor_tensor(T(7), T(7), T(6), ALU.mult), q)
            q = dve(lambda e: e.tensor_scalar(T(7), T(7), 1.0, cv[:, 3:4], ALU.add, ALU.mult), q)
            q = dve(lambda e: e.tensor_tensor(T(1), T(1), T(7), ALU.add), q, u)
            q = dve(lambda e: e.scalar_tensor_tensor(T(8), PS[:, 1, :], cv[:, 0:1], T(1), ALU.add, ALU.mult), q, c_ok)
            q = dve(lambda e: e.tensor_tensor_scan(T(9), T(5), T(8), 0.0, ALU.mult, ALU.add), q)
            q = dve(lambda e: e.scalar_tensor_tensor(T(10), PS[:, 2, :], cv[:, 1:2], T(9), ALU.add, ALU.mult), q)
            WO = W["WoutBD"].rearrange("p (b n) -> p b n", b=8)
            yr = Ring([3, 4, 5, 6])
            tr = Ring([0, 2, 4, 6])
            for t in range(4):
                for hf in range(2):
                    bk, bf = yr.take()
                    m = pe(lambda e, t=t, hf=hf, bk=bk: e.matmul(PS[:, bk, :], tb[:, 10, t * P:(t + 1) * P],
                                                                 WO[:, 4 * hf:4 * hf + 4, :], start=True, stop=True), q, bf)
                    xv = X[:, 16 * hf + t:16 * hf + 16:4, :] if 16 * hf + 16 <= NT else None
                    v = PS[:, bk, :].rearrange("p (b n) -> p b n", b=4)
                    s, sf = tr.take()
                    tmp = tb[:, s, :].rearrange("p (b n) -> p b n", b=4)
                    a = dve(lambda e, v=v, tmp=tmp: e.tensor_tensor(
                        tmp, v, W["boutB"].unsqueeze(1).to_broadcast([P, 4, P]), ALU.add), m, sf, q)
                    yr.free(bk, a)
                    a = dve(lambda e, tmp=tmp, hf=hf: e.tensor_tensor(tmp, tmp, GA1[:, 4 * hf:4 * hf + 4, :], ALU.mult), a)
                    a = pool(lambda e, tmp=tmp, xv=xv: e.tensor_tensor(xv, xv, tmp, ALU.add), a)
                    tr.free(s, a)
            barrier()
            C.close()

            return GA1, GB1, Z, ld_p3

        GA1, GB1, Z, ld_p3 = ssm()

        def ffn1():
            D = ExitStack()
            Hd = sb("Hd", [P, 2, 514], F32, D)
            XD = sb("XD", [P, 1, 512], F32, D)
            XDh = sb("XDh", [P, 2, 512], F32R, D)
            XDl = sb("XDl", [P, 2, 512], F32R, D)
            X1 = sb("X1", [P, 3, 512], F32, D)
            X1h = sb("X1h", [P, 3, 512], F32R, D)
            X1l = sb("X1l", [P, 3, 512], F32R, D)
            pwh = sb("pwh", [P, P], F32R, D)
            pwl = sb("pwl", [P, P], F32R, D)
            EWh = sb("EWh", [P, 8, P], F32R, D)
            EWl = sb("EWl", [P, 8, P], F32R, D)
            sx = sb("sx", [P, 2, 512], F32, D)
            gt = sb("gt1", [P, 2, 4, 8], F32, D)
            lg = sb("lg1", [P, 4, 8], F32, D)
            wk = sb("wk1", [P, 5, 4, 8], F32, D)
            gT = sb("gT1", [8, 2, 512], F32, D)
            ye = sb("ye", [P, 2, 512], F32, D)
            gbs = sb("gbs1", [P, 6, 512], F32, D)
            ty = sb("ty1", [P, 2, 512], F32, D)
            acc = sb("acc1", [P, 2, 512], F32, D)
            HR = sb("HR", [P, NT, P], F32, D)
            hrT = sb("hrT", [P, 2, 512], F32, D)
            ff = sb("ff", [P, 2, 512], F32, D)
            tmpo = sb("tmpo", [P, 4, 4, P], F32, D)
            dg = nc.dram_tensor("dg1", [8, 8, 512], F32, kind="Internal").ap()
            s_gw = [dsem(f"s_gx{i}") for i in range(2)]
            s_g = [dsem(f"s_gy{i}") for i in range(6)]
            zr, hdr, xdr, xhr, x1r, sxr = (Ring(range(n)) for n in (2, 2, 1, 2, 3, 2))
            yer, gsr, tyr, accr, hrr, gTr, gtr = (Ring(range(n)) for n in (2, 6, 2, 2, 2, 2, 2))
            misc, yr = Ring([4, 5, 6, 7]), Ring([0, 1])
            dw = W["dw"]
            EW = W["ewT"].rearrange("p (e n) -> p e n", e=8)
            pz = pool(lambda e: e.memset(Hd[:, :, 0:2], 0.0))
            pw_ok = halves(W["pwT"], pwh[:], pwl[:], dve, dve, ld_p3)
            ew_ok = halves(W["ewT"], EWh[:].rearrange("p e n -> p (e n)"), EWl[:].rearrange("p e n -> p (e n)"), act, pool)
            ST = {}

            def prep(b):
                while not hdr:
                    yield
                h, hf = hdr.take()
                (a0,), _ = yield from ln_batch(b, Z, zr, misc, [Hd[:, h, 2:514]], mf[:, 1, 4, b:b + 1],
                                               mf[:, 1, 3, b:b + 1], [pool, dve, pool, pool], hf)
                while not (xdr and xhr):
                    yield
                x, xf = xdr.take()
                o = XD[:, x, :]
                c = dve(lambda e: e.tensor_scalar(o, Hd[:, h, 0:512], dw[:, 0:1], W["dwb"], ALU.mult, ALU.add), a0, pz, xf)
                for k in range(1, 3):
                    yield
                    c = dve(lambda e, k=k: e.scalar_tensor_tensor(o, Hd[:, h, k:k + 512], dw[:, k:k + 1], o,
                                                                  ALU.mult, ALU.add), c)
                yield
                y, yf = xhr.take()
                ok = halves(XD[:, x], XDh[:, y], XDl[:, y], act, dve, c, yf)
                xdr.free(x, ok[1])
                yield
                yield
                while not misc:
                    yield
                bk, bf = misc.take()
                m = product(PS[:, bk, :], (pwh[:], pwl[:]), (XDh[:, y], XDl[:, y]), True, True, ok, pw_ok, bf)
                xhr.free(y, m)
                yield
                s, sf = sxr.take()
                a = act(lambda e: e.activation(sx[:, s], PS[:, bk, :], ACT.Silu, bias=W["pwb"]), m, sf)
                misc.free(bk, a)
                yield
                while not x1r:
                    yield
                x, xf = x1r.take()
                a = pool(lambda e: e.tensor_tensor(X1[:, x], sx[:, s], Hd[:, h, 2:514], ALU.add), a, a0, xf)
                sxr.free(s, a)
                hdr.free(h, a)
                yield
                yield
                ST["x", b] = x, a, halves(X1[:, x], X1h[:, x], X1l[:, x], act, dve, a)
                while not misc:
                    yield
                bk, bf = misc.take()
                L = PS[:, bk, 0:32].rearrange("p (t e) -> p t e", t=4)
                for t in range(4):
                    m = pe(lambda e, t=t: e.matmul(L[:, t, :], X1[:, x, t * P:(t + 1) * P], W["rw1T"],
                                                   start=True, stop=True), a, bf)
                yield
                yield
                a = dve(lambda e: e.tensor_tensor(lg[:], L, W["rb1B"].unsqueeze(1).to_broadcast([P, 4, 8]), ALU.add), m)
                misc.free(bk, a)
                a, m1, m2, oh1, oh2, bc = yield from top2(lg[:], wk, a)
                d, w1, w2 = (wk[:, 4, :, i] for i in (5, 6, 7))
                a = dve(lambda e: e.tensor_tensor(d, m1, m2, ALU.subtract), a)
                yield
                a = act(lambda e: e.activation(d, d, ACT.Tanh, scale=0.5), a)
                yield
                c = dve(lambda e: e.tensor_scalar(w1, d, 0.5, 0.5, ALU.mult, ALU.add), a)
                a = dve(lambda e: e.tensor_scalar(w2, d, -0.5, 0.5, ALU.mult, ALU.add), a)
                a = dve(lambda e: e.tensor_tensor(oh1, oh1, bc(w1), ALU.mult), c)
                a = dve(lambda e: e.tensor_tensor(oh2, oh2, bc(w2), ALU.mult), a)
                yield
                g, gf = gtr.take()
                ok = dve(lambda e: e.tensor_tensor(gt[:, g], oh1, oh2, ALU.add), a, gf)
                yield
                while not (misc and gTr):
                    yield
                bk, bf = misc.take()
                for t in range(4):
                    m = pe(lambda e, t=t: e.transpose(PS[0:8, bk, t * P:(t + 1) * P], gt[:, g, t, :], ident), ok, bf)
                gtr.free(g, m)
                yield
                s, sf = gTr.take()
                c = act(lambda e: e.activation(gT[:, s], PS[0:8, bk, :], ACT.Copy), m, sf)
                misc.free(bk, c)
                wr = sp.dma(dg[b], gT[:, s], s_gw[b % 2], c)
                gTr.free(s, wr)
                ST["gw", b] = wr

            def load_g(b, e_):
                s, f = gsr.take()
                ST["gb", b, e_] = s, sp.dma(gbs[:, s], dg[b, e_:e_ + 1, :].to_broadcast([P, 512]), s_g[s], f, ST["gw", b])

            def expert(b, e_):
                x, _, ok = ST["x", b]
                bk, bf = yr.take()
                m = product(PS[:, bk, :], (EWh[:, e_, :], EWl[:, e_, :]), (X1h[:, x], X1l[:, x]), True, True, ok, ew_ok, bf)
                y, yf = yer.take()
                a = act(lambda e: e.activation(ye[:, y], PS[:, bk, :], ACT.Silu, bias=W["ebT"][:, e_:e_ + 1]), m, yf)
                yr.free(bk, a)
                q, ld = ST["gb", b, e_]
                if e_ == 0:
                    ST["acc"] = accr.take()
                s, sf = ST["acc"]
                t, tf = (None, sf) if e_ == 0 else tyr.take()
                dst = acc[:, s] if e_ == 0 else ty[:, t]
                mu = dve(lambda e: e.tensor_tensor(dst, ye[:, y], gbs[:, q], ALU.mult), ld, a, tf)
                gsr.free(q, mu)
                yer.free(y, mu)
                if e_:
                    mu = pool(lambda e: e.tensor_tensor(acc[:, s], acc[:, s], dst, ALU.add), mu, ST["a"])
                    tyr.free(t, mu)
                ST["a"] = mu
                if e_ == 7:
                    ST["acc", b] = s, mu

            def post(b):
                yield
                yield
                s, a = ST["acc", b]
                x = ST["x", b][0]
                while not misc:
                    yield
                bk, bf = misc.take()
                for t in range(4):
                    o = PS[:, bk, t * P:(t + 1) * P]
                    pe(lambda e, t=t, o=o: e.matmul(o, acc[:, s, t * P:(t + 1) * P], W["owT"], start=True, stop=False), a, bf)
                    m = pe(lambda e, t=t, o=o: e.matmul(o, X1[:, x, t * P:(t + 1) * P], ident, start=False, stop=True))
                accr.free(s, m)
                x1r.free(x, m)
                yield
                yield
                v = PS[:, bk, :].rearrange("p (t n) -> p t n", t=4)
                h = HR[:, 4 * b:4 * b + 4, :]
                a = dve(lambda e: e.tensor_tensor(h, v, W["obB"].unsqueeze(1).to_broadcast([P, 4, P]), ALU.add), m)
                misc.free(bk, a)
                rs = yield from ln_stats(b, HR, 1e-6, False, a)
                for t in range(4):
                    i = 4 * b + t
                    a = dve(lambda e, i=i: e.scalar_tensor_tensor(HR[:, i, :], HR[:, i, :], lnw[:, 4, i:i + 1], W["nwB"],
                                                                  ALU.mult, ALU.mult), rs)
                    yield
                while not (misc and hrr):
                    yield
                bk, bf = misc.take()
                for t in range(4):
                    m = pe(lambda e, t=t: e.transpose(PS[:, bk, t * P:(t + 1) * P], HR[:, 4 * b + t, :], ident), a, bf)
                yield
                s, sf = hrr.take()
                c = act(lambda e: e.activation(hrT[:, s], PS[:, bk, :], ACT.Copy), m, sf)
                misc.free(bk, c)
                yield
                q = b % 4
                m = pe(lambda e: e.matmul(PS[32 * q:32 * q + 32, 2 + b // 4, :], W["fdT"], hrT[:, s],
                                          start=True, stop=True), c)
                hrr.free(s, m)
                if q < 3:
                    return
                hf = b // 4
                yield
                ST["ff", hf] = act(lambda e: e.activation(ff[:, hf], PS[:, 2 + hf, :], ACT.Gelu, bias=W["fdb"]), m)
                for t in range(4):
                    tasks.spawn(ff_out(hf, t))
                    yield

            FU = W["fuBD"].rearrange("p (b n) -> p b n", b=4)
            tr = Ring([0, 1, 2, 3])
            s_o = dsem("s_o")

            def ff_out(hf, t):
                while not (misc and tr):
                    yield
                bk, bf = misc.take()
                s, sf = tr.take()
                m = pe(lambda e: e.matmul(PS[:, bk, :], ff[:, hf, t * P:(t + 1) * P], FU, start=True, stop=True),
                       ST["ff", hf], bf)
                yield
                v = PS[:, bk, :].rearrange("p (b n) -> p b n", b=4)
                tmp = tmpo[:, s]
                xv = X[:, 16 * hf + t:16 * hf + 16:4, :]
                hv = HR[:, 16 * hf + t:16 * hf + 16:4, :]
                a = dve(lambda e: e.tensor_tensor(tmp, v, hv, ALU.add), m, sf)
                misc.free(bk, a)
                yield
                a = pool(lambda e: e.tensor_tensor(tmp, tmp, W["fubB"].unsqueeze(1).to_broadcast([P, 4, P]), ALU.add), a)
                yield
                yield
                a = dve(lambda e: e.tensor_tensor(tmp, tmp, GB1[:, 4 * hf:4 * hf + 4, :], ALU.mult), a)
                a = dve(lambda e: e.tensor_tensor(xv, xv, tmp, ALU.add), a)
                tr.free(s, a)
                ST["o"] = sp.dma(out_d[:, 16 * hf + t:16 * hf + 16:4, :], xv, s_o, a)

            tasks = Tasks()
            tasks.spawn(prep(0))
            while ("x", 0) not in ST:
                tasks.tick()
            work = [(b, e_) for b in range(NB) for e_ in range(8)]
            for n, (b, e_) in enumerate(work):
                if e_ == 0 and b + 1 < NB:
                    tasks.spawn(prep(b + 1))
                while ("gw", b) not in ST:
                    tasks.tick()
                for d in range(n, n + 5):
                    if d < len(work) and ("gb",) + work[d] not in ST and ("gw", work[d][0]) in ST and gsr:
                        load_g(*work[d])
                expert(b, e_)
                tasks.tick(4)
                if e_ == 7:
                    tasks.spawn(post(b))
            tasks.finish()
            last = ST["o"]
            D.close()
            sp(lambda e: e.nop(), last)

        ffn1()

        for q in queues:
            q.count()
        block = ctx.enter_context(nc.Block())

        @block.sync
        def _(e):
            sp.emit(e)

        @block.gpsimd
        def _(e):
            pool.emit(e)

        @block.vector
        def _(e):
            dve.emit(e)

        @block.scalar
        def _(e):
            act.emit(e)

        @block.tensor
        def _(e):
            pe.emit(e)


def kernel(**inputs):
    import concourse.bacc as bacc
    from concourse.bass_utils import run_bass_kernel_spmd

    I = {k: np.asarray(v) for k, v in inputs.items()}
    col = lambda a: np.asarray(a).reshape(-1, 1)
    rows = lambda a: np.broadcast_to(np.asarray(a).reshape(1, -1), (P, np.asarray(a).size))
    z = lambda *s: np.zeros(s, np.float32)
    bd = z(P, 8, P)
    for b in range(8):
        bd[16 * b:16 * b + 16, b, :] = I["L1_attn_Wout"]
    fu = z(P, 4, P)
    for b in range(4):
        fu[32 * b:32 * b + 32, b, :] = I["L1_ffn_ff_up_w"].T
    bin_ = I["L1_attn_b_in"]
    b5 = np.stack([np.tile(v, 8) for v in (bin_[0:16], bin_[16:48:2], bin_[17:48:2], bin_[48:80:2], bin_[49:80:2])], 1)
    W1 = np.concatenate([I["L0_ffn_W1"], I["L0_ffn_Ws1"][None]], 0)
    b1 = np.concatenate([I["L0_ffn_b1"], I["L0_ffn_bs1"][None]], 0)
    W2 = np.concatenate([I["L0_ffn_W2"], I["L0_ffn_Ws2"][None]], 0)
    b2p = z(P, P)
    b2p[0:8] = I["L0_ffn_b2"]
    b2p[8] = I["L0_ffn_bs2"]
    w12 = np.stack([W1.transpose(2, 0, 1), W2.reshape(9, P, 4, P).transpose(3, 0, 2, 1).reshape(P, 9, 512)], 2)
    parts = {
        "c": np.concatenate([I["L0_c"].T, I["L1_c"].T], 1), "wmod0": I["L0_wmod"], "ident": np.eye(P, dtype=np.float32),
        "bq": col(I["L0_attn_bq"]), "bk": col(I["L0_attn_bk"]),
        "WqT": I["L0_attn_Wq"].T, "WkT": I["L0_attn_Wk"].T, "WvT": I["L0_attn_Wv"].T, "WoT": I["L0_attn_Wo"].T,
        "bvB": rows(I["L0_attn_bv"]), "boB": rows(I["L0_attn_bo"]),
        "b2p": b2p, "b1T": b1.reshape(9, 4, P).transpose(2, 0, 1).reshape(P, -1),
        "wr0": I["L0_ffn_w_router"].T, "desc": rows(np.arange(8, 0, -1).astype(np.float32)),
        "wmod1": I["L1_wmod"], "convw": I["L1_attn_conv_w"][:, 0, :], "convb": col(I["L1_attn_conv_b"]),
        "Win": I["L1_attn_Win"], "bin5": b5, "Alog": col(np.tile(I["L1_attn_A_log"], 8)), "WoutBD": bd.reshape(P, -1),
        "boutB": rows(I["L1_attn_b_out"]), "dw": I["L1_ffn_dw_kernel"][:, 0, :], "dwb": col(I["L1_ffn_dw_bias"]),
        "pwT": I["L1_ffn_pw_w"].T, "pwb": col(I["L1_ffn_pw_b"]), "rw1T": I["L1_ffn_router_w"].T,
        "rb1B": rows(I["L1_ffn_router_b"]), "ewT": I["L1_ffn_expert_w"].transpose(2, 0, 1).reshape(P, -1),
        "ebT": I["L1_ffn_expert_b"].T, "owT": I["L1_ffn_out_w"].T, "obB": rows(I["L1_ffn_out_b"]),
        "nwB": rows(I["L1_ffn_norm_w"]), "fdT": I["L1_ffn_ff_down_w"].T, "fdb": col(np.tile(I["L1_ffn_ff_down_b"], 4)),
        "fuBD": fu.reshape(P, -1), "fubB": rows(I["L1_ffn_ff_up_b"]),
    }
    small = z(8, 8, P)
    for i, n in enumerate("qkvo"):
        small[0:8, i] = I[f"L0_attn_A{n}"]
        small[0:8, 4 + i] = I[f"L0_attn_B{n}"].T
    arrays = {"x": np.ascontiguousarray(I["L0_attn_x"].reshape(NT, P, P).transpose(1, 0, 2))}
    for i, pack in ((0, PACK0), (1, PACK1), (3, PACK3)):
        arrays[f"p{i}"] = np.ascontiguousarray(np.concatenate([parts[n].reshape(P, w) for n, w in pack], 1))
    arrays["w12"] = np.ascontiguousarray(w12)
    arrays["small"] = small.reshape(8, -1)
    nc = bacc.Bacc("TRN2", target_bir_lowering=False, num_devices=1)
    args = [nc.dram_tensor(f"in_{n}", a.shape, F32, kind="ExternalInput").ap() for n, a in arrays.items()]
    args.append(nc.dram_tensor("out_0", (P, NT, P), F32, kind="ExternalOutput").ap())
    adaln_kernel(nc, *args)
    r = run_bass_kernel_spmd(nc, [{f"in_{n}": a for n, a in arrays.items()}], core_ids=[0])
    y = np.asarray(r.results[0]["out_0"])
    return np.ascontiguousarray(y.transpose(1, 0, 2)).reshape(8, 512, P)
```

```python
from contextlib import ExitStack

import numpy as np

import concourse.bass as bass
from concourse import mybir

P = 128
NB = 8
NT = 32
F32 = mybir.dt.float32
F32R = mybir.dt.float32r
BF16 = mybir.dt.bfloat16
ALU = mybir.AluOpType
ACT = mybir.ActivationFunctionType
AX = mybir.AxisListType

PACK0 = [("c", 16), ("wmod0", 768), ("ident", 128), ("bq", 1), ("bk", 1), ("WqT", 128), ("WkT", 128),
         ("WvT", 128), ("WoT", 128), ("bvB", 128), ("boB", 128)]
PACK1 = [("b1T", 36), ("wr0", 8), ("desc", 8), ("b2p", 128)]
PACK2 = [("wmod1", 768), ("convw", 4), ("convb", 1), ("Win", 80), ("bin5", 5), ("Alog", 1), ("WoutBD", 1024),
         ("boutB", 128)]
PACK3 = [("dw", 3), ("dwb", 1), ("pwT", 128), ("pwb", 1), ("rw1T", 8), ("rb1B", 8),
         ("ewT", 1024), ("ebT", 8), ("owT", 128), ("obB", 128), ("nwB", 128), ("fdT", 32), ("fdb", 1),
         ("fuBD", 512), ("fubB", 128)]

QTERM = [0, 0, 1, 1, 0, 2]
KTERM = [0, 1, 0, 1, 2, 0]


def width(pack):
    return sum(w for _, w in pack)


def columns(ap):
    return int(np.prod(ap.shape[1:]))


class Note:

    def activation(self, *a, **k):
        return lambda e: e.activation(*a, **k), columns(a[0])

    def bn_stats(self, *a, **k):
        return lambda e: e.bn_stats(*a, **k), columns(a[1])

    def memset(self, *a, **k):
        return lambda e: e.memset(*a, **k), columns(a[0])

    def mul(self, *a, **k):
        return lambda e: e.mul(*a, **k), columns(a[0])

    def reciprocal(self, *a, **k):
        return lambda e: e.reciprocal(*a, **k), 6 * columns(a[0])

    def scalar_tensor_tensor(self, *a, **k):
        return lambda e: e.scalar_tensor_tensor(*a, **k), columns(a[0])

    def tensor_copy(self, *a, **k):
        return lambda e: e.tensor_copy(*a, **k), columns(a[0])

    def tensor_reduce(self, *a, **k):
        return lambda e: e.tensor_reduce(*a, **k), columns(a[1])

    def tensor_scalar(self, *a, **k):
        return lambda e: e.tensor_scalar(*a, **k), columns(a[0])

    def tensor_tensor(self, *a, **k):
        return lambda e: e.tensor_tensor(*a, **k), columns(a[0]) * (96 if a[3] == ALU.pow else 1)

    def tensor_tensor_scan(self, *a, **k):
        return lambda e: e.tensor_tensor_scan(*a, **k), columns(a[0])

    def transpose(self, *a, **k):
        return lambda e: e.transpose(*a, **k), 2 * columns(a[0])

    def matmul(self, *a, **k):
        return lambda e: e.matmul(*a, **k), columns(a[0]) * (4 if a[1].dtype == F32 else 1) // (4 if a[0].shape[0] <= 32 else 1)

    def nop(self, *a, **k):
        return lambda e: e.nop(*a, **k), 0


NOTE = Note()


class Op:

    def __init__(self, fn, waits, sem=None, val=None):
        self.fn, self.waits, self.sem, self.val = fn, waits, sem, val
        self.t = 0.0
        self.asked = False


class Queue:

    def __init__(self, sem, fixed, per_column):
        self.sem, self.ops, self.gate = sem, [], []
        self.fixed, self.per_column, self.clock = fixed, per_column, 0.0

    def put(self, op, cost, late=0.0):
        op.waits = flat(op.waits) + self.gate
        self.gate = []
        for w in op.waits:
            w.asked = True
            self.clock = max(self.clock, w.t + 0.12)
        self.clock += cost
        op.t = self.clock + late
        self.ops.append(op)
        return op

    def __call__(self, fn, *waits):
        call, n = fn(NOTE)
        return self.put(Op(call, waits, self.sem), self.fixed + n * self.per_column)

    def dma(self, out, in_, dsem, *waits):
        dsem[1] += 16
        return self.put(Op(lambda e: e.dma_start(out, in_), waits, dsem[0], dsem[1]), 0.4,
                        2.0 + out.shape[0] * columns(out) / 45e3)

    def count(self):
        n = 0
        for op in self.ops:
            if op.sem is self.sem and op.asked:
                n += 1
                op.val = n

    def emit(self, eng):
        seen = {}
        for op in self.ops:
            need = {}
            for w in op.waits:
                need[id(w.sem)] = max(need.get(id(w.sem), (0, None))[0], w.val), w.sem
            for k, (v, s) in need.items():
                if seen.get(k, 0) < v:
                    eng.wait_ge(s, v)
                    seen[k] = v
            ins = op.fn(eng)
            if op.sem is not self.sem:
                ins.then_inc(op.sem, 16)
            elif op.asked:
                ins.then_inc(self.sem, 1)


def flat(ws):
    out = []
    for w in ws:
        if isinstance(w, (list, tuple)):
            out += flat(w)
        elif w is not None:
            out.append(w)
    return out


class Ring:

    def __init__(self, slots):
        self.slots = [(s, None) for s in slots]

    def __bool__(self):
        return bool(self.slots)

    def take(self):
        return self.slots.pop(0)

    def free(self, s, op):
        self.slots.append((s, op))


class Tasks:

    def __init__(self, pace):
        self.all, self.pace = [], pace

    def spawn(self, *gens):
        self.all += [[g, 0.0] for g in gens]

    def step(self, a):
        y = next(a[0], self)
        if y is self:
            self.all.remove(a)
            return True
        a[1] = max([w.t for w in flat([y])], default=0.0)
        return y is not None

    def tick(self, n=1):
        for _ in range(n):
            for a in list(self.all):
                if a[1] <= self.pace.clock:
                    self.step(a)

    def push(self):
        if not any([self.step(a) for a in list(self.all) if a[1] <= self.pace.clock]):
            later = [a for a in self.all if a[1] > self.pace.clock]
            if later:
                self.step(min(later, key=lambda a: a[1]))

    def fill(self, t):
        while any([self.step(a) for a in sorted(self.all, key=lambda a: a[1]) if a[1] <= t]):
            pass

    def finish(self):
        while self.all:
            self.push()


def adaln_kernel(nc, x_d, p0_d, p1_d, p2_d, p3_d, w12_d, small_d, out_d):
    ctx = ExitStack()
    with ctx:
        def sem(name):
            return ctx.enter_context(nc.semaphore(name))

        def sb(name, shape, dt=F32, c=None):
            return (c or ctx).enter_context(nc.sbuf_tensor(name, shape, dt))

        pe, dve, act, pool, sp = (Queue(sem(n), f, c) for n, f, c in (
            ("s_pe", 0.0, 0.42e-3), ("s_dve", 0.06, 1.05e-3), ("s_act", 0.19, 0.7e-3), ("s_pool", 0.15, 2.1e-3),
            ("s_sp", 0.05, 0.0)))
        queues = [pe, dve, act, pool, sp]

        def dsem(name):
            return [sem(name), 0]

        def barrier():
            last = [q.ops[-1] for q in queues if q.ops]
            for q in queues:
                q.gate = q.gate + last
                for w in last:
                    w.asked = True

        PS = ctx.enter_context(nc.psum_tensor("PS", [P, 8, 512], F32))
        X = sb("X", [P, NT, P])
        p0 = sb("p0", [P, width(PACK0)])
        p1 = sb("p1", [P, width(PACK1)])
        small = sb("small", [8, 8 * P])
        stage = sb("stage", [P, 2, 2, 512])
        stats = sb("stats", [P, NT, 6])
        lnw = sb("lnw", [P, 6, NT])
        half = sb("half", [P, 32])
        eb = sb("eb", [P, 32])
        cs = sb("cs", [P, 16])
        cst = sb("cst", [P, 3, 16])
        mf = sb("mf", [P, 2, 6, 8])
        mft = sb("mft", [P, 2, 2, 8])

        def views(t, pack):
            d, o = {}, 0
            for n, w in pack:
                d[n] = t[:, o:o + w]
                o += w
            return d

        W = views(p0, PACK0)
        W.update(views(p1, PACK1))
        ident = W["ident"]

        s_x = [dsem(f"s_x{i}") for i in range(8)]
        s_p0, s_p1, s_p2, s_p3, s_small = (dsem(n) for n in ("s_p0", "s_p1", "s_p2", "s_p3", "s_small"))
        s_w12 = [dsem(f"s_w12{i}") for i in range(2)]
        ld_x = [sp.dma(X[:, 0:4, :], x_d[:, 0:4, :], s_x[0])]
        ld_p0 = act.dma(p0[:], p0_d, s_p0)
        ld_small = sp.dma(small[:], small_d, s_small)
        ld_x += [sp.dma(X[:, 4 * i:4 * i + 4, :], x_d[:, 4 * i:4 * i + 4, :], s_x[i]) for i in range(1, 8)]
        ld_p1 = sp.dma(p1[:], p1_d, s_p1)
        wld = {e_: (i, sp.dma(stage[:, i], w12_d[:, e_], s_w12[i])) for i, e_ in enumerate((8, 0))}
        half_ok = pool(lambda e: e.memset(half[:], -0.5))
        eb_ok = pool(lambda e: e.memset(eb[:], float(np.e)))

        def clip_gate(out, g, t0, t1, *w):
            a = dve(lambda e: e.tensor_scalar(t0, g, 0.0, 2.0, ALU.is_ge, ALU.mult), *w)
            b = dve(lambda e: e.scalar_tensor_tensor(t1, t0, 1.0, g, ALU.subtract, ALU.mult), a)
            b = dve(lambda e: e.tensor_scalar(t1, t1, 0.25, None, ALU.max), b)
            return dve(lambda e: e.scalar_tensor_tensor(out, t0, 1.0, t1, ALU.subtract, ALU.mult), a, b)

        def mod_rows(L, k, wmod, dst, t0, t1, banks, *w):
            mms = []
            for b in range(8):
                o = PS[:, banks[b // 4], 128 * (b % 4):128 * (b % 4) + 128]
                l = cs[:, 8 * L + b:8 * L + b + 1].to_broadcast([P, P])
                mms.append(pe(lambda e, o=o, l=l: e.matmul(o, l, wmod[:, k * P:(k + 1) * P], start=True, stop=True), *w))
            g = PS[:, banks[0]:banks[0] + 2, :].rearrange("p a n -> p (a n)")
            return clip_gate(dst[:].rearrange("p b n -> p (b n)"), g, t0, t1, mms[-1])

        def mod_cols(L, wmod, bank, *w):
            o = PS[:, bank, 0:48].rearrange("p (k b) -> p k b", k=6)
            for k in range(6):
                m = pe(lambda e, k=k: e.matmul(o[:, k, :], wmod[:, k * P:(k + 1) * P], cs[:, 8 * L:8 * L + 8],
                                               start=True, stop=True), *w)
            c = dve(lambda e: e.tensor_copy(mf[:, L], o), m)
            r = []
            for k in (1, 4):
                r.append(dve(lambda e, k=k: e.tensor_scalar(mf[:, L, k], mf[:, L, k], 1.0, None, ALU.add), c))
            for k in (2, 5):
                r.append(clip_gate(mf[:, L, k], mf[:, L, k], mft[:, 0, k // 3], mft[:, 1, k // 3], c))
            return r

        def ln_stats(b, src, eps, centred, *w):
            a = 4 * b
            for t in range(4):
                s = dve(lambda e, t=t: e.bn_stats(stats[:, a + t, :], src[:, a + t, :]), *w)
                if t == 1:
                    yield ()
            me, mo, ve, vo = (stats[:, a:a + 4, i] for i in (1, 4, 2, 5))
            m, d, v, _, rs, nm = (lnw[:, i, a:a + 4] for i in range(6))
            if centred:
                o1 = dve(lambda e: e.tensor_tensor(m, me, mo, ALU.add), s)
                o2 = dve(lambda e: e.tensor_tensor(d, me, mo, ALU.subtract), s)
                o3 = dve(lambda e: e.tensor_tensor(v, ve, vo, ALU.add), s)
                o4 = dve(lambda e: e.scalar_tensor_tensor(d, d, 0.25, d, ALU.mult, ALU.mult), o2)
            else:
                o1 = dve(lambda e: e.tensor_tensor(m, me, me, ALU.mult), s)
                o2 = dve(lambda e: e.tensor_tensor(d, mo, mo, ALU.mult), s)
                o3 = dve(lambda e: e.tensor_tensor(v, ve, vo, ALU.add), s)
                o4 = dve(lambda e: e.tensor_tensor(d, m, d, ALU.add), o1, o2)
                o4 = dve(lambda e: e.tensor_scalar(d, d, 0.5, None, ALU.mult), o4)
            yield o4
            o5 = dve(lambda e: e.scalar_tensor_tensor(v, v, 1.0 / 128, d, ALU.mult, ALU.add), o3, o4)
            o6 = dve(lambda e: e.tensor_scalar(v, v, eps, None, ALU.add), o5)
            yield o6
            o8 = pool(lambda e: e.tensor_tensor(rs, v, half[:, 0:4], ALU.pow), o6, half_ok)
            yield o8
            if centred:
                o8 = dve(lambda e: e.scalar_tensor_tensor(nm, m, -0.5, rs, ALU.mult, ALU.mult), o8, o1)
                yield o8
            return o8

        early = {}

        def ln_batch(b, Z, zr, banks, dsts, scale, shift, engs, *w):
            st = early.pop(b) if b in early else (yield from ln_stats(b, X, 1e-5, True, *w))
            while not zr:
                yield
            z, zfree = zr.take()
            os = []
            for t in range(4):
                i = 4 * b + t
                zt, rs, nm = Z[:, z, t, :], lnw[:, 4, i:i + 1], lnw[:, 5, i:i + 1]
                if engs[t] is act:
                    o = act(lambda e: e.activation(zt, X[:, i, :], ACT.Identity, bias=nm, scale=rs), st, zfree)
                else:
                    o = engs[t](lambda e: e.tensor_scalar(zt, X[:, i, :], rs, nm, ALU.mult, ALU.add), st, zfree)
                os.append(o)
                if t == 1:
                    yield ()
            yield os
            while not banks:
                yield
            bk, bfree = banks.take()
            yield bfree
            for t in range(4):
                m = pe(lambda e, t=t: e.transpose(PS[:, bk, t * P:(t + 1) * P], Z[:, z, t, :], ident), os[t], bfree)
            zr.free(z, m)
            yield m
            hs = []
            for dst in dsts:
                hs.append(act(lambda e, dst=dst: e.activation(dst, PS[:, bk, :], ACT.Identity, bias=shift, scale=scale),
                              m, *w))
                yield ()
            banks.free(bk, hs[-1])
            return hs, os

        o = act(lambda e: e.activation(cst[:, 0], W["c"], ACT.Exp, scale=-1.0), ld_p0)
        o = dve(lambda e: e.tensor_scalar(cst[:, 1], cst[:, 0], 1.0, None, ALU.add), o)
        o = dve(lambda e: e.reciprocal(cst[:, 2], cst[:, 1]), o)
        cs_ok = dve(lambda e: e.tensor_tensor(cs[:], W["c"], cst[:, 2], ALU.mult), o, ld_p0)
        mc0 = mod_cols(0, W["wmod0"], 0, cs_ok, ld_p0)

        def attention():
            A = ExitStack()
            Q = sb("Q", [P, 3, 16, 512], BF16, A)
            K = sb("K", [P, 3, 8, 512], BF16, A)
            E = sb("E", [P, 2, 4, 2, 512], F32, A)
            V = sb("V", [P, 3, 4, 16, 9], F32, A)
            Wq, Wk, Wv, Wo = (sb(n, [P, P], F32, A) for n in ("Wq", "Wk", "Wv", "Wo"))
            bqs = sb("bqs", [P, 2], F32, A)
            GA = sb("GA", [P, 8, P], F32, A)
            GB = sb("GB", [P, 8, P], F32, A)
            Z = sb("Z", [P, 1, 4, P], F32, A)
            hT = sb("hT", [P, 1, 512], F32, A)
            qf = sb("qf", [P, 2, 512], F32, A)
            SPL = sb("SPL", [P, 2, 3, 512], BF16, A)
            mx = sb("mx", [P, 2, 4, 16], F32, A)
            nmf = sb("nmf", [8, 512], F32, A)
            nms = sb("nms", [8, 3, 512], BF16, A)
            ov = sb("ov", [P, 2, 512], F32, A)
            rec = sb("rec", [P, 4, 4], F32, A)
            otok = sb("otok", [P, 4, P], F32, A)
            oT = sb("oT", [P, 512], F32, A)
            dqk = nc.dram_tensor("dqk", [8, 2, 3, P, 512], BF16, kind="Internal").ap()
            dmx = nc.dram_tensor("dmx", [8, 2, 3, 8, 512], BF16, kind="Internal").ap()

            SC = float(1.0 / np.sqrt(np.float32(8.0)))
            t0 = E[:, 0].rearrange("p a b n -> p (a b n)")[:, 0:1024]
            t1 = E[:, 0].rearrange("p a b n -> p (a b n)")[:, 1024:2048]
            weff = {}
            for i in range(4):
                m = pe(lambda e, i=i: e.matmul(PS[:, 1, i * P:(i + 1) * P], small[0:8, i * P:(i + 1) * P],
                                               small[0:8, (4 + i) * P:(5 + i) * P], start=True, stop=True), ld_small)
            for i, (n, dst) in enumerate((("q", Wq), ("k", Wk), ("v", Wv), ("o", Wo))):
                weff[n] = dve(lambda e, i=i, n=n, dst=dst: e.scalar_tensor_tensor(
                    dst[:], PS[:, 1, i * P:(i + 1) * P], 2.0, W[f"W{n}T"], ALU.mult, ALU.add), m, ld_p0)
            bqs_ok = [dve(lambda e: e.tensor_scalar(bqs[:, 0:1], W["bq"], SC, None, ALU.mult), ld_p0),
                      dve(lambda e: e.tensor_copy(bqs[:, 1:2], W["bk"]), ld_p0)]
            qz = [pool(lambda e: e.memset(Q[:, 0].bitcast(F32), 0.0))]
            kz = []
            vz = [pool(lambda e, i=i: e.memset(V[:, i, :, :, 8:9], 1.0)) for i in range(3)]
            oz = dve(lambda e: e.memset(PS[:, 6, :], 0.0))

            misc = Ring([7])
            zr = Ring([0])
            hr = Ring([0])
            fr = Ring([0, 1])
            sr = Ring([0, 1])
            mring = Ring([3, 4, 5])
            sring = Ring([2])
            ering = Ring([])
            ovr = Ring([0, 1])
            pvring = Ring([6])
            s_w = [dsem(f"s_w{i}") for i in range(2)]
            s_q = [dsem(f"s_q{i}") for i in range(3)]
            s_mw = [dsem(f"s_mw{i}") for i in range(2)]
            s_m = [dsem(f"s_m{i}") for i in range(2)]
            S = {}
            done = {}

            def split(src, dst, a, *w):
                h = act(lambda e: e.activation(dst[:, 0], src, ACT.Copy), a, *w)
                yield h
                r = pool(lambda e: e.tensor_tensor(src, src, dst[:, 0], ALU.subtract), h)
                yield r
                m = act(lambda e: e.activation(dst[:, 1], src, ACT.Copy), r)
                yield m
                return pool(lambda e: e.tensor_tensor(dst[:, 2], src, dst[:, 1], ALU.subtract), m)

            def prep_qk(b, i, hop):
                while not (misc and fr and sr):
                    yield
                bk, bf = misc.take()
                f, ff = fr.take()
                s, sf = sr.take()
                yield [bf, ff, sf]
                w, wop = ((Wq, weff["q"]), (Wk, weff["k"]))[i]
                m = pe(lambda e: e.matmul(PS[:, bk, :], w[:], hT[:, 0], start=True, stop=True), hop, wop, bf)
                yield m
                a = act(lambda e: e.activation(qf[:, f], PS[:, bk, :], ACT.Identity, bias=bqs[:, i:i + 1],
                                               scale=(SC, 1.0)[i]), m, bqs_ok, ff)
                misc.free(bk, a)
                d = yield from split(qf[:, f], SPL[:, s], a, sf)
                fr.free(f, d)
                wr = sp.dma(dqk[b, i].rearrange("t p n -> p t n"), SPL[:, s], s_w[i], d)
                sr.free(s, wr)
                u = b % 3
                while b >= 3 and (b - 3, "done") not in S:
                    yield
                prev = S.get((b - 3, "E"))
                for par in range(2):
                    for t in range(6):
                        src = dqk[b, i, (QTERM, KTERM)[i][t]].rearrange("(p two d) n -> two d p n", two=2, d=8)[par]
                        r = slice(par * 48 + t * 8, par * 48 + t * 8 + 8)
                        dst = Q[r, u, par:16:2, :] if i == 0 else K[r, u]
                        S[b, "qk"] = (act if b == 0 and i == 1 else sp).dma(dst, src, s_q[u], wr, prev,
                                                                           qz[u] if i == 0 else None)
                S[b, "qkn"] = S.get((b, "qkn"), 0) + 1

            def prep(b):
                while not hr:
                    yield
                h, hf = hr.take()
                (hop,), zop = yield from ln_batch(b, Z, zr, misc, [hT[:, 0]], mf[:, 0, 1, b:b + 1], mf[:, 0, 0, b:b + 1],
                                                  [dve] * 4 if b == 0 else [pool] * 4, mc0, hf, ld_x[b])
                tasks.spawn(prep_qk(b, 0, hop))
                yield ()
                tasks.spawn(prep_qk(b, 1, hop))
                yield ()
                while not misc:
                    yield
                bk, bf = misc.take()
                yield bf
                for t in range(4):
                    m = pe(lambda e, t=t: e.matmul(PS[:, bk, t * P:(t + 1) * P], hT[:, 0, t * P:(t + 1) * P], Wv[:],
                                                   start=True, stop=True), hop, weff["v"], bf)
                yield m
                hr.free(h, m)
                v = b % 3
                while b >= 3 and (b - 3, "done") not in S:
                    yield
                S[b, "v"] = dve(lambda e: e.tensor_tensor(
                    V[:, v, :, :, 0:8], PS[:, bk, :].rearrange("p (t h d) -> p t h d", t=4, h=16),
                    W["bvB"].rearrange("p (h d) -> p h d", h=16).unsqueeze(1).to_broadcast([P, 4, 16, 8]), ALU.add),
                    m, vz, S.get((b - 3, "pv")))
                misc.free(bk, S[b, "v"])
                while "gb" not in S:
                    yield
                xv = X[:, 4 * b:4 * b + 4, :]
                S[b, "xb"] = pool(lambda e: e.tensor_tensor(xv, xv, GB[:, b:b + 1, :].to_broadcast([P, 4, P]), ALU.add),
                                  zop, S["gb"])

            def max_unit(b, i):
                h, qt = i // 4, i % 4
                while S.get((b, "qkn")) != 2:
                    tasks.push()
                u = b % 3
                bk, bf = mring.take()
                m = pe(lambda e: e.matmul(PS[:, bk, :], Q[0:96, u, h, qt * P:(qt + 1) * P], K[0:96, u, h // 2, :],
                                          start=True, stop=True), S[b, "qk"], bf)
                r = dve(lambda e: e.tensor_reduce(mx[:, b % 2, qt, h:h + 1], PS[:, bk, :], AX.X, ALU.max), m,
                        S.get((b - 2, "mt")))
                mring.free(bk, r)
                if i % 32 == 31:
                    S[b, "mx", i // 32] = r

            def max_rows(b, half):
                yield S[b, "mx", half]
                while not (misc and nmr):
                    yield
                bk, bf = misc.take()
                _, nf = nmr.take()
                yield [bf, nf]
                for t in range(4):
                    m = pe(lambda e, t=t: e.transpose(PS[0:8, bk, t * P:(t + 1) * P],
                                                      mx[:, b % 2, t, 8 * half:8 * half + 8], ident), S[b, "mx", half], bf)
                S[b, "mt"] = m
                yield m
                a = act(lambda e: e.mul(nmf[:], PS[0:8, bk, :], -1.0), m, nf)
                misc.free(bk, a)
                d = yield from split(nmf[:], nms, a, nf)
                yield d
                wr = act.dma(dmx[b, half].rearrange("t h n -> h t n"), nms[:], s_mw[half], d)
                nmr.free(0, wr)
                yield wr
                S[b, "m", half] = act.dma(Q[96:99, b % 3, 8 * half:8 * half + 8, :], dmx[b, half], s_m[half], wr)

            def exp_unit(b, i):
                g, kp, j, c = i // 16, i // 8 % 2, i // 2 % 4, i % 2
                h, u, kt = 4 * g + j, b % 3, 2 * kp + c
                while (b, "m", h // 8) not in S or (b, "v") not in S:
                    tasks.push()
                bk, bf = sring.take()
                m = pe(lambda e: e.matmul(PS[:, bk, :], K[0:99, u, h // 2, kt * P:(kt + 1) * P], Q[0:99, u, h, :],
                                          start=True, stop=True), S[b, "qk"], S[b, "m", h // 8], kz, bf)
                S[b, "E"] = m
                if i % 8 == 0:
                    S["e"] = ering.take()
                es, ef = S["e"]
                a = act(lambda e: e.activation(E[:, es, j, c], PS[:, bk, :], ACT.Exp), m, ef)
                sring.free(bk, a)
                return es, a

            def pv(b, g, kp, c, es, a):
                kt = 2 * kp + c
                if kt == 0:
                    S["pvb"] = pvring.take()
                bk, bf = S["pvb"]
                for j in range(4):
                    m = pe(lambda e, j=j: e.matmul(PS[32 * j:32 * j + 9, bk, :], V[:, b % 3, kt, 4 * g + j, :],
                                                   E[:, es, j, c, :], start=(kt == 0), stop=(kt == 3)),
                           a, S[b, "v"], bf, oz)
                S[b, "pv"] = m
                if c == 1:
                    ering.free(es, m)
                if kt == 3:
                    o, of = ovr.take()
                    cp = act(lambda e: e.activation(ov[:, o], PS[:, bk, :], ACT.Copy), m, of)
                    pvring.free(bk, cp)
                    S["ov"] = o, cp
                    tasks.spawn(heads_out(b, g))

            def heads_out(b, g):
                o, cp = S["ov"]
                yield cp
                while not misc:
                    yield
                bk, bf = misc.take()
                yield bf
                for t in range(4):
                    m = pe(lambda e, t=t: e.transpose(PS[:, bk, t * P:(t + 1) * P], ov[:, o, t * P:(t + 1) * P], ident), cp, bf)
                ovr.free(o, m)
                yield m
                v = PS[:, bk, :].rearrange("p (t j r) -> p t j r", t=4, j=4)
                r = dve(lambda e: e.reciprocal(rec[:], v[:, :, :, 8]), m)
                yield r
                S["o"] = dve(lambda e: e.tensor_tensor(
                    otok[:].rearrange("p t (g j d) -> p t g j d", g=4, j=4)[:, :, g], v[:, :, :, 0:8],
                    rec[:].unsqueeze(3).to_broadcast([P, 4, 4, 8]), ALU.mult), r, S.get("otr"))
                misc.free(bk, S["o"])
                if g < 3:
                    return
                S[b, "done"] = True
                yield S["o"]
                while not misc:
                    yield
                bk, bf = misc.take()
                yield bf
                for t in range(4):
                    m = pe(lambda e, t=t: e.transpose(PS[:, bk, t * P:(t + 1) * P], otok[:, t, :], ident), S["o"], bf)
                S["otr"] = m
                yield m
                S["oT"] = act(lambda e: e.activation(oT[:], PS[:, bk, :], ACT.Copy), m, S.get("om"))
                misc.free(bk, S["oT"])
                yield S["oT"]
                while not misc:
                    yield
                bk, bf = misc.take()
                yield bf
                for t in range(4):
                    m = pe(lambda e, t=t: e.matmul(PS[:, bk, t * P:(t + 1) * P], oT[:, t * P:(t + 1) * P], Wo[:],
                                                   start=True, stop=True), S["oT"], weff["o"], bf)
                S["om"] = m
                yield m
                v = PS[:, bk, :].rearrange("p (t n) -> p t n", t=4)
                xv = X[:, 4 * b:4 * b + 4, :]
                a = dve(lambda e: e.tensor_tensor(v, v, GA[:, b:b + 1, :].to_broadcast([P, 4, P]), ALU.mult), m, S["ga"])
                yield a
                S["x", b] = dve(lambda e: e.tensor_tensor(xv, v, xv, ALU.add), a, S[b, "xb"])
                misc.free(bk, S["x", b])
                if b < 2:
                    done[b] = yield from ln_stats(b, X, 1e-5, True, S["x", b])

            LEAD = 62
            tasks = Tasks(pe)
            nmr = Ring([0])
            mdone = [0]

            def max_next():
                n = mdone[0]
                if n >= 64 * NB:
                    return
                max_unit(n // 64, n % 64)
                mdone[0] += 1
                if n % 32 == 31:
                    tasks.spawn(max_rows(n // 64, n // 32 % 2))

            tasks.spawn(prep(0))
            while S.get((0, "qkn")) != 2:
                tasks.push()
            kz += [dve(lambda e: e.memset(K[96:99], 1.0))]
            S["ga"] = mod_rows(0, 2, W["wmod0"], GA, t0, t1, [0, 1], mc0, list(weff.values()))
            for i in range(2):
                sring.free(i, S["ga"])
                ering.free(i, S["ga"])
            S["gb"] = pool(lambda e: e.tensor_tensor(GB[:], GA[:], W["boB"].unsqueeze(1).to_broadcast([P, 8, P]),
                                                     ALU.mult), S["ga"])
            qz += [pool(lambda e, i=i: e.memset(Q[:, i].bitcast(F32), 0.0)) for i in (1, 2)]
            tasks.spawn(prep(1))
            for i in range(LEAD):
                max_next()
                tasks.tick()
            pend = []
            for b in range(NB):
                for i in range(64):
                    if i == 4 and b + 2 < NB:
                        tasks.spawn(prep(b + 2))
                    es, a = exp_unit(b, i)
                    max_next()
                    tasks.tick()
                    if pend and i % 4 == 3:
                        pend.pop(0)()
                    if i % 8 == 7:
                        g, kp = i // 16, i // 8 % 2
                        for c in range(2):
                            pend.append(lambda b=b, g=g, kp=kp, c=c, es=es, a=a: pv(b, g, kp, c, es, a))
            for f in pend:
                f()
                tasks.tick(2)
            tasks.finish()
            barrier()
            A.close()
            early.update(done)

        attention()

        def first(src, m, s, t, oh, bc, desc, *w):
            a = dve(lambda e: e.tensor_reduce(m, src, AX.X, ALU.max), *w)
            a = dve(lambda e: e.tensor_tensor(t, src, bc(m), ALU.is_equal), a)
            yield ()
            a = dve(lambda e: e.tensor_tensor(t, t, desc, ALU.mult), a, ld_p1)
            a = dve(lambda e: e.tensor_reduce(s, t, AX.X, ALU.max), a)
            return dve(lambda e: e.tensor_tensor(oh, t, bc(s), ALU.is_equal), a)

        def top2(M, wk, *w):
            oh1, oh2, t, w2 = (wk[:, i] for i in range(4))
            m1, m2, s = (wk[:, 4, :, i] for i in range(3))
            bc = lambda a: a.unsqueeze(2).to_broadcast([P, 4, 8])
            desc = W["desc"].unsqueeze(1).to_broadcast([P, 4, 8])
            a = yield from first(M, m1, s, t, oh1, bc, desc, *w)
            yield ()
            a = dve(lambda e: e.tensor_scalar(w2, oh1, -3.0e38, None, ALU.mult), a)
            a = dve(lambda e: e.tensor_tensor(w2, w2, M, ALU.add), a)
            yield ()
            a = yield from first(w2, m2, s, t, oh2, bc, desc, a)
            yield ()
            return a, m1, m2, oh1, oh2, bc

        def halves(src, hi, lo, eng_hi, eng_lo, *w):
            a = (act(lambda e: e.activation(hi, src, ACT.Copy), *w) if eng_hi is act
                 else eng_hi(lambda e: e.tensor_copy(hi, src), *w))
            b = eng_lo(lambda e: e.tensor_tensor(lo, src, hi.bitcast(F32), ALU.subtract), a)
            return a, b

        def product(o, ws, xs, start, stop, *w):
            (wh, wl), (xh, xl) = ws, xs
            pe(lambda e: e.matmul(o, wh, xh, start=start, stop=False), *w)
            pe(lambda e: e.matmul(o, wl, xh, start=False, stop=False))
            return pe(lambda e: e.matmul(o, wh, xl, start=False, stop=stop))

        def ffn0():
            B = ExitStack()
            Wh = sb("Wh", [P, 9, 2, 512], F32R, B)
            Wl = sb("Wl", [P, 9, 2, 512], F32R, B)
            Hf = sb("Hf", [P, 2, 512], F32, B)
            Hh = sb("Hh", [P, 2, 512], F32R, B)
            Hl = sb("Hl", [P, 2, 512], F32R, B)
            Z = sb("Zb", [P, 1, 4, P], F32, B)
            Gf = sb("Gf", [P, 3, 512], F32, B)
            Gh = sb("Gh", [P, 8, 512], F32R, B)
            Gl = sb("Gl", [P, 8, 512], F32R, B)
            gbs = sb("gbs", [P, 4, 512], F32, B)
            ty = sb("ty", [P, 2, 512], F32, B)
            acc = sb("acc", [P, 2, 512], F32, B)
            gt = sb("gt", [P, 2, 4, 9], F32, B)
            lg = sb("lg", [P, 4, 8], F32, B)
            wk = sb("wk", [P, 5, 4, 8], F32, B)
            gT = sb("gT", [P, 2, 512], F32, B)
            gsc = sb("gsc", [P, 8], F32, B)
            dg = nc.dram_tensor("dg", [8, 8, 512], F32, kind="Internal").ap()

            SCALE = float(1.0 / np.sqrt(1.25))
            gsc_ok = dve(lambda e: e.tensor_scalar(gsc[:], mf[:, 0, 5, :], SCALE, None, ALU.mult), mc0)
            gz = pool(lambda e: e.memset(gT[:], 0.0))
            g1s = [pool(lambda e, i=i: e.memset(gt[:, i, :, 8:9], 1.0)) for i in range(2)]
            s_gw = [dsem(f"s_gw{i}") for i in range(2)]
            s_g = [dsem(f"s_g{i}") for i in range(4)]
            zr, hr, stg, misc = Ring([0]), Ring([0, 1]), Ring([]), Ring([5, 6, 7])
            upr, dnr, wkr = Ring([0, 1, 2]), Ring([3, 4]), Ring([0])
            gfr, gr, gsr, tyr, accr, gTr, gtr = (Ring(range(n)) for n in (3, 8, 4, 2, 2, 2, 2))
            b1T = W["b1T"].rearrange("p (e f) -> p e f", e=9)
            order = (8, 0, 1, 2, 3, 4, 5, 6, 7)
            work = [(b, e_) for b in range(NB) for e_ in order]
            wok, hok, gok, ST, done = {}, {}, {}, {}, {}

            def load_w(e_):
                s, f = stg.take()
                wld[e_] = s, sp.dma(stage[:, s], w12_d[:, e_], s_w12[s], f)

            def split_w(e_):
                s, ld = wld[e_]
                v = lambda t: t.rearrange("p a n -> p (a n)")
                wok[e_] = halves(v(stage[:, s]), v(Wh[:, e_]), v(Wl[:, e_]), *((act, pool) if e_ == 8 else (dve, dve)), ld)
                stg.free(s, wok[e_][1])

            def prep(b):
                while not hr:
                    yield
                h, hf = hr.take()
                (a1, a2), _ = yield from ln_batch(b, Z, zr, misc, [Hf[:, h], Hh[:, h]], mf[:, 0, 4, b:b + 1],
                                                  mf[:, 0, 3, b:b + 1], [dve] * 4, hf)
                lo = dve(lambda e: e.tensor_tensor(Hl[:, h], Hf[:, h], Hh[:, h].bitcast(F32), ALU.subtract), a2)
                hok[b] = h, a2, lo
                while not misc:
                    yield
                bk, bf = misc.take()
                yield bf
                L = PS[:, bk, 0:32].rearrange("p (t e) -> p t e", t=4)
                for t in range(4):
                    m = pe(lambda e, t=t: e.matmul(L[:, t, :], Hf[:, h, t * P:(t + 1) * P], W["wr0"],
                                                   start=True, stop=True), a2, bf, ld_p1)
                yield m
                bc = lambda a: a.unsqueeze(2).to_broadcast([P, 4, 8])
                mx, sm = wk[:, 4, :, 4], wk[:, 4, :, 5]
                while not wkr:
                    yield
                _, wf = wkr.take()
                a = dve(lambda e: e.tensor_reduce(mx, L, AX.X, ALU.max), m, wf)
                a = dve(lambda e: e.tensor_tensor(lg[:], L, bc(mx), ALU.subtract), a)
                misc.free(bk, a)
                yield a
                f = lg[:].rearrange("p t e -> p (t e)")
                a = pool(lambda e: e.tensor_tensor(f, eb[:], f, ALU.pow), a, eb_ok)
                yield a
                a = dve(lambda e: e.tensor_reduce(sm, lg[:], AX.X, ALU.add), a)
                a = dve(lambda e: e.reciprocal(mx, sm), a)
                yield ()
                a = dve(lambda e: e.tensor_tensor(lg[:], lg[:], bc(mx), ALU.mult), a)
                a, _, _, oh1, oh2, _ = yield from top2(lg[:], wk, a)
                a = dve(lambda e: e.tensor_tensor(oh1, oh1, oh2, ALU.add), a)
                yield ()
                while not gtr:
                    yield
                g, gf = gtr.take()
                ok = dve(lambda e: e.tensor_tensor(gt[:, g, :, 0:8], oh1, lg[:], ALU.mult), a, gf)
                wkr.free(0, ok)
                yield ok
                while not (misc and gTr):
                    yield
                bk, bf = misc.take()
                yield bf
                for t in range(4):
                    m = pe(lambda e, t=t: e.transpose(PS[0:9, bk, t * P:(t + 1) * P], gt[:, g, t, :], ident), ok, bf, g1s)
                gtr.free(g, m)
                yield m
                while not gTr:
                    yield
                s, sf = gTr.take()
                c = act(lambda e: e.activation(gT[0:9, s], PS[0:9, bk, :], ACT.Copy), m, sf, gz)
                misc.free(bk, c)
                gok[b] = s, c, sp.dma(dg[b], gT[0:8, s], s_gw[b % 2], c)

            def load_g(b, e_):
                s, f = gsr.take()
                ST["gb", b, e_] = s, sp.dma(gbs[:, s], dg[b, e_:e_ + 1, :].to_broadcast([P, 512]), s_g[s], f, gok[b][2])

            def up(b, e_, fc):
                h, hi, lo = hok[b]
                bk, bf = upr.take()
                m = product(PS[:, bk, :], [w[:, e_, 0, fc * P:(fc + 1) * P] for w in (Wh, Wl)], (Hh[:, h], Hl[:, h]),
                            True, True, hi, lo, wok[e_], bf)
                if e_ == 7 and fc == 3:
                    hr.free(h, m)
                f, ff = gfr.take()
                a = act(lambda e: e.activation(Gf[:, f], PS[:, bk, :], ACT.Gelu_apprx_tanh,
                                               bias=b1T[:, e_, fc:fc + 1]), m, ff)
                upr.free(bk, a)
                g, gf = gr.take()
                ok = halves(Gf[:, f], Gh[:, g], Gl[:, g], act if fc % 2 else dve, pool if fc == 3 else dve, a, gf)
                gfr.free(f, ok[1])
                ST["g", b, e_, fc] = g, ok

            def down(b, e_, fc):
                if fc == 0:
                    ST["d"] = dnr.take()
                bk, bf = ST["d"]
                g, ok = ST["g", b, e_, fc]
                m = product(PS[:, bk, :], [w[:, e_, 1, fc * P:(fc + 1) * P] for w in (Wh, Wl)], (Gh[:, g], Gl[:, g]),
                            fc == 0, fc == 3 and e_ != 8, ok, bf)
                gr.free(g, m)
                if fc < 3:
                    return
                if e_ == 8:
                    while b not in gok:
                        tasks.push()
                    q, c, wr = gok[b]
                    m = pe(lambda e: e.matmul(PS[:, bk, :], W["b2p"], gT[:, q], start=False, stop=True), c, ld_p1)
                    gTr.free(q, [m, wr])
                    s, sf = accr.take()
                    ST["acc"] = s
                    a = act(lambda e: e.activation(acc[:, s], PS[:, bk, :], ACT.Copy), m, sf)
                    dnr.free(bk, a)
                else:
                    s = ST["acc"]
                    if ("gb", b, e_) not in ST:
                        load_g(b, e_)
                    q, ld = ST["gb", b, e_]
                    y, yf = tyr.take()
                    mu = dve(lambda e: e.tensor_tensor(ty[:, y], PS[:, bk, :], gbs[:, q], ALU.mult), m, ld, yf)
                    gsr.free(q, mu)
                    dnr.free(bk, mu)
                    a = pool(lambda e: e.tensor_tensor(acc[:, s], acc[:, s], ty[:, y], ALU.add), mu, ST["a"])
                    tyr.free(y, a)
                ST["a"] = a

            def finish(b):
                s, a = ST["acc"], ST["a"]
                yield a
                o = dve(lambda e: e.tensor_scalar(acc[:, s], acc[:, s], gsc[:, b:b + 1], None, ALU.mult), a, gsc_ok)
                yield o
                while not misc:
                    yield
                bk, bf = misc.take()
                yield bf
                for t in range(4):
                    m = pe(lambda e, t=t: e.transpose(PS[:, bk, t * P:(t + 1) * P], acc[:, s, t * P:(t + 1) * P], ident), o, bf)
                accr.free(s, m)
                yield m
                xv = X[:, 4 * b:4 * b + 4, :]
                v = PS[:, bk, :].rearrange("p (t n) -> p t n", t=4)
                x = dve(lambda e: e.tensor_tensor(xv, v, xv, ALU.add), m)
                misc.free(bk, x)
                if b < NB - 1:
                    done[b] = yield from ln_stats(b, X, 1e-5, True, x)

            tasks = Tasks(pe)
            tasks.spawn(prep(0))
            split_w(8)
            while 0 not in hok:
                tasks.push()
            for n in range(len(work) + 1):
                if n < 8:
                    split_w(order[n + 1])
                if n < 7:
                    load_w(order[n + 2])
                if n == 9:
                    _, freed = zip(*(stg.take() for _ in range(2)))
                    ST["p2"] = sp.dma(stage[:].rearrange("p a b n -> p (a b n)")[:, 0:width(PACK2)], p2_d, s_p2, freed)
                for fc in range(4):
                    for d in range(n, n + 3):
                        if d < len(work) and work[d][1] != 8 and ("gb",) + work[d] not in ST and work[d][0] in gok and gsr:
                            load_g(*work[d])
                    if n < len(work):
                        up(*work[n], fc)
                    if n > 0:
                        down(*work[n - 1], fc)
                    tasks.tick()
                if n % 9 == 0 and n // 9 + 1 < NB:
                    tasks.spawn(prep(n // 9 + 1))
                if n > 0 and work[n - 1][1] == 7:
                    tasks.spawn(finish(work[n - 1][0]))
            tasks.finish()
            barrier()
            B.close()
            early.update(done)
            return ST["p2"]

        ld_p2 = ffn0()

        def ssm():
            C = ExitStack()
            p3 = sb("p3", [P, width(PACK3)])
            W.update(views(p3, PACK3))
            W.update(views(stage[:].rearrange("p a b n -> p (a b n)"), PACK2))
            ld_p3 = sp.dma(p3[:], p3_d, s_p3)
            GA1 = sb("GA1", [P, 8, P])
            GB1 = sb("GB1", [P, 8, P])
            Z = sb("Zc", [P, 2, 4, P])
            BG = sb("BG", [P, 8, P], F32, C)
            Zs = sb("Zs", [P, 4, 4, P], F32, C)
            Hc = sb("Hc", [P, 5, 516], F32, C)
            XC = sb("XC", [P, 3, 512], F32, C)
            WP = sb("WP", [P, 3, 240], F32, C)
            WPh = sb("WPh", [P, 3, 240], F32R, C)
            WPl = sb("WPl", [P, 3, 240], F32R, C)
            XCh = sb("XCh", [P, 3, 512], F32R, C)
            XCl = sb("XCl", [P, 3, 512], F32R, C)
            tb = sb("tb", [P, 12, 512], F32, C)
            cv = sb("cv", [P, 12], F32, C)
            tA, tB = tb[:, 0:2].rearrange("p a n -> p (a n)"), tb[:, 2:4].rearrange("p a n -> p (a n)")
            mc1 = mod_cols(1, W["wmod1"], 0, ld_p2)

            z0 = pool(lambda e: e.memset(WP[:], 0.0))
            Win = W["Win"]
            pr = lambda o: Win[:, o:o + 32].rearrange("p (n k) -> p n k", k=2)
            a = dve(lambda e: e.tensor_copy(WP[:, 0, 112:128], Win[:, 0:16]), z0, ld_p2)
            wp_ok = [a]
            for i, o in ((1, 16), (2, 48)):
                a = dve(lambda e, i=i, o=o: e.tensor_tensor(WP[:, i, 112:128], pr(o)[:, :, 0], pr(o)[:, :, 1], ALU.add), z0)
                wp_ok.append(dve(lambda e, i=i: e.tensor_scalar(WP[:, i, 112:128], WP[:, i, 112:128], 0.5, None, ALU.mult), a))
            b5 = W["bin5"]
            c_ok = []
            for i in range(2):
                a = dve(lambda e, i=i: e.tensor_tensor(cv[:, i:i + 1], b5[:, 1 + 2 * i:2 + 2 * i], b5[:, 2 + 2 * i:3 + 2 * i], ALU.add), ld_p2)
                c_ok.append(dve(lambda e, i=i: e.tensor_scalar(cv[:, i:i + 1], cv[:, i:i + 1], 0.5, None, ALU.mult), a))
            a = act(lambda e: e.activation(cv[:, 6:7], W["Alog"], ACT.Exp), ld_p2)
            a = dve(lambda e: e.tensor_scalar(cv[:, 2:3], cv[:, 6:7], -1.0, None, ALU.mult), a)
            a3 = dve(lambda e: e.tensor_scalar(cv[:, 3:4], cv[:, 6:7], 1e-4, None, ALU.is_lt), a)
            a = dve(lambda e: e.tensor_scalar(cv[:, 7:8], cv[:, 3:4], -1.0, 1.0, ALU.mult, ALU.add), a3)
            a = dve(lambda e: e.scalar_tensor_tensor(cv[:, 8:9], cv[:, 2:3], cv[:, 7:8], cv[:, 3:4], ALU.mult, ALU.add), a)
            a = dve(lambda e: e.reciprocal(cv[:, 9:10], cv[:, 8:9]), a)
            a4 = dve(lambda e: e.tensor_tensor(cv[:, 4:5], cv[:, 9:10], cv[:, 7:8], ALU.mult), a)
            a5 = dve(lambda e: e.tensor_tensor(cv[:, 5:6], cv[:, 2:3], cv[:, 3:4], ALU.mult), a3)

            zr, banks = Ring([0, 1, 2, 3]), Ring([5, 6, 7])
            p0z = pool(lambda e: e.memset(Hc[:, :, 0:1], 0.0))
            p1z = pool(lambda e: e.memset(Hc[:, :, 513:516], 0.0))
            p2z = pool(lambda e: e.memset(XC[:], 0.0))
            for i in range(3):
                wp_ok.append(halves(WP[:, i], WPh[:, i], WPl[:, i], dve, dve, wp_ok[i]))
            xr, xhr, hcr = Ring([0, 1, 2]), Ring([0, 1, 2]), Ring([0, 1, 2, 3, 4])
            cw = W["convw"]
            bank_free = mc1
            last, gb1, xb = [], [], []
            turn = [0]

            def conv(b):
                while not hcr:
                    yield
                hb_, hbf = hcr.take()
                (h,), zop = yield from ln_batch(b, Zs, zr, banks, [Hc[:, hb_, 1:513]], mf[:, 1, 1, b:b + 1],
                                              mf[:, 1, 0, b:b + 1], [act, pool, act, pool], mc1, hbf)
                while not (xr and xhr and turn[0] == b):
                    yield
                x, xf = xr.take()
                o = XC[:, x, 0:511]
                a = act(lambda e: e.activation(o, Hc[:, hb_, 0:511], ACT.Identity, bias=W["convb"], scale=cw[:, 0:1]),
                        h, p0z, p1z, p2z, xf)
                yield a
                for k in range(1, 4):
                    a = dve(lambda e, k=k: e.scalar_tensor_tensor(
                        o, Hc[:, hb_, k:k + 511], cw[:, k:k + 1], o, ALU.mult, ALU.add), a)
                hcr.free(hb_, a)
                yield ()
                while not xhr:
                    yield
                y, yf = xhr.take()
                ok = halves(XC[:, x], XCh[:, y], XCl[:, y], act, dve, a, yf)
                xr.free(x, ok[1])
                yield ok
                for i in range(3):
                    c = slice(112 - 16 * b, 240 - 16 * b)
                    m = product(PS[:, i, :], (WPh[:, i, c], WPl[:, i, c]), (XCh[:, y], XCl[:, y]), b == 0, b == 7,
                                ok, wp_ok, bank_free)
                xhr.free(y, m)
                turn[0] += 1
                last[:] = [m]
                while not gb1:
                    yield
                xv = X[:, 4 * b:4 * b + 4, :]
                xb.append(pool(lambda e: e.tensor_tensor(xv, xv, BG[:, b:b + 1, :].to_broadcast([P, 4, P]), ALU.add),
                               zop, gb1))

            tasks = Tasks(dve)
            for b in range(NB):
                tasks.spawn(conv(b))
            for _ in range(12):
                tasks.push()
            g1 = mod_rows(1, 2, W["wmod1"], GA1, tA, tB, [3, 4], ld_p2)
            gb1 += [pool(lambda e: e.tensor_tensor(BG[:], GA1[:], W["boutB"].unsqueeze(1).to_broadcast([P, 8, P]), ALU.mult),
                         g1)]
            tasks.finish()
            m = last[0]
            T = lambda i: tb[:, i, :]
            z_ = dve(lambda e: e.tensor_scalar(T(0), PS[:, 0, :], b5[:, 0:1], None, ALU.add), m, g1)
            a = dve(lambda e: e.scalar_tensor_tensor(T(1), T(0), -1.0, T(0), ALU.mult, ALU.max), z_)
            a = act(lambda e: e.activation(T(2), T(1), ACT.Exp, scale=-1.0), a)
            a = act(lambda e: e.activation(T(3), T(2), ACT.Ln, bias=1.0), a)
            g2 = mod_rows(1, 5, W["wmod1"], GB1, tb[:, 8:10].rearrange("p a n -> p (a n)"),
                          tb[:, 10:12].rearrange("p a n -> p (a n)"), [3, 4], ld_p2, g1)
            spl = dve(lambda e: e.scalar_tensor_tensor(T(4), T(0), 0.0, T(3), ALU.max, ALU.add), a)
            ab = act(lambda e: e.activation(T(5), T(4), ACT.Exp, scale=cv[:, 2:3]), spl, a5)
            u = dve(lambda e: e.tensor_scalar(T(1), T(5), -1.0, cv[:, 4:5], ALU.add, ALU.mult), ab, a4)
            d = dve(lambda e: e.tensor_scalar(T(6), T(4), cv[:, 5:6], None, ALU.mult), spl)
            q = dve(lambda e: e.tensor_scalar(T(7), T(6), 1.0 / 6.0, 0.5, ALU.mult, ALU.add), d)
            q = dve(lambda e: e.tensor_tensor(T(7), T(7), T(6), ALU.mult), q)
            q = dve(lambda e: e.tensor_scalar(T(7), T(7), 1.0, cv[:, 3:4], ALU.add, ALU.mult), q)
            q = dve(lambda e: e.tensor_tensor(T(1), T(1), T(7), ALU.add), q, u)
            q = dve(lambda e: e.scalar_tensor_tensor(T(8), PS[:, 1, :], cv[:, 0:1], T(1), ALU.add, ALU.mult), q, c_ok)
            q = dve(lambda e: e.tensor_tensor_scan(T(9), T(5), T(8), 0.0, ALU.mult, ALU.add), q)
            q = dve(lambda e: e.scalar_tensor_tensor(T(10), PS[:, 2, :], cv[:, 1:2], T(9), ALU.add, ALU.mult), q)
            WO = W["WoutBD"].rearrange("p (b n) -> p b n", b=8)
            yr = Ring([5, 6, 7, 3, 4])
            tr = Ring([0, 2, 4, 6])
            for t in range(4):
                for hf in range(2):
                    bk, bf = yr.take()
                    m = pe(lambda e, t=t, hf=hf, bk=bk: e.matmul(PS[:, bk, :], tb[:, 10, t * P:(t + 1) * P],
                                                                 WO[:, 4 * hf:4 * hf + 4, :], start=True, stop=True), q, bf)
                    xv = X[:, 16 * hf + t:16 * hf + 16:4, :]
                    v = PS[:, bk, :].rearrange("p (b n) -> p b n", b=4)
                    s, sf = tr.take()
                    tmp = tb[:, s, :].rearrange("p (b n) -> p b n", b=4)
                    a = dve(lambda e: e.tensor_tensor(tmp, v, GA1[:, 4 * hf:4 * hf + 4, :], ALU.mult), m, sf, q)
                    yr.free(bk, a)
                    a = (dve, pool)[hf](lambda e: e.tensor_tensor(xv, xv, tmp, ALU.add), a, xb)
                    tr.free(s, a)
            barrier()
            C.close()

            return GA1, GB1, Z, ld_p3

        GA1, GB1, Z, ld_p3 = ssm()

        def ffn1():
            D = ExitStack()
            Hd = sb("Hd", [P, 3, 514], F32, D)
            XD = sb("XD", [P, 2, 512], F32, D)
            XDh = sb("XDh", [P, 2, 512], F32R, D)
            XDl = sb("XDl", [P, 2, 512], F32R, D)
            X1 = sb("X1", [P, 4, 512], F32, D)
            X1h = sb("X1h", [P, 4, 512], F32R, D)
            X1l = sb("X1l", [P, 4, 512], F32R, D)
            pwh = sb("pwh", [P, P], F32R, D)
            pwl = sb("pwl", [P, P], F32R, D)
            EWh = sb("EWh", [P, 8, P], F32R, D)
            EWl = sb("EWl", [P, 8, P], F32R, D)
            sx = sb("sx", [P, 2, 512], F32, D)
            gt = sb("gt1", [P, 3, 4, 8], F32, D)
            lgs = sb("lg1", [P, 2, 4, 8], F32, D)
            wks = sb("wk1", [P, 2, 5, 4, 8], F32, D)
            gT = sb("gT1", [8, 2, 512], F32, D)
            ye = sb("ye", [P, 4, 512], F32, D)
            gbs = sb("gbs1", [P, 8, 512], F32, D)
            ty = sb("ty1", [P, 4, 512], F32, D)
            acc = sb("acc1", [P, 2, 512], F32, D)
            HR = sb("HR", [P, NT, P], F32, D)
            hrT = sb("hrT", [P, 2, 512], F32, D)
            ff = sb("ff", [P, 2, 512], F32, D)
            tmpo = sb("tmpo", [P, 4, 4, P], F32, D)
            dg = nc.dram_tensor("dg1", [8, 8, 512], F32, kind="Internal").ap()
            s_gw = [dsem(f"s_gx{i}") for i in range(2)]
            s_g = [dsem(f"s_gy{i}") for i in range(8)]
            zr, hdr, xdr, xhr, x1r, sxr, wkr = (Ring(range(n)) for n in (2, 3, 2, 2, 4, 2, 2))
            yer, gsr, tyr, accr, hrr, gTr, gtr = (Ring(range(n)) for n in (4, 8, 4, 2, 2, 2, 3))
            misc, yr = Ring([4, 5, 6, 7]), Ring([0, 1])
            dw = W["dw"]
            EW = W["ewT"].rearrange("p (e n) -> p e n", e=8)
            pz = pool(lambda e: e.memset(Hd[:, :, 0:2], 0.0))
            pw_ok = halves(W["pwT"], pwh[:], pwl[:], dve, dve, ld_p3)
            ew_ok = halves(W["ewT"], EWh[:].rearrange("p e n -> p (e n)"), EWl[:].rearrange("p e n -> p (e n)"), act, pool)
            ST = {}

            def prep(b):
                while not hdr:
                    yield
                h, hf = hdr.take()
                (a0,), _ = yield from ln_batch(b, Z, zr, misc, [Hd[:, h, 2:514]], mf[:, 1, 4, b:b + 1],
                                               mf[:, 1, 3, b:b + 1], [act, act, pool, act], hf)
                while not xdr:
                    yield
                x, xf = xdr.take()
                o = XD[:, x, :]
                c = act(lambda e: e.activation(o, Hd[:, h, 0:512], ACT.Identity, bias=W["dwb"], scale=dw[:, 0:1]), a0, pz, xf)
                yield c
                for k in range(1, 3):
                    c = dve(lambda e, k=k: e.scalar_tensor_tensor(o, Hd[:, h, k:k + 512], dw[:, k:k + 1], o,
                                                                  ALU.mult, ALU.add), c)
                yield ()
                while not xhr:
                    yield
                y, yf = xhr.take()
                ok = halves(XD[:, x], XDh[:, y], XDl[:, y], act, dve, c, yf)
                xdr.free(x, ok[1])
                yield ok
                while not misc:
                    yield
                bk, bf = misc.take()
                yield bf
                m = product(PS[:, bk, :], (pwh[:], pwl[:]), (XDh[:, y], XDl[:, y]), True, True, ok, pw_ok, bf)
                xhr.free(y, m)
                yield m
                while not sxr:
                    yield
                s, sf = sxr.take()
                a = act(lambda e: e.activation(sx[:, s], PS[:, bk, :], ACT.Silu, bias=W["pwb"]), m, sf)
                misc.free(bk, a)
                yield a
                while not x1r:
                    yield
                x, xf = x1r.take()
                a = pool(lambda e: e.tensor_tensor(X1[:, x], sx[:, s], Hd[:, h, 2:514], ALU.add), a, a0, xf)
                sxr.free(s, a)
                hdr.free(h, a)
                yield a
                ST["x", b] = x, a, halves(X1[:, x], X1h[:, x], X1l[:, x], act, dve, a)
                while not misc:
                    yield
                bk, bf = misc.take()
                yield bf
                L = PS[:, bk, 0:32].rearrange("p (t e) -> p t e", t=4)
                for t in range(4):
                    m = pe(lambda e, t=t: e.matmul(L[:, t, :], X1[:, x, t * P:(t + 1) * P], W["rw1T"],
                                                   start=True, stop=True), a, bf)
                yield m
                while not wkr:
                    yield
                wi, wf = wkr.take()
                lg, wk = lgs[:, wi], wks[:, wi]
                a = dve(lambda e: e.tensor_tensor(lg, L, W["rb1B"].unsqueeze(1).to_broadcast([P, 4, 8]), ALU.add), m, wf)
                misc.free(bk, a)
                a, m1, m2, oh1, oh2, bc = yield from top2(lg, wk, a)
                d, w1, w2 = (wk[:, 4, :, i] for i in (5, 6, 7))
                a = dve(lambda e: e.tensor_tensor(d, m1, m2, ALU.subtract), a)
                yield a
                a = act(lambda e: e.activation(d, d, ACT.Tanh, scale=0.5), a)
                yield a
                c = dve(lambda e: e.tensor_scalar(w1, d, 0.5, 0.5, ALU.mult, ALU.add), a)
                a = dve(lambda e: e.tensor_scalar(w2, d, -0.5, 0.5, ALU.mult, ALU.add), a)
                a = dve(lambda e: e.tensor_tensor(oh1, oh1, bc(w1), ALU.mult), c)
                a = dve(lambda e: e.tensor_tensor(oh2, oh2, bc(w2), ALU.mult), a)
                yield a
                while not gtr:
                    yield
                g, gf = gtr.take()
                ok = dve(lambda e: e.tensor_tensor(gt[:, g], oh1, oh2, ALU.add), a, gf)
                wkr.free(wi, ok)
                yield ok
                while not (misc and gTr):
                    yield
                bk, bf = misc.take()
                yield bf
                for t in range(4):
                    m = pe(lambda e, t=t: e.transpose(PS[0:8, bk, t * P:(t + 1) * P], gt[:, g, t, :], ident), ok, bf)
                gtr.free(g, m)
                yield m
                while not gTr:
                    yield
                s, sf = gTr.take()
                c = act(lambda e: e.activation(gT[:, s], PS[0:8, bk, :], ACT.Copy), m, sf)
                misc.free(bk, c)
                wr = sp.dma(dg[b], gT[:, s], s_gw[b % 2], c)
                gTr.free(s, wr)
                ST["gw", b] = wr

            def load_g(b, e_):
                s, f = gsr.take()
                ST["gb", b, e_] = s, sp.dma(gbs[:, s], dg[b, e_:e_ + 1, :].to_broadcast([P, 512]), s_g[s], f, ST["gw", b])

            def expert(b, e_):
                x, _, ok = ST["x", b]
                bk, bf = yr.take()
                m = product(PS[:, bk, :], (EWh[:, e_, :], EWl[:, e_, :]), (X1h[:, x], X1l[:, x]), True, True, ok, ew_ok, bf)
                y, yf = yer.take()
                a = act(lambda e: e.activation(ye[:, y], PS[:, bk, :], ACT.Silu, bias=W["ebT"][:, e_:e_ + 1]), m, yf)
                yr.free(bk, a)
                ST["y"] = y, a

            def gated(b, e_):
                y, a = ST["y"]
                q, ld = ST["gb", b, e_]
                if max(ld.t, a.t) > dve.clock:
                    tasks.fill(max(ld.t, a.t))
                if e_ == 0:
                    while not accr:
                        tasks.push()
                    ST["acc"] = accr.take()
                s, sf = ST["acc"]
                t, tf = (None, sf) if e_ == 0 else tyr.take()
                dst = acc[:, s] if e_ == 0 else ty[:, t]
                mu = dve(lambda e: e.tensor_tensor(dst, ye[:, y], gbs[:, q], ALU.mult), ld, a, tf)
                gsr.free(q, mu)
                yer.free(y, mu)
                if e_:
                    mu = pool(lambda e: e.tensor_tensor(acc[:, s], acc[:, s], dst, ALU.add), mu, ST["a"])
                    tyr.free(t, mu)
                ST["a"] = mu
                if e_ == 7:
                    ST["acc", b] = s, mu

            def post(b):
                s, a = ST["acc", b]
                yield a
                x = ST["x", b][0]
                while not misc:
                    yield
                bk, bf = misc.take()
                yield bf
                for t in range(4):
                    o = PS[:, bk, t * P:(t + 1) * P]
                    pe(lambda e, t=t, o=o: e.matmul(o, acc[:, s, t * P:(t + 1) * P], W["owT"], start=True, stop=False), a, bf)
                    m = pe(lambda e, t=t, o=o: e.matmul(o, X1[:, x, t * P:(t + 1) * P], ident, start=False, stop=True))
                accr.free(s, m)
                x1r.free(x, m)
                yield m
                v = PS[:, bk, :].rearrange("p (t n) -> p t n", t=4)
                h = HR[:, 4 * b:4 * b + 4, :]
                a = dve(lambda e: e.tensor_tensor(h, v, W["obB"].unsqueeze(1).to_broadcast([P, 4, P]), ALU.add), m)
                misc.free(bk, a)
                rs = yield from ln_stats(b, HR, 1e-6, False, a)
                for t in range(4):
                    i = 4 * b + t
                    a = dve(lambda e, i=i: e.scalar_tensor_tensor(HR[:, i, :], HR[:, i, :], lnw[:, 4, i:i + 1], W["nwB"],
                                                                  ALU.mult, ALU.mult), rs)
                    yield ()
                yield a
                while not (misc and hrr):
                    yield
                bk, bf = misc.take()
                yield bf
                for t in range(4):
                    m = pe(lambda e, t=t: e.transpose(PS[:, bk, t * P:(t + 1) * P], HR[:, 4 * b + t, :], ident), a, bf)
                yield m
                while not hrr:
                    yield
                s, sf = hrr.take()
                c = act(lambda e: e.activation(hrT[:, s], PS[:, bk, :], ACT.Copy), m, sf)
                misc.free(bk, c)
                yield c
                q = b % 4
                m = pe(lambda e: e.matmul(PS[32 * q:32 * q + 32, 2 + b // 4, :], W["fdT"], hrT[:, s],
                                          start=True, stop=True), c)
                hrr.free(s, m)
                if q < 3:
                    return
                hf = b // 4
                yield m
                ST["ff", hf] = act(lambda e: e.activation(ff[:, hf], PS[:, 2 + hf, :], ACT.Gelu, bias=W["fdb"]), m)
                for t in range(4):
                    tasks.spawn(ff_out(hf, t))
                    yield ()

            FU = W["fuBD"].rearrange("p (b n) -> p b n", b=4)
            tr = Ring([0, 1, 2, 3])
            s_o = dsem("s_o")

            def ff_out(hf, t):
                while not (misc and tr):
                    yield
                bk, bf = misc.take()
                s, sf = tr.take()
                yield [bf, sf]
                m = pe(lambda e: e.matmul(PS[:, bk, :], ff[:, hf, t * P:(t + 1) * P], FU, start=True, stop=True),
                       ST["ff", hf], bf)
                yield m
                v = PS[:, bk, :].rearrange("p (b n) -> p b n", b=4)
                tmp = tmpo[:, s]
                xv = X[:, 16 * hf + t:16 * hf + 16:4, :]
                hv = HR[:, 16 * hf + t:16 * hf + 16:4, :]
                a = dve(lambda e: e.tensor_tensor(tmp, v, hv, ALU.add), m, sf)
                misc.free(bk, a)
                yield a
                a = pool(lambda e: e.tensor_tensor(tmp, tmp, W["fubB"].unsqueeze(1).to_broadcast([P, 4, P]), ALU.add), a)
                yield a
                a = dve(lambda e: e.tensor_tensor(tmp, tmp, GB1[:, 4 * hf:4 * hf + 4, :], ALU.mult), a)
                a = dve(lambda e: e.tensor_tensor(xv, xv, tmp, ALU.add), a)
                tr.free(s, a)
                ST["o"] = sp.dma(out_d[:, 16 * hf + t:16 * hf + 16:4, :], xv, s_o, a)

            tasks = Tasks(pe)
            tasks.spawn(prep(0), prep(1), prep(2))
            while ("x", 0) not in ST:
                tasks.push()
            work = [(b, e_) for b in range(NB) for e_ in range(8)]
            for n, (b, e_) in enumerate(work):
                if e_ == 0 and b + 3 < NB:
                    tasks.spawn(prep(b + 3))
                while ("gw", b) not in ST:
                    tasks.push()
                for d in range(n, n + 8):
                    if d < len(work) and ("gb",) + work[d] not in ST and ("gw", work[d][0]) in ST and gsr:
                        load_g(*work[d])
                prev = ST.get("y")
                expert(b, e_)
                if n:
                    cur, ST["y"] = ST["y"], prev
                    gated(*work[n - 1])
                    ST["y"] = cur
                    if e_ == 0:
                        tasks.spawn(post(b - 1))
                tasks.tick(8)
            gated(*work[-1])
            tasks.spawn(post(NB - 1))
            tasks.finish()
            last = ST["o"]
            D.close()
            sp(lambda e: e.nop(), last)

        ffn1()

        for q in queues:
            q.count()
        block = ctx.enter_context(nc.Block())

        @block.sync
        def _(e):
            sp.emit(e)

        @block.gpsimd
        def _(e):
            pool.emit(e)

        @block.vector
        def _(e):
            dve.emit(e)

        @block.scalar
        def _(e):
            act.emit(e)

        @block.tensor
        def _(e):
            pe.emit(e)


def kernel(**inputs):
    import concourse.bacc as bacc
    from concourse.bass_utils import run_bass_kernel_spmd

    I = {k: np.asarray(v) for k, v in inputs.items()}
    col = lambda a: np.asarray(a).reshape(-1, 1)
    rows = lambda a: np.broadcast_to(np.asarray(a).reshape(1, -1), (P, np.asarray(a).size))
    z = lambda *s: np.zeros(s, np.float32)
    bd = z(P, 8, P)
    for b in range(8):
        bd[16 * b:16 * b + 16, b, :] = I["L1_attn_Wout"]
    fu = z(P, 4, P)
    for b in range(4):
        fu[32 * b:32 * b + 32, b, :] = I["L1_ffn_ff_up_w"].T
    bin_ = I["L1_attn_b_in"]
    b5 = np.stack([np.tile(v, 8) for v in (bin_[0:16], bin_[16:48:2], bin_[17:48:2], bin_[48:80:2], bin_[49:80:2])], 1)
    W1 = np.concatenate([I["L0_ffn_W1"], I["L0_ffn_Ws1"][None]], 0)
    b1 = np.concatenate([I["L0_ffn_b1"], I["L0_ffn_bs1"][None]], 0)
    W2 = np.concatenate([I["L0_ffn_W2"], I["L0_ffn_Ws2"][None]], 0)
    b2p = z(P, P)
    b2p[0:8] = I["L0_ffn_b2"]
    b2p[8] = I["L0_ffn_bs2"]
    w12 = np.stack([W1.transpose(2, 0, 1), W2.reshape(9, P, 4, P).transpose(3, 0, 2, 1).reshape(P, 9, 512)], 2)
    parts = {
        "c": np.concatenate([I["L0_c"].T, I["L1_c"].T], 1), "wmod0": I["L0_wmod"], "ident": np.eye(P, dtype=np.float32),
        "bq": col(I["L0_attn_bq"]), "bk": col(I["L0_attn_bk"]),
        "WqT": I["L0_attn_Wq"].T, "WkT": I["L0_attn_Wk"].T, "WvT": I["L0_attn_Wv"].T, "WoT": I["L0_attn_Wo"].T,
        "bvB": rows(I["L0_attn_bv"]), "boB": rows(I["L0_attn_bo"]),
        "b2p": b2p, "b1T": b1.reshape(9, 4, P).transpose(2, 0, 1).reshape(P, -1),
        "wr0": I["L0_ffn_w_router"].T, "desc": rows(np.arange(8, 0, -1).astype(np.float32)),
        "wmod1": I["L1_wmod"], "convw": I["L1_attn_conv_w"][:, 0, :], "convb": col(I["L1_attn_conv_b"]),
        "Win": I["L1_attn_Win"], "bin5": b5, "Alog": col(np.tile(I["L1_attn_A_log"], 8)), "WoutBD": bd.reshape(P, -1),
        "boutB": rows(I["L1_attn_b_out"]), "dw": I["L1_ffn_dw_kernel"][:, 0, :], "dwb": col(I["L1_ffn_dw_bias"]),
        "pwT": I["L1_ffn_pw_w"].T, "pwb": col(I["L1_ffn_pw_b"]), "rw1T": I["L1_ffn_router_w"].T,
        "rb1B": rows(I["L1_ffn_router_b"]), "ewT": I["L1_ffn_expert_w"].transpose(2, 0, 1).reshape(P, -1),
        "ebT": I["L1_ffn_expert_b"].T, "owT": I["L1_ffn_out_w"].T, "obB": rows(I["L1_ffn_out_b"]),
        "nwB": rows(I["L1_ffn_norm_w"]), "fdT": I["L1_ffn_ff_down_w"].T, "fdb": col(np.tile(I["L1_ffn_ff_down_b"], 4)),
        "fuBD": fu.reshape(P, -1), "fubB": rows(I["L1_ffn_ff_up_b"]),
    }
    small = z(8, 8, P)
    for i, n in enumerate("qkvo"):
        small[0:8, i] = I[f"L0_attn_A{n}"]
        small[0:8, 4 + i] = I[f"L0_attn_B{n}"].T
    arrays = {"x": np.ascontiguousarray(I["L0_attn_x"].reshape(NT, P, P).transpose(1, 0, 2))}
    for i, pack in ((0, PACK0), (1, PACK1), (2, PACK2), (3, PACK3)):
        arrays[f"p{i}"] = np.ascontiguousarray(np.concatenate([parts[n].reshape(P, w) for n, w in pack], 1))
    arrays["w12"] = np.ascontiguousarray(w12)
    arrays["small"] = small.reshape(8, -1)
    nc = bacc.Bacc("TRN2", target_bir_lowering=False, num_devices=1)
    args = [nc.dram_tensor(f"in_{n}", a.shape, F32, kind="ExternalInput").ap() for n, a in arrays.items()]
    args.append(nc.dram_tensor("out_0", (P, NT, P), F32, kind="ExternalOutput").ap())
    adaln_kernel(nc, *args)
    r = run_bass_kernel_spmd(nc, [{f"in_{n}": a for n, a in arrays.items()}], core_ids=[0])
    y = np.asarray(r.results[0]["out_0"])
    return np.ascontiguousarray(y.transpose(1, 0, 2)).reshape(8, 512, P)
```
